# Optimizing a Trainium2 kernel written in Bass

```python
import numpy as np
import jax
import jax.numpy as jnp

def _softmax(x, axis=-1):
    return jax.nn.softmax(x, axis=axis)

def _gelu(x):
    return jax.nn.gelu(x, approximate=True)

def _silu(x):
    return jax.nn.silu(x)

def _sigmoid(x):
    return jax.nn.sigmoid(x)

def _layernorm(x, axis=-1, eps=1e-05):
    m = jnp.mean(x, axis=axis, keepdims=True)
    v = jnp.var(x, axis=axis, keepdims=True)
    return (x - m) / jnp.sqrt(v + eps)

def _scatter_add(tgt, idx, src, axis=0):
    return tgt.at[idx].add(src)

def _segment_sum(src, seg, n):
    return jax.ops.segment_sum(src, seg, n)
kernel_name = 'mk_xattn_ffn_d4_seqx_r8_a24234'

def setup_inputs(seed: int=0):
    np.random.seed(seed)
    _w = jnp.asarray

    def _rec_inputs():
        import jax
        import jax.numpy as jnp
        _rk = jax.random.key(seed)
        x = -0.0003929 + 0.9999 * jax.random.normal(jax.random.fold_in(_rk, 1), (16, 128, 128), jnp.float32)
        _lenS = 128 - jax.random.randint(jax.random.fold_in(_rk, 7), (16,), 0, max(1, 128 // 4) + 1, jnp.int32)
        _lenS2 = 128 - jax.random.randint(jax.random.fold_in(_rk, 8), (16,), 0, max(1, 128 // 4) + 1, jnp.int32)
        _ctx_1024P = jax.random.normal(jax.random.fold_in(_rk, 11), (16, 16, 128), jnp.float32)
        _ctx_1024c = jax.random.dirichlet(jax.random.fold_in(_rk, 511), 0.3 * jnp.ones((16,), jnp.float32), (16, 128))
        _ctx_1024t = jnp.einsum('bsk,bkd->bsd', _ctx_1024c, _ctx_1024P)
        _ctx_1024t = _ctx_1024t * jax.lax.rsqrt(jnp.mean(jnp.square(_ctx_1024t)) + 1e-12) * 0.953939
        ctx_1024 = 2.81802e-05 + 1.00001 * (_ctx_1024t + 0.3 * jax.random.normal(jax.random.fold_in(_rk, 611), (16, 128, 128), jnp.float32))
        return (x, ctx_1024)
    x, ctx_1024 = _rec_inputs()

    def _L0_xattn_setup():
        import jax, jax.numpy as jnp
        import numpy as np
        import math
        D_MODEL = 128
        N_HEADS = 16
        C = 1
        B, L = (8, 256)

        def _glorot(key, fan):
            lim = np.sqrt(6.0 / (fan + fan)).astype(np.float32)
            return jax.random.uniform(key, (fan, fan), jnp.float32, -lim, lim)
        key = jax.random.key(seed)
        ks = jax.random.split(key, 7)
        queries = jax.random.normal(ks[0], (B, L, D_MODEL), jnp.float32)
        keys = jax.random.normal(ks[1], (B, L, D_MODEL), jnp.float32)
        values = jax.random.normal(ks[2], (B, L, D_MODEL), jnp.float32)
        wq = _glorot(ks[3], D_MODEL)
        wk = _glorot(ks[4], D_MODEL)
        wv = _glorot(ks[5], D_MODEL)
        wo = _glorot(ks[6], D_MODEL)
        return {'queries': queries, 'keys': keys, 'values': values, 'wq': wq, 'wk': wk, 'wv': wv, 'wo': wo}
    _L0_xattn_all = _L0_xattn_setup()
    _L0_xattn_in = {k: v for k, v in _L0_xattn_all.items() if k in ('wq', 'wk', 'wv', 'wo')}
    del _L0_xattn_all

    def _L0_ffn_setup():
        import jax, jax.numpy as jnp
        import numpy as np
        E = 8
        G = 4
        LG = 2
        TOPK = 2
        ROUTE_SCALE = 1.0

        def _grouped_mm(x, w, counts):
            counts = counts.astype(jnp.int32)
            if hasattr(jax.lax, 'ragged_dot'):
                return jax.lax.ragged_dot(x, w, counts)
            offs = jnp.cumsum(counts)
            eid = jnp.searchsorted(offs, jnp.arange(x.shape[0]), side='right')
            oh = jax.nn.one_hot(eid, w.shape[0], dtype=x.dtype)
            return jnp.einsum('nd,ne,edh->nh', x, oh, w)
        key = jax.random.key(seed)
        ks = jax.random.split(key, 8)
        bs, slen, dim, hid, shid = (2, 256, 128, 64, 128)
        std = 0.02
        return {'x': jax.random.normal(ks[0], (bs, slen, dim), jnp.float32), 'w_gate': jax.random.normal(ks[1], (E, dim), jnp.float32) * std, 'w1': jax.random.normal(ks[2], (E, dim, hid), jnp.float32) * std, 'w2': jax.random.normal(ks[3], (E, hid, dim), jnp.float32) * std, 'w3': jax.random.normal(ks[4], (E, dim, hid), jnp.float32) * std, 'sw1': jax.random.normal(ks[5], (shid, dim), jnp.float32) * std, 'sw2': jax.random.normal(ks[6], (dim, shid), jnp.float32) * std, 'sw3': jax.random.normal(ks[7], (shid, dim), jnp.float32) * std, 'expert_bias': jnp.zeros((E,), jnp.float32)}
    _L0_ffn_all = _L0_ffn_setup()
    _L0_ffn_in = {k: v for k, v in _L0_ffn_all.items() if k in ('w_gate', 'w1', 'w2', 'w3', 'sw1', 'sw2', 'sw3', 'expert_bias')}
    del _L0_ffn_all

    def _L1_xattn_setup():
        import jax, jax.numpy as jnp
        import numpy as np
        B, S, D_IN, D_MODEL = (4, 256, 128, 128)
        key = jax.random.key(seed)
        ks = jax.random.split(key, 9)
        return {'q': jax.random.normal(ks[0], (B, S, D_IN), jnp.float32), 'k': jax.random.normal(ks[1], (B, S, D_IN), jnp.float32), 'v': jax.random.normal(ks[2], (B, S, D_IN), jnp.float32), 'Wq': jax.random.normal(ks[3], (D_IN, D_MODEL), jnp.float32) * 0.02, 'bq': jax.random.normal(ks[4], (D_MODEL,), jnp.float32) * 0.02, 'Wk': jax.random.normal(ks[5], (D_IN, D_MODEL), jnp.float32) * 0.02, 'bk': jax.random.normal(ks[6], (D_MODEL,), jnp.float32) * 0.02, 'Wv': jax.random.normal(ks[7], (D_IN, D_MODEL), jnp.float32) * 0.02, 'bv': jax.random.normal(ks[8], (D_MODEL,), jnp.float32) * 0.02}
    _L1_xattn_all = _L1_xattn_setup()
    _L1_xattn_in = {k: v for k, v in _L1_xattn_all.items() if k in ('Wq', 'bq', 'Wk', 'bk', 'Wv', 'bv')}
    del _L1_xattn_all

    def _L1_ffn_setup():
        import jax, jax.numpy as jnp
        import numpy as np
        E = 8
        K = 2
        key = jax.random.key(seed)
        ks = jax.random.split(key, 6)
        B, S, D, F = (4, 256, 128, 512)
        s_d = 1.0 / np.sqrt(D).astype(np.float32)
        s_f = 1.0 / np.sqrt(F).astype(np.float32)
        return {'x': jax.random.normal(ks[0], (B, S, D), jnp.float32), 'ln_w': jnp.ones((D,), jnp.float32), 'Wg': jax.random.normal(ks[1], (D, E), jnp.float32) * s_d, 'bg': jnp.zeros((E,), jnp.float32), 'W1a': jax.random.normal(ks[2], (E, D, F), jnp.float32) * s_d, 'b1a': jnp.zeros((E, F), jnp.float32), 'W1b': jax.random.normal(ks[3], (E, D, F), jnp.float32) * s_d, 'b1b': jnp.zeros((E, F), jnp.float32), 'W2': jax.random.normal(ks[4], (E, F, D), jnp.float32) * s_f, 'b2': jnp.zeros((E, D), jnp.float32)}
    _L1_ffn_all = _L1_ffn_setup()
    _L1_ffn_in = {k: v for k, v in _L1_ffn_all.items() if k in ('ln_w', 'Wg', 'bg', 'W1a', 'b1a', 'W1b', 'b1b', 'W2', 'b2')}
    del _L1_ffn_all

    def _L2_xattn_setup():
        import jax, jax.numpy as jnp
        import numpy as np
        B, L, D = (8, 256, 128)
        key = jax.random.key(seed)
        k1, k2, k3 = jax.random.split(key, 3)
        enc_outputs = jax.random.normal(k1, (B, L, D), dtype=jnp.float32)
        x = jax.random.normal(k2, (B, L, D), dtype=jnp.float32)
        Wq = jax.random.normal(k3, (D, D), dtype=jnp.float32) * (1.0 / np.sqrt(D))
        return {'enc_outputs': enc_outputs, 'x': x, 'Wq': Wq}
    _L2_xattn_all = _L2_xattn_setup()
    _L2_xattn_in = {k: v for k, v in _L2_xattn_all.items() if k in ('Wq',)}
    del _L2_xattn_all

    def _L2_ffn_setup():
        import jax, jax.numpy as jnp
        import numpy as np
        EPS = 1e-05

        def _ln(x, g, b):
            mu = jnp.mean(x, axis=-1, keepdims=True)
            var = jnp.mean(jnp.square(x - mu), axis=-1, keepdims=True)
            return (x - mu) * jax.lax.rsqrt(var + EPS) * g + b

        def _forward(x, index_b, index_t, sw1, sb1, sw2, sb2, sw3, sb3, s_ln_g, s_ln_b, sg_w, sg_b, eg_w, eg_b, exp_bias, ew1, eb1, ew2, eb2, ew3, eb3, sel_ln_g, sel_ln_b):
            x1 = jnp.einsum('btd,hd->bth', x, sw1) + sb1
            x2 = jnp.einsum('btd,hd->bth', x, sw2) + sb2
            sh = _ln(jax.nn.silu(x1) * x2, s_ln_g, s_ln_b)
            shared_out = jnp.einsum('bth,dh->btd', sh, sw3) + sb3
            x_moe = x[index_b, index_t]
            shared_scores = jax.nn.sigmoid(x_moe @ sg_w.T + sg_b)
            expert_scores = jax.nn.sigmoid(x_moe @ eg_w.T + eg_b)
            top1_idx = jnp.argmax(expert_scores + exp_bias, axis=-1)
            top1_score = jnp.take_along_axis(expert_scores, top1_idx[:, None], axis=-1)
            weights = jax.nn.softmax(jnp.concatenate([shared_scores, top1_score], axis=-1), axis=-1)
            shared_w, expert_w = (weights[:, 0], weights[:, 1])
            shared_moe_out = shared_out[index_b, index_t] * shared_w[:, None]
            h1 = jnp.einsum('md,ehd->meh', x_moe, ew1) + eb1
            h2 = jnp.einsum('md,ehd->meh', x_moe, ew2) + eb2
            z = _ln(jax.nn.silu(h1) * h2, sel_ln_g, sel_ln_b)
            out_all = jnp.einsum('meh,edh->med', z, ew3) + eb3
            expert_out = jnp.take_along_axis(out_all, top1_idx[:, None, None], axis=1)[:, 0]
            expert_moe_out = expert_out * expert_w[:, None]
            final_out = shared_out.at[index_b, index_t].set(shared_moe_out + expert_moe_out)
            return final_out
        B, T, D, E, H, M = (2, 256, 128, 8, 64, 256)
        key = jax.random.key(seed)
        ks = jax.random.split(key, 24)
        s = 0.02
        inp = {}
        inp['x'] = jax.random.normal(ks[0], (B, T, D), jnp.float32)
        flat = jnp.arange(M, dtype=jnp.int32) * 2
        inp['index_b'] = flat // T
        inp['index_t'] = flat % T
        inp['sw1'] = jax.random.normal(ks[1], (H, D), jnp.float32) * s
        inp['sb1'] = jnp.zeros((H,), jnp.float32)
        inp['sw2'] = jax.random.normal(ks[2], (H, D), jnp.float32) * s
        inp['sb2'] = jnp.zeros((H,), jnp.float32)
        inp['sw3'] = jax.random.normal(ks[3], (D, H), jnp.float32) * s
        inp['sb3'] = jnp.zeros((D,), jnp.float32)
        inp['s_ln_g'] = jnp.ones((H,), jnp.float32)
        inp['s_ln_b'] = jnp.zeros((H,), jnp.float32)
        inp['sg_w'] = jax.random.normal(ks[4], (1, D), jnp.float32) * s
        inp['sg_b'] = jnp.zeros((1,), jnp.float32)
        inp['eg_w'] = jax.random.normal(ks[5], (E, D), jnp.float32) * s
        inp['eg_b'] = jnp.zeros((E,), jnp.float32)
        inp['exp_bias'] = jnp.zeros((E,), jnp.float32)
        inp['ew1'] = jax.random.normal(ks[6], (E, H, D), jnp.float32) * s
        inp['eb1'] = jnp.zeros((E, H), jnp.float32)
        inp['ew2'] = jax.random.normal(ks[7], (E, H, D), jnp.float32) * s
        inp['eb2'] = jnp.zeros((E, H), jnp.float32)
        inp['ew3'] = jax.random.normal(ks[8], (E, D, H), jnp.float32) * s
        inp['eb3'] = jnp.zeros((E, D), jnp.float32)
        inp['sel_ln_g'] = jnp.ones((H,), jnp.float32)
        inp['sel_ln_b'] = jnp.zeros((H,), jnp.float32)
        return inp
    _L2_ffn_all = _L2_ffn_setup()
    _L2_ffn_in = {k: v for k, v in _L2_ffn_all.items() if k in ('index_b', 'index_t', 'sw1', 'sb1', 'sw2', 'sb2', 'sw3', 'sb3', 's_ln_g', 's_ln_b', 'sg_w', 'sg_b', 'eg_w', 'eg_b', 'exp_bias', 'ew1', 'eb1', 'ew2', 'eb2', 'ew3', 'eb3', 'sel_ln_g', 'sel_ln_b')}
    del _L2_ffn_all

    def _L3_xattn_setup():
        import jax, jax.numpy as jnp
        import numpy as np
        HEADS = 16
        key = jax.random.key(seed)
        k1, k2, k3, k4 = jax.random.split(key, 4)
        B, T, S, W = (2, 256, 256, 128)
        x = jax.random.normal(k1, (B, T, W), dtype=jnp.float32)
        cond_k = jax.random.normal(k2, (B, S, W), dtype=jnp.float32)
        cond_v = jax.random.normal(k3, (B, S, W), dtype=jnp.float32)
        w_proj = jax.random.normal(k4, (W, W), dtype=jnp.float32) * 0.02
        b_proj = jnp.zeros((W,), dtype=jnp.float32)
        return {'x': x, 'cond_k': cond_k, 'cond_v': cond_v, 'w_proj': w_proj, 'b_proj': b_proj}
    _L3_xattn_all = _L3_xattn_setup()
    _L3_xattn_in = {k: v for k, v in _L3_xattn_all.items() if k in ('w_proj', 'b_proj')}
    del _L3_xattn_all

    def _L3_ffn_setup():
        import jax, jax.numpy as jnp
        import numpy as np
        N_EMBD = 128
        N_EXPERTS = 8
        TOP_K = 2
        CAPACITY_FACTOR = 1.25
        key = jax.random.key(seed)
        ks = jax.random.split(key, 8)
        B, T, C, E, H = (8, 256, N_EMBD, N_EXPERTS, 4 * N_EMBD)
        w = lambda k, shape: jax.random.normal(k, shape, jnp.float32) * 0.02
        return {'x': jax.random.normal(ks[0], (B, T, C), jnp.float32), 'rW1': w(ks[1], (C, H)), 'rb1': jnp.zeros((H,), jnp.float32), 'rW2': w(ks[2], (H, H)), 'rb2': jnp.zeros((H,), jnp.float32), 'rW3': w(ks[3], (H, E)), 'rb3': jnp.zeros((E,), jnp.float32), 'eW1': w(ks[4], (E, C, H)), 'eb1': jnp.zeros((E, H), jnp.float32), 'eW2': w(ks[5], (E, H, C)), 'eb2': jnp.zeros((E, C), jnp.float32)}
    _L3_ffn_all = _L3_ffn_setup()
    _L3_ffn_in = {k: v for k, v in _L3_ffn_all.items() if k in ('rW1', 'rb1', 'rW2', 'rb2', 'rW3', 'rb3', 'eW1', 'eb1', 'eW2', 'eb2')}
    del _L3_ffn_all
    return {'x': x, 'ctx_1024': ctx_1024, 'L0_xattn_wq': _L0_xattn_in['wq'], 'L0_xattn_wk': _L0_xattn_in['wk'], 'L0_xattn_wv': _L0_xattn_in['wv'], 'L0_xattn_wo': _L0_xattn_in['wo'], 'L0_ffn_w_gate': _L0_ffn_in['w_gate'], 'L0_ffn_w1': _L0_ffn_in['w1'], 'L0_ffn_w2': _L0_ffn_in['w2'], 'L0_ffn_w3': _L0_ffn_in['w3'], 'L0_ffn_sw1': _L0_ffn_in['sw1'], 'L0_ffn_sw2': _L0_ffn_in['sw2'], 'L0_ffn_sw3': _L0_ffn_in['sw3'], 'L0_ffn_expert_bias': _L0_ffn_in['expert_bias'], 'L1_xattn_Wq': _L1_xattn_in['Wq'], 'L1_xattn_bq': _L1_xattn_in['bq'], 'L1_xattn_Wk': _L1_xattn_in['Wk'], 'L1_xattn_bk': _L1_xattn_in['bk'], 'L1_xattn_Wv': _L1_xattn_in['Wv'], 'L1_xattn_bv': _L1_xattn_in['bv'], 'L1_ffn_ln_w': _L1_ffn_in['ln_w'], 'L1_ffn_Wg': _L1_ffn_in['Wg'], 'L1_ffn_bg': _L1_ffn_in['bg'], 'L1_ffn_W1a': _L1_ffn_in['W1a'], 'L1_ffn_b1a': _L1_ffn_in['b1a'], 'L1_ffn_W1b': _L1_ffn_in['W1b'], 'L1_ffn_b1b': _L1_ffn_in['b1b'], 'L1_ffn_W2': _L1_ffn_in['W2'], 'L1_ffn_b2': _L1_ffn_in['b2'], 'L2_xattn_Wq': _L2_xattn_in['Wq'], 'L2_ffn_index_b': _L2_ffn_in['index_b'], 'L2_ffn_index_t': _L2_ffn_in['index_t'], 'L2_ffn_sw1': _L2_ffn_in['sw1'], 'L2_ffn_sb1': _L2_ffn_in['sb1'], 'L2_ffn_sw2': _L2_ffn_in['sw2'], 'L2_ffn_sb2': _L2_ffn_in['sb2'], 'L2_ffn_sw3': _L2_ffn_in['sw3'], 'L2_ffn_sb3': _L2_ffn_in['sb3'], 'L2_ffn_s_ln_g': _L2_ffn_in['s_ln_g'], 'L2_ffn_s_ln_b': _L2_ffn_in['s_ln_b'], 'L2_ffn_sg_w': _L2_ffn_in['sg_w'], 'L2_ffn_sg_b': _L2_ffn_in['sg_b'], 'L2_ffn_eg_w': _L2_ffn_in['eg_w'], 'L2_ffn_eg_b': _L2_ffn_in['eg_b'], 'L2_ffn_exp_bias': _L2_ffn_in['exp_bias'], 'L2_ffn_ew1': _L2_ffn_in['ew1'], 'L2_ffn_eb1': _L2_ffn_in['eb1'], 'L2_ffn_ew2': _L2_ffn_in['ew2'], 'L2_ffn_eb2': _L2_ffn_in['eb2'], 'L2_ffn_ew3': _L2_ffn_in['ew3'], 'L2_ffn_eb3': _L2_ffn_in['eb3'], 'L2_ffn_sel_ln_g': _L2_ffn_in['sel_ln_g'], 'L2_ffn_sel_ln_b': _L2_ffn_in['sel_ln_b'], 'L3_xattn_w_proj': _L3_xattn_in['w_proj'], 'L3_xattn_b_proj': _L3_xattn_in['b_proj'], 'L3_ffn_rW1': _L3_ffn_in['rW1'], 'L3_ffn_rb1': _L3_ffn_in['rb1'], 'L3_ffn_rW2': _L3_ffn_in['rW2'], 'L3_ffn_rb2': _L3_ffn_in['rb2'], 'L3_ffn_rW3': _L3_ffn_in['rW3'], 'L3_ffn_rb3': _L3_ffn_in['rb3'], 'L3_ffn_eW1': _L3_ffn_in['eW1'], 'L3_ffn_eb1': _L3_ffn_in['eb1'], 'L3_ffn_eW2': _L3_ffn_in['eW2'], 'L3_ffn_eb2': _L3_ffn_in['eb2']}

def reference(x, ctx_1024, L0_xattn_wq, L0_xattn_wk, L0_xattn_wv, L0_xattn_wo, L0_ffn_w_gate, L0_ffn_w1, L0_ffn_w2, L0_ffn_w3, L0_ffn_sw1, L0_ffn_sw2, L0_ffn_sw3, L0_ffn_expert_bias, L1_xattn_Wq, L1_xattn_bq, L1_xattn_Wk, L1_xattn_bk, L1_xattn_Wv, L1_xattn_bv, L1_ffn_ln_w, L1_ffn_Wg, L1_ffn_bg, L1_ffn_W1a, L1_ffn_b1a, L1_ffn_W1b, L1_ffn_b1b, L1_ffn_W2, L1_ffn_b2, L2_xattn_Wq, L2_ffn_index_b, L2_ffn_index_t, L2_ffn_sw1, L2_ffn_sb1, L2_ffn_sw2, L2_ffn_sb2, L2_ffn_sw3, L2_ffn_sb3, L2_ffn_s_ln_g, L2_ffn_s_ln_b, L2_ffn_sg_w, L2_ffn_sg_b, L2_ffn_eg_w, L2_ffn_eg_b, L2_ffn_exp_bias, L2_ffn_ew1, L2_ffn_eb1, L2_ffn_ew2, L2_ffn_eb2, L2_ffn_ew3, L2_ffn_eb3, L2_ffn_sel_ln_g, L2_ffn_sel_ln_b, L3_xattn_w_proj, L3_xattn_b_proj, L3_ffn_rW1, L3_ffn_rb1, L3_ffn_rW2, L3_ffn_rb2, L3_ffn_rW3, L3_ffn_rb3, L3_ffn_eW1, L3_ffn_eb1, L3_ffn_eW2, L3_ffn_eb2):
    import jax
    import jax.numpy as jnp

    def _L0_xattn_ref(queries, keys, values, wq, wk, wv, wo):
        import jax, jax.numpy as jnp
        import numpy as np
        import math
        D_MODEL = 128
        N_HEADS = 16
        C = 1
        B, L = (8, 256)

        def _glorot(key, fan):
            lim = np.sqrt(6.0 / (fan + fan)).astype(np.float32)
            return jax.random.uniform(key, (fan, fan), jnp.float32, -lim, lim)
        Bv, Lv, _ = queries.shape
        H = N_HEADS
        Dh = D_MODEL // N_HEADS
        Q = (queries @ wq).reshape(Bv, Lv, H, Dh).transpose(0, 2, 3, 1)
        K = (keys @ wk).reshape(Bv, Lv, H, Dh).transpose(0, 2, 3, 1)
        V = (values @ wv).reshape(Bv, Lv, H, Dh).transpose(0, 2, 3, 1)
        corr = jnp.fft.irfft(jnp.fft.rfft(Q, axis=-1) * jnp.conj(jnp.fft.rfft(K, axis=-1)), n=Lv, axis=-1)
        k_top = int(math.floor(C * math.log(Lv)))
        top_vals, top_idx = jax.lax.top_k(corr, k_top)
        w = jax.nn.softmax(top_vals, axis=-1)
        t = jnp.arange(Dh)
        out = jnp.zeros_like(V)
        for i in range(k_top):
            gather_idx = (t[None, None, :] - top_idx[..., i]) % Dh
            rolled = jnp.take_along_axis(V, gather_idx[..., None], axis=2)
            out = out + w[..., i, None] * rolled
        out = out.transpose(0, 2, 1, 3).reshape(Bv, Lv, D_MODEL)
        return out @ wo

    def _L0_ffn_ref(x, w_gate, w1, w2, w3, sw1, sw2, sw3, expert_bias):
        import jax, jax.numpy as jnp
        import numpy as np
        E = 8
        G = 4
        LG = 2
        TOPK = 2
        ROUTE_SCALE = 1.0

        def _grouped_mm(x, w, counts):
            counts = counts.astype(jnp.int32)
            if hasattr(jax.lax, 'ragged_dot'):
                return jax.lax.ragged_dot(x, w, counts)
            offs = jnp.cumsum(counts)
            eid = jnp.searchsorted(offs, jnp.arange(x.shape[0]), side='right')
            oh = jax.nn.one_hot(eid, w.shape[0], dtype=x.dtype)
            return jnp.einsum('nd,ne,edh->nh', x, oh, w)
        bs, slen, dim = x.shape
        xf = x.reshape(-1, dim)
        N = xf.shape[0]
        logits = xf @ w_gate.T
        scores = jax.nn.softmax(logits.astype(jnp.float32), axis=-1)
        original = scores
        s = (scores + expert_bias).reshape(N, G, E // G)
        group_scores = jax.lax.top_k(s, 2)[0].sum(-1)
        top_groups = jax.lax.top_k(group_scores, LG)[1]
        keep = jnp.zeros((N, G), bool).at[jnp.arange(N)[:, None], top_groups].set(True)
        masked = jnp.where(keep[:, :, None], s, -jnp.inf).reshape(N, E)
        topk_idx = jax.lax.top_k(masked, TOPK)[1]
        weights = (jnp.take_along_axis(original, topk_idx, axis=1) * ROUTE_SCALE).astype(x.dtype)
        counts = jnp.bincount(topk_idx.reshape(-1), length=E)
        flat_idx = topk_idx.reshape(-1)
        routed_in = xf[flat_idx]
        routed_in = (routed_in.astype(jnp.float32) * weights.reshape(-1, 1)).astype(x.dtype)
        h = jax.nn.silu(_grouped_mm(routed_in, w1, counts)) * _grouped_mm(routed_in, w3, counts)
        routed_out = _grouped_mm(h, w2, counts)
        shared = jax.nn.silu(xf @ sw1.T) * (xf @ sw3.T) @ sw2.T
        out = shared.at[flat_idx].add(routed_out)
        return out.reshape(bs, slen, dim)

    def _L1_xattn_ref(q, k, v, Wq, bq, Wk, bk, Wv, bv):
        import jax, jax.numpy as jnp
        import numpy as np
        B, S, D_IN, D_MODEL = (4, 256, 128, 128)
        qp = jnp.einsum('bsd,de->bse', q, Wq) + bq
        kp = jnp.einsum('bsd,de->bse', k, Wk) + bk
        vp = jnp.einsum('bsd,de->bse', v, Wv) + bv
        scale = 1.0 / jnp.sqrt(jnp.asarray(kp.shape[-1], jnp.float32))
        logits = jnp.einsum('bqe,bke->bqk', qp, kp) * scale
        attn = jax.nn.softmax(logits, axis=-1)
        return jnp.einsum('bqk,bke->bqe', attn, vp)

    def _L1_ffn_ref(x, ln_w, Wg, bg, W1a, b1a, W1b, b1b, W2, b2):
        import jax, jax.numpy as jnp
        import numpy as np
        E = 8
        K = 2
        B, S, D = x.shape
        eps = jnp.finfo(x.dtype).eps
        xn = x * jax.lax.rsqrt(jnp.mean(x * x, axis=-1, keepdims=True) + eps) * ln_w
        logits = xn @ Wg + bg
        vals, idx = jax.lax.top_k(logits, K)
        topk_w = jax.nn.softmax(vals, axis=-1)
        we = jnp.sum(jax.nn.one_hot(idx, E, dtype=x.dtype) * topk_w[..., None], axis=-2)
        T = B * S
        xf = xn.reshape(T, D)
        wef = we.reshape(T, E).T

        def step(acc, params):
            W1a_e, b1a_e, W1b_e, b1b_e, W2_e, b2_e, w_e = params
            a = xf @ W1a_e + b1a_e
            b = xf @ W1b_e + b1b_e
            y = jax.nn.silu(a) * b @ W2_e + b2_e
            return (acc + w_e[:, None] * y, None)
        out0 = jnp.zeros_like(xf)
        out, _ = jax.lax.scan(step, out0, (W1a, b1a, W1b, b1b, W2, b2, wef))
        return out.reshape(B, S, D)

    def _L2_xattn_ref(enc_outputs, x, Wq):
        import jax, jax.numpy as jnp
        import numpy as np
        B, L, D = (8, 256, 128)
        d_k = x.shape[-1]
        q = jnp.einsum('bld,hd->blh', x, Wq)
        k = jnp.einsum('bld,hd->blh', enc_outputs, Wq)
        v = k
        scores = jnp.einsum('bqh,bkh->bqk', q, k) / jnp.sqrt(jnp.float32(d_k))
        Lq, Lk = (scores.shape[1], scores.shape[2])
        causal = jnp.tril(jnp.ones((Lq, Lk), dtype=bool))
        scores = jnp.where(causal, scores, -jnp.inf)
        attn = jax.nn.softmax(scores, axis=-1)
        return jnp.einsum('bqk,bkh->bqh', attn, v)

    def _L2_ffn_ref(x, index_b, index_t, sw1, sb1, sw2, sb2, sw3, sb3, s_ln_g, s_ln_b, sg_w, sg_b, eg_w, eg_b, exp_bias, ew1, eb1, ew2, eb2, ew3, eb3, sel_ln_g, sel_ln_b):
        import jax, jax.numpy as jnp
        import numpy as np
        EPS = 1e-05

        def _ln(x, g, b):
            mu = jnp.mean(x, axis=-1, keepdims=True)
            var = jnp.mean(jnp.square(x - mu), axis=-1, keepdims=True)
            return (x - mu) * jax.lax.rsqrt(var + EPS) * g + b

        def _forward(x, index_b, index_t, sw1, sb1, sw2, sb2, sw3, sb3, s_ln_g, s_ln_b, sg_w, sg_b, eg_w, eg_b, exp_bias, ew1, eb1, ew2, eb2, ew3, eb3, sel_ln_g, sel_ln_b):
            x1 = jnp.einsum('btd,hd->bth', x, sw1) + sb1
            x2 = jnp.einsum('btd,hd->bth', x, sw2) + sb2
            sh = _ln(jax.nn.silu(x1) * x2, s_ln_g, s_ln_b)
            shared_out = jnp.einsum('bth,dh->btd', sh, sw3) + sb3
            x_moe = x[index_b, index_t]
            shared_scores = jax.nn.sigmoid(x_moe @ sg_w.T + sg_b)
            expert_scores = jax.nn.sigmoid(x_moe @ eg_w.T + eg_b)
            top1_idx = jnp.argmax(expert_scores + exp_bias, axis=-1)
            top1_score = jnp.take_along_axis(expert_scores, top1_idx[:, None], axis=-1)
            weights = jax.nn.softmax(jnp.concatenate([shared_scores, top1_score], axis=-1), axis=-1)
            shared_w, expert_w = (weights[:, 0], weights[:, 1])
            shared_moe_out = shared_out[index_b, index_t] * shared_w[:, None]
            h1 = jnp.einsum('md,ehd->meh', x_moe, ew1) + eb1
            h2 = jnp.einsum('md,ehd->meh', x_moe, ew2) + eb2
            z = _ln(jax.nn.silu(h1) * h2, sel_ln_g, sel_ln_b)
            out_all = jnp.einsum('meh,edh->med', z, ew3) + eb3
            expert_out = jnp.take_along_axis(out_all, top1_idx[:, None, None], axis=1)[:, 0]
            expert_moe_out = expert_out * expert_w[:, None]
            final_out = shared_out.at[index_b, index_t].set(shared_moe_out + expert_moe_out)
            return final_out
        return _forward(x, index_b, index_t, sw1, sb1, sw2, sb2, sw3, sb3, s_ln_g, s_ln_b, sg_w, sg_b, eg_w, eg_b, exp_bias, ew1, eb1, ew2, eb2, ew3, eb3, sel_ln_g, sel_ln_b)

    def _L3_xattn_ref(x, cond_k, cond_v, w_proj, b_proj):
        import jax, jax.numpy as jnp
        import numpy as np
        HEADS = 16
        B, T, W = x.shape
        S = cond_k.shape[1]
        H = HEADS
        d = W // H
        scale = 1.0 / jnp.sqrt(jnp.sqrt(jnp.float32(d)))
        q = x.reshape(B, T, H, d) * scale
        k = cond_k.reshape(B, S, H, d) * scale
        v = cond_v.reshape(B, S, H, d)
        scores = jnp.einsum('bthd,bshd->bhts', q, k)
        w = jax.nn.softmax(scores.astype(jnp.float32), axis=-1).astype(scores.dtype)
        out = jnp.einsum('bhts,bshd->bthd', w, v).reshape(B, T, W)
        return out @ w_proj.T + b_proj

    def _L3_ffn_ref(x, rW1, rb1, rW2, rb2, rW3, rb3, eW1, eb1, eW2, eb2):
        import jax, jax.numpy as jnp
        import numpy as np
        N_EMBD = 128
        N_EXPERTS = 8
        TOP_K = 2
        CAPACITY_FACTOR = 1.25
        B, T, C = x.shape
        E = rb3.shape[0]
        k = TOP_K
        capacity = int(T / E * CAPACITY_FACTOR)
        h = jax.nn.relu(x @ rW1 + rb1)
        h = jax.nn.relu(h @ rW2 + rb2)
        scales = jax.nn.softmax(h @ rW3 + rb3, axis=-1)
        topk_scales, topk_experts = jax.lax.top_k(scales, k)
        e_flat = topk_experts.reshape(B, T * k)
        onehot = jax.nn.one_hot(e_flat, E, dtype=jnp.int32)
        pos_excl = jnp.cumsum(onehot, axis=1) - onehot
        pos = jnp.take_along_axis(pos_excl, e_flat[..., None], axis=-1)[..., 0]
        keep = pos < capacity
        pos_c = jnp.where(keep, pos, capacity)
        b_idx = jnp.broadcast_to(jnp.arange(B)[:, None], (B, T * k))
        x_rep = jnp.repeat(x, k, axis=1)
        dispatched = jnp.zeros((E, B, capacity, C), x.dtype)
        dispatched = dispatched.at[e_flat, b_idx, pos_c].set(jnp.where(keep[..., None], x_rep, 0.0), mode='drop')
        hh = jax.nn.relu(jnp.einsum('ebnc,ech->ebnh', dispatched, eW1) + eb1[:, None, None, :])
        eout = jnp.einsum('ebnh,ehc->ebnc', hh, eW2) + eb2[:, None, None, :]
        gathered = eout[e_flat, b_idx, pos_c]
        gathered = jnp.where(keep[..., None], gathered, 0.0).reshape(B, T, k, C)
        out = jnp.sum(topk_scales[..., None] * gathered, axis=2)
        return out
    x = x + _L0_xattn_ref(_layernorm(x, axis=-1), ctx_1024, ctx_1024, L0_xattn_wq, L0_xattn_wk, L0_xattn_wv, L0_xattn_wo)
    x = x + _L0_ffn_ref(_layernorm(x, axis=-1), L0_ffn_w_gate, L0_ffn_w1, L0_ffn_w2, L0_ffn_w3, L0_ffn_sw1, L0_ffn_sw2, L0_ffn_sw3, L0_ffn_expert_bias)
    x = x + _L1_xattn_ref(_layernorm(x, axis=-1), ctx_1024, ctx_1024, L1_xattn_Wq, L1_xattn_bq, L1_xattn_Wk, L1_xattn_bk, L1_xattn_Wv, L1_xattn_bv)
    x = x + _L1_ffn_ref(_layernorm(x, axis=-1), L1_ffn_ln_w, L1_ffn_Wg, L1_ffn_bg, L1_ffn_W1a, L1_ffn_b1a, L1_ffn_W1b, L1_ffn_b1b, L1_ffn_W2, L1_ffn_b2)
    x = x + _L2_xattn_ref(ctx_1024, _layernorm(x, axis=-1), L2_xattn_Wq)
    x = x + _L2_ffn_ref(_layernorm(x, axis=-1), L2_ffn_index_b, L2_ffn_index_t, L2_ffn_sw1, L2_ffn_sb1, L2_ffn_sw2, L2_ffn_sb2, L2_ffn_sw3, L2_ffn_sb3, L2_ffn_s_ln_g, L2_ffn_s_ln_b, L2_ffn_sg_w, L2_ffn_sg_b, L2_ffn_eg_w, L2_ffn_eg_b, L2_ffn_exp_bias, L2_ffn_ew1, L2_ffn_eb1, L2_ffn_ew2, L2_ffn_eb2, L2_ffn_ew3, L2_ffn_eb3, L2_ffn_sel_ln_g, L2_ffn_sel_ln_b)
    x = x + _L3_xattn_ref(_layernorm(x, axis=-1), ctx_1024, ctx_1024, L3_xattn_w_proj, L3_xattn_b_proj)
    x = x + _L3_ffn_ref(_layernorm(x, axis=-1), L3_ffn_rW1, L3_ffn_rb1, L3_ffn_rW2, L3_ffn_rb2, L3_ffn_rW3, L3_ffn_rb3, L3_ffn_eW1, L3_ffn_eb1, L3_ffn_eW2, L3_ffn_eb2)
    return x

_drawn_inputs = setup_inputs


def setup_inputs(seed=0):
    import zlib

    import numpy as np

    out = dict(_drawn_inputs(seed))
    spreads = {'L0_ffn_expert_bias': (0.0, 0.8),
     'L1_ffn_ln_w': (1.0, 0.2),
     'L1_ffn_bg': (0.0, 0.1),
     'L1_ffn_b1a': (0.0, 0.1),
     'L1_ffn_b1b': (0.0, 0.1),
     'L1_ffn_b2': (0.0, 0.1),
     'L2_ffn_sb1': (0.0, 0.1),
     'L2_ffn_sb2': (0.0, 0.1),
     'L2_ffn_sb3': (0.0, 0.1),
     'L2_ffn_s_ln_g': (1.0, 0.6),
     'L2_ffn_s_ln_b': (0.0, 0.8),
     'L2_ffn_eg_b': (0.0, 0.695),
     'L2_ffn_exp_bias': (0.0, 0.457),
     'L2_ffn_eb1': (0.0, 0.8),
     'L2_ffn_eb2': (0.0, 0.8),
     'L2_ffn_eb3': (0.0, 0.8),
     'L2_ffn_sel_ln_g': (1.0, 0.6),
     'L2_ffn_sel_ln_b': (0.0, 0.8),
     'L3_xattn_b_proj': (0.0, 0.1),
     'L3_ffn_rb1': (0.0, 0.8),
     'L3_ffn_rb2': (0.0, 0.8),
     'L3_ffn_rb3': (0.0, 0.8),
     'L3_ffn_eb1': (0.0, 0.8),
     'L3_ffn_eb2': (0.0, 0.8)}
    factors = {'L0_ffn_w_gate': 8.0,
     'L0_ffn_w1': 8.0,
     'L0_ffn_w2': 8.0,
     'L0_ffn_w3': 8.0,
     'L0_ffn_sw1': 5.157,
     'L0_ffn_sw2': 3.756,
     'L0_ffn_sw3': 5.406,
     'L1_xattn_Wq': 4.606,
     'L1_xattn_bq': 8.0,
     'L1_xattn_Wk': 5.446,
     'L1_xattn_bk': 8.0,
     'L2_ffn_sg_w': 8.0,
     'L2_ffn_eg_w': 4.102,
     'L2_ffn_ew1': 4.902,
     'L2_ffn_ew2': 4.727,
     'L2_ffn_ew3': 4.426,
     'L3_ffn_rW1': 8.0,
     'L3_ffn_rW2': 8.0,
     'L3_ffn_rW3': 8.0,
     'L3_ffn_eW1': 8.0,
     'L3_ffn_eW2': 8.0}
    for name, (base, spread) in spreads.items():
        noise = np.random.default_rng([zlib.crc32(name.encode()), seed]).standard_normal(out[name].shape)
        drawn = base * np.exp(spread * noise) if base else spread * noise
        out[name] = jnp.asarray(drawn.astype(out[name].dtype))
    for name, factor in factors.items():
        out[name] = (out[name] * factor).astype(out[name].dtype)
    return out
```

```python
import math
from contextlib import ExitStack

import numpy as np

import concourse.bass as bass
from concourse import mybir

F32 = mybir.dt.float32
I32 = mybir.dt.int32
U32 = mybir.dt.uint32
ALU = mybir.AluOpType
ACT = mybir.ActivationFunctionType
AX = mybir.AxisListType

P = 128
B = 16
D = 128
T = 128
E = 8
QUAD = 4
GROUPS = B // QUAD
LN_EPS = 1e-5
RMS_EPS = float(np.finfo(np.float32).eps)
FAR = 1e30

CORR_TOP = int(math.floor(math.log(T)))
HEAD = 8
HEADS = D // HEAD
HID0 = 64
PAIRS = E * E
HID1 = 512
CH1 = HID1 // P
CAP1 = 52
HID2 = 64
M2 = 256
HID3 = 512
CH3 = HID3 // P
CAP = int(T / E * 1.25)
SLOTS = E * CAP
UPTO = 8

PACKS = {
    "fourier": [("dft", 2 * T), ("wk", D), ("wq", D), ("idft", 2 * T), ("wv", D), ("wo", D), ("ident", P)],
    "consts": [("blockmask", HEADS), ("dmod", 1), ("iota8", HEAD), ("prio", E), ("prio4", 4), ("lower", E * E),
               ("rownum", 2 * B), ("ones", P), ("before", P), ("causal", P), ("slot", CAP1), ("token", B),
               ("tokenrow", B * T), ("earlier", 2 * M2)],
    "l0f": [("wgateT", E), ("sw1T", P), ("sw3T", P), ("sw2T", D), ("ebias", E), ("w13", E * 2 * HID0), ("w2", E * D)],
    "l1x": [("Wq", D), ("Wk", D), ("Wv", D), ("bq", 1), ("bk", 1), ("bv", D)],
    "l1f": [("lnw", 1), ("Wg", E), ("bg", E), ("b2", E), ("b1a", E * CH1), ("b1b", E * CH1)],
    "l2": [("WqT", D), ("sw12T", 2 * HID2), ("sb12", 2 * HID2), ("sw3T", D), ("sb3", D), ("slng", 1), ("slnb", 1),
           ("gateT", E + 1), ("gateb", E + 1), ("expbias", E), ("ew1T", E * HID2), ("ew2T", E * HID2),
           ("eb1", E * HID2), ("eb2", E * HID2), ("ew3", E // 2 * D), ("eb3", D), ("sellng", HID2), ("sellnb", HID2)],
    "l3": [("wprojT", D), ("bproj", D), ("rb1", CH3), ("rb2", CH3), ("rW3", CH3 * E), ("rb3", E), ("eb1", E * CH3),
           ("eb2", E), ("rW1", HID3), ("rW2", CH3 * HID3)],
}


def pack_offsets(pack):
    at, out = 0, {}
    for name, n in PACKS[pack]:
        out[name] = (at, at + n)
        at += n
    return out, at


def build(nc, dram, out, upto):
    f = ExitStack()
    with f:
        sems = {}

        resting = [("l0x_" + n, c) for n, c in (
            ("khat_mm", B // 2), ("khat", B // 2), ("k_mm", 2 * GROUPS), ("k", 2 * GROUPS), ("u_mm", GROUPS), ("u", GROUPS),
            ("v_mm", GROUPS), ("v", GROUPS), ("qhat_mm", GROUPS), ("qhat", GROUPS), ("q_mm", GROUPS), ("prod", GROUPS),
            ("corr_mm", GROUPS), ("diff", 1), ("exp", 1), ("mix", GROUPS), ("mix_turned", GROUPS), ("mixed", GROUPS),
            ("out_mm", GROUPS))] + [("l0f_" + n, c) for n, c in (
                ("logits", 1), ("gate", GROUPS), ("up", GROUPS), ("gated", GROUPS), ("shared", GROUPS), ("added", GROUPS),
                ("counts", 1), ("local", 1), ("picked", 1), ("pair", 1))]
        heirs = ["l3x_" + n for n in ("values", "keys0", "keys1", "score", "probs", "turned", "probsT", "weigh", "weighed",
                                      "back", "att", "att_turned", "attT", "out", "cleared", "start", "largest")] + [
            "l3f_" + n for n in ("start", "first", "route1", "second", "route2", "third", "centred", "exp")]
        inherits = dict(zip(heirs, resting))

        def spent(name):
            return inherits[name][1]

        def sem(name):
            if name in inherits:
                name = inherits[name][0]
            if name not in sems:
                sems[name] = f.enter_context(nc.semaphore(name))
            return sems[name]

        every = ("l0x", "l0f", "l1x", "l1", "l2x", "l2f", "l3x", "l3")
        adds = {"norm_" + what: [(tag, n * (2 if tag == "l1" and what in ("var", "rstd") else 1)) for tag in every
                                 if not (tag == "l0x" and what in ("turned", "xnT"))]
                for what, n in (("var", 1), ("rstd", 1), ("xn", GROUPS), ("turned", GROUPS), ("xnT", GROUPS))}
        adds["norm_xn0"] = adds["norm_square"] = [("l1", GROUPS)]
        for what in ("start", "k_mm", "v_mm", "k", "v", "q_mm", "q", "logits", "neg", "exp", "turned2", "attnT", "out"):
            adds["attn_" + what] = [("l1x", 1 if what == "start" else GROUPS), ("l2x", 1 if what == "start" else GROUPS)]
        for what, n1, n3 in (("taken", 1, 1), ("before_mm", 1, 1), ("onehot", GROUPS, GROUPS), ("slots_mm", B, B),
                             ("slots", B, B), ("gate_mm", 2 * E * CH1, 0), ("silu", 2 * E * CH1, 0),
                             ("up_mm", 2 * E * CH1, E * CH3), ("hidden", 2 * E * CH1, E * CH3), ("down_mm", 2 * E, E),
                             ("y", 2 * E, E), ("weighted", 1, 1), ("turn_w", B, B), ("turn_y", B, B), ("turned_w", B, B),
                             ("turned_y", B, B), ("combined", B, B), ("ring0", 8 * E, 8 * E), ("ring1", 8 * E, 8 * E)):
            adds["slotted_" + what] = [("l1", n1), ("l3", n3)]

        def past(tag, name):
            tags = [t for t, _ in adds[name]]
            return sum(n for _, n in adds[name][:tags.index(tag)])

        def sb(name, shape, dt=F32):
            return f.enter_context(nc.sbuf_tensor(name, shape, dt))

        def spread(ap, axis, shape):
            return ap.unsqueeze(axis).to_broadcast(shape)

        ps = f.enter_context(nc.psum_tensor("ps", [P, 8, 512], F32))

        def bank(i):
            return ps[:, i, :]

        def bank4(i):
            return ps[:, i, :].rearrange("p (b c) -> p b c", b=QUAD)

        packed, field = {}, {}
        for pack in PACKS:
            offsets, width = pack_offsets(pack)
            packed[pack] = sb(f"pack_{pack}", [P, width])
            for name, (lo, hi) in offsets.items():
                field[pack, name] = packed[pack][:, lo:hi]
        x = sb("x", [P, B, D])
        xn = sb("xn", [P, B, D])
        xnT = sb("xnT", [P, B, T])
        ctx_tok = sb("ctx_tok", [P, B, D])
        ctxT = sb("ctxT", [P, B, T])
        stats = sb("stats", [P, B, 6])
        meanvar = sb("meanvar", [P, B, 2])
        vareps = sb("vareps", [P, B])
        rstd = sb("rstd", [P, B])
        minushalf = sb("minushalf", [P, B])
        index_sb = sb("index_sb", [P, 2, M2 + M2 // P], I32)
        arena_a = sb("arena_a", [P, 8192])
        arena_b = sb("arena_b", [P, 15360])

        def carve(arena):
            at = [0]

            def take(n, pattern=None, **sizes):
                ap = arena[:, at[0]:at[0] + n]
                at[0] += n
                assert at[0] <= arena.shape[1], at[0]
                return ap.rearrange(pattern, **sizes) if pattern else ap
            return take

        ident = field["fourier", "ident"]
        chain = [0]

        def link(v, ins):
            chain[0] += 1
            ins.then_inc(sem("vector_chain"), 1)
            v.wait_ge(sem("vector_chain"), chain[0])

        V = nc.vector
        S = nc.scalar
        TE = nc.tensor

        def norm(tag, rms=None):
            def vector(v):
                for b in range(B):
                    last = V.bn_stats(stats[:, b, :], x[:, b, :])
                link(v, last)
                for b in range(B):
                    last = V.bn_aggr(meanvar[:, b, :], stats[:, b, :])
                link(v, last)
                V.tensor_scalar_add(vareps[:, :], meanvar[:, :, 1], LN_EPS).then_inc(sem("norm_var"), 1)
                v.wait_ge(sem("norm_rstd"), past(tag, "norm_rstd") + 1)
                for b in range(B):
                    last = V.tensor_scalar(xn[:, b, :], x[:, b, :], meanvar[:, b, 0:1], rstd[:, b:b + 1],
                                           ALU.subtract, ALU.mult)
                    if b % QUAD == QUAD - 1:
                        last.then_inc(sem("norm_xn0" if rms else "norm_xn"), 1)
                if rms:
                    for g in range(GROUPS):
                        v.wait_ge(sem("norm_square"), past(tag, "norm_square") + g + 1)
                        last = V.tensor_reduce(vareps[:, QUAD * g:QUAD * g + QUAD], rms[0][:, QUAD * g:QUAD * g + QUAD, :],
                                               AX.X, ALU.add)
                    link(v, last)
                    V.tensor_scalar(vareps[:, :], vareps[:, :], 1.0 / D, RMS_EPS, ALU.mult,
                                    ALU.add).then_inc(sem("norm_var"), 1)
                    v.wait_ge(sem("norm_rstd"), past(tag, "norm_rstd") + 2)
                    for b in range(B):
                        last = V.tensor_scalar(xn[:, b, :], xn[:, b, :], rstd[:, b:b + 1], None, ALU.mult)
                        if b % QUAD == QUAD - 1:
                            last.then_inc(sem("norm_xn"), 1)

            def gpsimd(g):
                for i in range(2 if rms else 1):
                    g.wait_ge(sem("norm_var"), past(tag, "norm_var") + i + 1)
                    nc.gpsimd.tensor_tensor(rstd[:, :], vareps[:, :], minushalf[:, :], ALU.pow).then_inc(sem("norm_rstd"), 1)

            def tensor(pe):
                for g in range(GROUPS):
                    pe.wait_ge(sem("norm_xn"), past(tag, "norm_xn") + g + 1)
                    for i in range(QUAD):
                        last = TE.transpose(bank4(g)[:, i, :], xn[:, QUAD * g + i, :], ident)
                    last.then_inc(sem("norm_turned"), 1)

            def scalar(a):
                if rms:
                    for g in range(GROUPS):
                        a.wait_ge(sem("norm_xn0"), past(tag, "norm_xn0") + g + 1)
                        S.activation(rms[0][:, QUAD * g:QUAD * g + QUAD, :], xn[:, QUAD * g:QUAD * g + QUAD, :],
                                     ACT.Square).then_inc(sem("norm_square"), 1)
                for g in range(GROUPS):
                    a.wait_ge(sem("norm_turned"), past(tag, "norm_turned") + g + 1)
                    S.activation(xnT[:, QUAD * g:QUAD * g + QUAD, :], bank4(g), ACT.Copy if not rms else ACT.Identity,
                                 scale=rms[1] if rms else 1.0).then_inc(sem("norm_xnT"), 1)
            return vector, gpsimd, tensor, scalar

        def first_largest(v, onehot, score, prio, best, shape):
            link(v, V.tensor_reduce(best, score, AX.X, ALU.max))
            link(v, V.tensor_tensor(onehot, score, spread(best, len(shape) - 1, shape), ALU.is_equal))
            link(v, V.tensor_tensor(onehot, onehot, prio, ALU.mult))
            link(v, V.tensor_reduce(best, onehot, AX.X, ALU.max))
            link(v, V.tensor_tensor(onehot, onehot, spread(best, len(shape) - 1, shape), ALU.is_equal))

        def l0_attention():
            ta, tb = carve(arena_a), carve(arena_b)
            k_hat = ta(B * 2 * T, "p (b f) -> p b f", b=B)
            k1 = ta(B * D, "p (b d) -> p b d", b=B)
            k2 = ta(B * D, "p (b d) -> p b d", b=B)
            q_hat = tb(B * T, "p (b f) -> p b f", b=B)
            values = tb(B * D, "p (b o) -> p b o", b=B)
            prod1 = tb(B * D, "p (b d) -> p b d", b=B)
            prod2 = tb(B * D, "p (b d) -> p b d", b=B)
            mix_T = prod1
            mix = prod2
            top = tb(B * 8, "p (b k) -> p b k", b=B)
            where = tb(B * 8, "p (b k) -> p b k", b=B).bitcast(U32)
            wsoft = tb(B * CORR_TOP, "p (b k) -> p b k", b=B)
            wsum = tb(B)
            shift = tb(B * CORR_TOP, "p (b k) -> p b k", b=B)
            shift_i = tb(B * CORR_TOP, "p (b k) -> p b k", b=B).bitcast(I32)
            hit = tb(B * CORR_TOP * HEAD, "p (b k r) -> p b k r", b=B, k=CORR_TOP)
            mix8 = tb(B * HEAD, "p (b r) -> p b r", b=B)
            F = lambda n: field["fourier", n]
            C = lambda n: field["consts", n]

            def tensor(pe):
                pe.wait_ge(sem("load_fourier"), 16)
                pe.wait_ge(sem("load_ctx"), 32)
                for u in range(B // 2):
                    if u >= 4:
                        pe.wait_ge(sem("l0x_khat"), u - 3)
                    for i in range(2):
                        last = TE.matmul(bank(u % 4)[:, 256 * i:256 * i + 256], ctx_tok[:, 2 * u + i, :], F("dft"),
                                         start=True, stop=True)
                    last.then_inc(sem("l0x_khat_mm"), 1)
                for h in range(2):
                    for g in range(GROUPS):
                        pe.wait_ge(sem("l0x_khat"), 2 * g + 2)
                        if h:
                            pe.wait_ge(sem("l0x_k"), g + 1)
                        for i in range(QUAD):
                            last = TE.matmul(bank4(4 + g)[:, i, :], k_hat[:, QUAD * g + i, T * h:T * h + T], F("wk"),
                                             start=True, stop=True)
                        last.then_inc(sem("l0x_k_mm"), 1)
                pe.wait_ge(sem("l0x_khat"), B // 2)
                for g in range(GROUPS):
                    for i in range(QUAD):
                        last = TE.matmul(bank4(g)[:, i, :], ctx_tok[:, QUAD * g + i, :], F("wo"), start=True, stop=True)
                    last.then_inc(sem("l0x_u_mm"), 1)
                for g in range(GROUPS):
                    pe.wait_ge(sem("l0x_u"), g + 1)
                    last = TE.matmul(bank(g), F("wv"), q_hat[:, QUAD * g:QUAD * g + QUAD, :], start=True, stop=True)
                    last.then_inc(sem("l0x_v_mm"), 1)
                for g in range(GROUPS):
                    pe.wait_ge(sem("norm_xn"), past("l0x", "norm_xn") + g + 1)
                    pe.wait_ge(sem("l0x_k"), GROUPS + g + 1)
                    for i in range(QUAD):
                        last = TE.matmul(bank4(4 + g)[:, i, :], xn[:, QUAD * g + i, :], F("dft")[:, 0:T],
                                         start=True, stop=True)
                    last.then_inc(sem("l0x_qhat_mm"), 1)
                for g in range(GROUPS):
                    pe.wait_ge(sem("l0x_qhat"), g + 1)
                    pe.wait_ge(sem("l0x_v"), g + 1)
                    for i in range(QUAD):
                        last = TE.matmul(bank4(g)[:, i, :], q_hat[:, QUAD * g + i, :], F("wq"), start=True, stop=True)
                    last.then_inc(sem("l0x_q_mm"), 1)
                for g in range(GROUPS):
                    pe.wait_ge(sem("l0x_prod"), g + 1)
                    for i in range(QUAD):
                        b = QUAD * g + i
                        TE.matmul(bank4(4 + g)[:, i, :], prod1[:, b, :], F("idft")[:, 0:T], start=True, stop=False)
                        last = TE.matmul(bank4(4 + g)[:, i, :], prod2[:, b, :], F("idft")[:, T:2 * T],
                                         start=False, stop=True)
                    last.then_inc(sem("l0x_corr_mm"), 1)
                for g in range(GROUPS):
                    pe.wait_ge(sem("l0x_mix"), g + 1)
                    for i in range(QUAD):
                        last = TE.transpose(bank4(g)[:, i, :], mix_T[:, QUAD * g + i, :], ident)
                    last.then_inc(sem("l0x_mix_turned"), 1)
                for g in range(GROUPS):
                    pe.wait_ge(sem("l0x_mixed"), g + 1)
                    for i in range(QUAD):
                        b = QUAD * g + i
                        last = TE.matmul(bank4(4 + g)[:, i, :], mix[:, b, :], values[:, b, :], start=True, stop=True)
                    last.then_inc(sem("l0x_out_mm"), 1)

            def scalar(a):
                for u in range(B // 2):
                    a.wait_ge(sem("l0x_khat_mm"), u + 1)
                    S.copy(k_hat[:, 2 * u:2 * u + 2, :], bank(u % 4).rearrange("p (b f) -> p b f", b=2)
                           ).then_inc(sem("l0x_khat"), 1)
                for g in range(GROUPS):
                    a.wait_ge(sem("l0x_u_mm"), g + 1)
                    S.copy(q_hat[:, QUAD * g:QUAD * g + QUAD, :], bank4(g)).then_inc(sem("l0x_u"), 1)
                for g in range(GROUPS):
                    a.wait_ge(sem("l0x_v_mm"), g + 1)
                    S.copy(values[:, QUAD * g:QUAD * g + QUAD, :], bank4(g)).then_inc(sem("l0x_v"), 1)
                a.wait_ge(sem("l0x_v_mm"), GROUPS)
                for g in range(GROUPS):
                    a.wait_ge(sem("l0x_qhat_mm"), g + 1)
                    S.copy(q_hat[:, QUAD * g:QUAD * g + QUAD, :], bank4(4 + g)).then_inc(sem("l0x_qhat"), 1)
                a.wait_ge(sem("l0x_diff"), 1)
                S.activation(wsoft, wsoft, ACT.Exp).then_inc(sem("l0x_exp"), 1)
                for g in range(GROUPS):
                    a.wait_ge(sem("l0x_mix_turned"), g + 1)
                    S.copy(mix[:, QUAD * g:QUAD * g + QUAD, :].rearrange("p b (r h) -> p b h r", h=HEADS),
                           bank4(g).rearrange("p b (h r) -> p b h r", h=HEADS)).then_inc(sem("l0x_mixed"), 1)

            def vector(v):
                for h, dst in enumerate((k1, k2)):
                    for g in range(GROUPS):
                        v.wait_ge(sem("l0x_k_mm"), GROUPS * h + g + 1)
                        V.tensor_copy(dst[:, QUAD * g:QUAD * g + QUAD, :], bank4(4 + g)).then_inc(sem("l0x_k"), 1)
                v.wait_ge(sem("load_x"), 16)
                norm_l0x[0](v)
                v.wait_ge(sem("l0x_k"), 2 * GROUPS)
                for g in range(GROUPS):
                    s = slice(QUAD * g, QUAD * g + QUAD)
                    v.wait_ge(sem("l0x_q_mm"), g + 1)
                    V.tensor_tensor(prod1[:, s, :], bank4(g), k1[:, s, :], ALU.mult)
                    V.tensor_tensor(prod2[:, s, :], bank4(g), k2[:, s, :], ALU.mult).then_inc(sem("l0x_prod"), 1)
                for g in range(GROUPS):
                    v.wait_ge(sem("l0x_corr_mm"), g + 1)
                    for i in range(QUAD):
                        b = QUAD * g + i
                        last = V.max(top[:, b, :], bank4(4 + g)[:, i, :])
                    link(v, last)
                    for i in range(QUAD):
                        b = QUAD * g + i
                        last = V.max_index(where[:, b, :], top[:, b, :], bank4(4 + g)[:, i, :])
                link(v, last)
                four = [P, B, CORR_TOP]
                V.tensor_tensor(wsoft, top[:, :, 0:CORR_TOP], top[:, :, 0:1].to_broadcast(four),
                                ALU.subtract).then_inc(sem("l0x_diff"), 1)
                link(v, V.tensor_copy(shift, where[:, :, 0:CORR_TOP]))
                link(v, V.tensor_scalar(shift_i, shift, -1.0, C("dmod"), ALU.mult, ALU.add))
                link(v, V.tensor_scalar(shift_i, shift_i, HEAD - 1, None, ALU.bitwise_and))
                link(v, V.tensor_copy(shift, shift_i))
                full = [P, B, CORR_TOP, HEAD]
                link(v, V.tensor_tensor(hit, spread(shift, 3, full),
                                        C("iota8").unsqueeze(1).unsqueeze(1).to_broadcast(full), ALU.is_equal))
                v.wait_ge(sem("l0x_exp"), 1)
                link(v, V.tensor_reduce(wsum, wsoft, AX.X, ALU.add))
                link(v, V.reciprocal(wsum, wsum))
                link(v, V.tensor_tensor(wsoft, wsoft, spread(wsum, 2, four), ALU.mult))
                link(v, V.tensor_tensor(hit, hit, spread(wsoft, 3, full), ALU.mult))
                link(v, V.tensor_reduce(mix8, hit.rearrange("p b k r -> p b r k"), AX.X, ALU.add))
                for g in range(GROUPS):
                    s = slice(QUAD * g, QUAD * g + QUAD)
                    shape = [P, QUAD, HEADS, HEAD]
                    V.tensor_tensor(mix_T[:, s, :].rearrange("p b (h r) -> p b h r", h=HEADS),
                                    spread(mix8[:, s, :], 2, shape),
                                    C("blockmask").unsqueeze(1).unsqueeze(3).to_broadcast(shape),
                                    ALU.mult).then_inc(sem("l0x_mix"), 1)
                for g in range(GROUPS):
                    s = slice(QUAD * g, QUAD * g + QUAD)
                    v.wait_ge(sem("l0x_out_mm"), g + 1)
                    last = V.tensor_tensor(x[:, s, :], bank4(4 + g), x[:, s, :], ALU.add)
                link(v, last)
            norm_l0x = norm("l0x")
            return vector, norm_l0x[1], tensor, scalar

        def l0_experts():
            ta, tb = carve(arena_a), carve(arena_b)
            F = lambda n: field["l0f", n]
            C = lambda n: field["consts", n]
            gated = ta(B * T, "p (b l) -> p b l", b=B)
            pairT = ta(B * T, "p (b r) -> p b r", b=B)
            silu = ta(2 * 512, "p (i c) -> p i c", i=2)
            picked = ta(E * P, "p (g k e h) -> p g k e h", g=E, k=2, e=E)
            pair13 = ta(2 * HID0)
            sums = ta(HID0)
            hiddenT = ta(PAIRS)
            pair = tb(B * 2 * PAIRS, "p (r e g) -> p r e g", r=2 * B, e=E)
            pre = tb(2 * B * HID0, "p (k b h) -> p k b h", k=2, b=B)
            act = tb(2 * B * HID0, "p (k b h) -> p k b h", k=2, b=B)
            score = tb(B * E, "p (b e) -> p b e", b=B)
            biased = tb(B * E, "p (b e) -> p b e", b=B)
            group = tb(B * 4, "p (b e) -> p b e", b=B)
            hot4 = tb(B * 4, "p (b e) -> p b e", b=B)
            keep4 = tb(B * 4, "p (b e) -> p b e", b=B)
            best = tb(B)
            chosen = tb(B * 2 * E, "p (b k e) -> p b k e", b=B, k=2)
            tmp = tb(B * 2 * E, "p (b k e) -> p b k e", b=B, k=2)
            weight = tb(B * 2, "p (b k) -> p b k", b=B)
            local = tb(E)
            ends = tb(E)
            low = tb(E * E, "p (e c) -> p e c", e=E)
            reached = tb(2 * B * (E + 1), "p (r e) -> p r e", r=2 * B)
            member = tb(2 * B * E, "p (r e) -> p r e", r=2 * B)
            by8 = [P, B, E]
            by4 = [P, B, 4]
            n = norm("l0f")
            logits = bank(7)[:, 0:B * E].rearrange("p (b e) -> p b e", b=B)

            def tensor(pe):
                n[2](pe)
                pe.wait_ge(sem("load_l0f"), 16)
                pe.wait_ge(sem("norm_xnT"), past("l0f", "norm_xnT") + GROUPS)
                for b in range(B):
                    last = TE.matmul(logits[:, b, :], xnT[:, b, :], F("wgateT"), start=True, stop=True)
                last.then_inc(sem("l0f_logits"), 1)
                def down(g):
                    pe.wait_ge(sem("l0f_gated"), g + 1)
                    if g >= 2:
                        pe.wait_ge(sem("l0f_added"), g - 1)
                    for i in range(QUAD):
                        last = TE.matmul(bank4(4 + g % 2)[:, i, :], gated[:, QUAD * g + i, :], F("sw2T"),
                                         start=True, stop=True)
                    last.then_inc(sem("l0f_shared"), 1)
                for g in range(GROUPS):
                    if g >= 2:
                        pe.wait_ge(sem("l0f_gated"), g - 1)
                    xb = xnT[:, QUAD * g:QUAD * g + QUAD, :]
                    TE.matmul(bank(g % 2), F("sw1T"), xb, start=True, stop=True).then_inc(sem("l0f_gate"), 1)
                    TE.matmul(bank(2 + g % 2), F("sw3T"), xb, start=True, stop=True).then_inc(sem("l0f_up"), 1)
                    if g:
                        down(g - 1)
                down(GROUPS - 1)
                pe.wait_ge(sem("l0f_local"), 1)
                TE.matmul(bank(7)[:, 256:256 + E], C("ones"), local, start=True, stop=True).then_inc(sem("l0f_counts"), 1)
                pe.wait_ge(sem("l0f_picked"), 1)
                for g in range(E):
                    last = TE.matmul(bank(6)[:, 0:2 * HID0], picked[:, g, :, :, :],
                                     F("w13")[:, 2 * HID0 * g:2 * HID0 * (g + 1)], start=(g == 0), stop=(g == E - 1))
                last.then_inc(sem("l0f_pair13_mm"), 1)
                pe.wait_ge(sem("l0f_pair"), 1)
                for g in range(GROUPS):
                    if g < 2:
                        pe.wait_ge(sem("l0f_gated"), GROUPS)
                    for i in range(QUAD):
                        last = TE.transpose(bank4(g)[:, i, :], pair[:, 2 * (QUAD * g + i):2 * (QUAD * g + i) + 2, :, :],
                                            ident)
                    last.then_inc(sem("l0f_pair_turned"), 1)
                pe.wait_ge(sem("l0f_pair13"), 1)
                pe.wait_ge(sem("l0f_pairT"), GROUPS)
                pe.wait_ge(sem("l0f_added"), GROUPS)
                for b in range(B):
                    for k in range(2):
                        last = TE.matmul(bank(4 + 2 * k + b // 8)[:, HID0 * (b % 8):HID0 * (b % 8) + HID0],
                                         pairT[PAIRS * k:PAIRS * k + PAIRS, b, :],
                                         pair13[PAIRS * k:PAIRS * k + PAIRS, 0:HID0], start=True, stop=True)
                last.then_inc(sem("l0f_pre_mm"), 1)
                pe.wait_ge(sem("l0f_act"), 1)
                for k in range(2):
                    for b in range(B):
                        last = TE.matmul(bank(0)[0:PAIRS, 0:HID0], pair[:, 2 * b + k, :, :], act[:, k, b, :],
                                         start=(k == 0 and b == 0), stop=(k == 1 and b == B - 1))
                last.then_inc(sem("l0f_sums_mm"), 1)
                pe.wait_ge(sem("l0f_hidden"), 1)
                TE.transpose(bank(1)[0:HID0, 0:PAIRS], sums[0:PAIRS, :], ident[0:PAIRS, 0:PAIRS]).then_inc(sem("l0f_hidden_turned"), 1)
                pe.wait_ge(sem("l0f_hiddenT"), 1)
                hT = hiddenT[0:HID0, :].rearrange("p (e g) -> p g e", e=E)
                for g in range(E):
                    last = TE.matmul(bank(2)[0:E, 0:D], hT[:, g, :], F("w2")[0:HID0, D * g:D * g + D],
                                     start=(g == 0), stop=(g == E - 1))
                last.then_inc(sem("l0f_routed"), 1)

            def scalar(a):
                n[3](a)
                a.wait_ge(sem("l0f_centred"), 1)
                S.activation(score, score, ACT.Exp).then_inc(sem("l0f_exp"), 1)
                for g in range(GROUPS):
                    a.wait_ge(sem("l0f_gate"), g + 1)
                    if g >= 2:
                        a.wait_ge(sem("l0f_gated"), g - 1)
                    S.activation(silu[:, g % 2, :], bank(g % 2), ACT.Silu).then_inc(sem("l0f_silu"), 1)
                for g in range(GROUPS):
                    a.wait_ge(sem("l0f_pair_turned"), g + 1)
                    S.copy(pairT[:, QUAD * g:QUAD * g + QUAD, :], bank4(g)).then_inc(sem("l0f_pairT"), 1)
                for k in range(2):
                    a.wait_ge(sem("l0f_pre"), k + 1)
                    S.activation(act[:, k, :, :], pre[:, k, :, :], ACT.Silu).then_inc(sem("l0f_silu2"), 1)

            def vector(v):
                n[0](v)
                v.wait_ge(sem("load_l0f"), 16)
                link(v, V.memset(picked, 0.0))
                v.wait_ge(sem("norm_xnT"), past("l0f", "norm_xnT") + 1)
                for g in range(E):
                    last = V.tensor_copy(picked[:, g, :, :, g], spread(xnT[:, 0, 0:E], 1, [P, 2, E]))
                last.then_inc(sem("l0f_picked"), 1)
                v.wait_ge(sem("l0f_logits"), 1)
                link(v, V.tensor_reduce(best, logits, AX.X, ALU.max))
                V.tensor_tensor(score, logits, spread(best, 2, by8), ALU.subtract).then_inc(sem("l0f_centred"), 1)
                def shared(g):
                    v.wait_ge(sem("l0f_silu"), g + 1)
                    v.wait_ge(sem("l0f_up"), g + 1)
                    V.tensor_tensor(gated[:, QUAD * g:QUAD * g + QUAD, :],
                                    silu[:, g % 2, :].rearrange("p (b l) -> p b l", b=QUAD),
                                    bank4(2 + g % 2), ALU.mult).then_inc(sem("l0f_gated"), 1)
                def shared_add(g):
                    v.wait_ge(sem("l0f_shared"), g + 1)
                    s = slice(QUAD * g, QUAD * g + QUAD)
                    V.tensor_tensor(x[:, s, :], bank4(4 + g % 2), x[:, s, :], ALU.add).then_inc(sem("l0f_added"), 1)
                v.wait_ge(sem("l0f_exp"), 1)
                link(v, V.tensor_reduce(best, score, AX.X, ALU.add))
                link(v, V.reciprocal(best, best))
                link(v, V.tensor_tensor(score, score, spread(best, 2, by8), ALU.mult))
                link(v, V.tensor_tensor(biased, score, spread(F("ebias"), 1, by8), ALU.add))
                pairs = biased.rearrange("p b (g i) -> p b g i", i=2)
                link(v, V.tensor_tensor(group, pairs[:, :, :, 0], pairs[:, :, :, 1], ALU.add))
                prio4 = spread(C("prio4"), 1, by4)
                prio = spread(C("prio"), 1, by8)
                first_largest(v, keep4, group, prio4, best, by4)
                link(v, V.scalar_tensor_tensor(group, keep4, -FAR, group, ALU.mult, ALU.add))
                first_largest(v, hot4, group, prio4, best, by4)
                link(v, V.tensor_tensor(keep4, keep4, hot4, ALU.add))
                link(v, V.tensor_scalar(keep4, keep4, -1.0, FAR, ALU.add, ALU.mult))
                link(v, V.tensor_tensor(pairs, pairs, spread(keep4, 3, [P, B, 4, 2]), ALU.add))
                shared(0)
                for k in range(2):
                    first_largest(v, chosen[:, :, k, :], biased, prio, best, by8)
                    if k == 0:
                        link(v, V.scalar_tensor_tensor(biased, chosen[:, :, k, :], -FAR, biased, ALU.mult, ALU.add))
                    shared(1 + k)
                    shared_add(k)
                link(v, V.tensor_tensor(tmp, chosen, spread(score, 2, [P, B, 2, E]), ALU.mult))
                link(v, V.tensor_reduce(weight, tmp, AX.X, ALU.add))
                V.tensor_reduce(local, chosen.rearrange("p b k e -> p e b k"), AX.XY, ALU.add).then_inc(sem("l0f_local"), 1)
                shared(3)
                shared_add(2)
                shared_add(3)
                v.wait_ge(sem("l0f_counts"), 1)
                link(v, V.tensor_tensor(low, C("lower").rearrange("p (e c) -> p e c", e=E),
                                        spread(bank(7)[:, 256:256 + E], 1, [P, E, E]), ALU.mult))
                link(v, V.tensor_reduce(ends, low, AX.X, ALU.add))
                rows9 = [P, 2 * B, E]
                V.memset(reached[:, :, 0], 1.0)
                link(v, V.tensor_tensor(reached[:, :, 1:E + 1], spread(C("rownum"), 2, rows9),
                                        spread(ends, 1, rows9), ALU.is_ge))
                link(v, V.tensor_tensor(member, reached[:, :, 0:E], reached[:, :, 1:E + 1], ALU.subtract))
                full = [P, 2 * B, E, E]
                V.tensor_tensor(pair, spread(chosen.rearrange("p b k e -> p (b k) e"), 3, full),
                                spread(member, 2, full), ALU.mult).then_inc(sem("l0f_pair"), 1)
                v.wait_ge(sem("l0f_pair13_mm"), 1)
                V.tensor_copy(pair13, bank(6)[:, 0:2 * HID0]).then_inc(sem("l0f_pair13"), 1)
                v.wait_ge(sem("l0f_pre_mm"), 1)
                for k in range(2):
                    V.tensor_tensor(pre[:, k, :, :], ps[:, 4 + 2 * k:6 + 2 * k, :].rearrange("p c (b h) -> p (c b) h", b=8),
                                    spread(weight[:, :, k], 2, [P, B, HID0]), ALU.mult).then_inc(sem("l0f_pre"), 1)
                v.wait_ge(sem("l0f_silu2"), 2)
                for k in range(2):
                    last = V.tensor_tensor(act[:, k, :, :], act[:, k, :, :], spread(weight[:, :, k], 2, [P, B, HID0]), ALU.mult)
                last.then_inc(sem("l0f_act"), 1)
                v.wait_ge(sem("l0f_sums_mm"), 1)
                V.tensor_tensor(sums[0:PAIRS, :], bank(0)[0:PAIRS, 0:HID0], pair13[0:PAIRS, HID0:2 * HID0],
                                ALU.mult).then_inc(sem("l0f_hidden"), 1)
                v.wait_ge(sem("l0f_hidden_turned"), 1)
                V.tensor_copy(hiddenT[0:HID0, :], bank(1)[0:HID0, 0:PAIRS]).then_inc(sem("l0f_hiddenT"), 1)
                v.wait_ge(sem("l0f_routed"), 1)
                link(v, V.tensor_tensor(x[0:E, 0, :], bank(2)[0:E, 0:D], x[0:E, 0, :], ALU.add))
            return vector, n[1], tensor, scalar

        def attention(tag, pack, wq, wk, wv, bq=None, bk=None, bv=None, causal=False):
            tb = carve(arena_b)
            qT = tb(B * T, "p (b l) -> p b l", b=B)
            attn = tb(B * T, "p (b l) -> p b l", b=B)
            attnT = tb(B * T, "p (b l) -> p b l", b=B)
            kT = tb(B * T, "p (b l) -> p b l", b=B)
            vals = tb(B * D, "p (b d) -> p b d", b=B)
            neg = tb(B)
            total = tb(B)
            F = lambda name: field[pack, name]
            scale = 1.0 / math.sqrt(D)
            n = norm(tag)
            quad = lambda ap, g: ap[:, QUAD * g:QUAD * g + QUAD, :]

            def tensor(pe):
                pe.wait_ge(sem("load_" + pack), 16)
                pe.wait_ge(sem("attn_start"), past(tag, "attn_start") + 1)
                for g in range(GROUPS):
                    TE.matmul(bank(g), F(wk), quad(ctxT, g), start=True, stop=True).then_inc(sem("attn_k_mm"), 1)
                    for i in range(QUAD):
                        last = TE.matmul(bank4(4 + g)[:, i, :], ctxT[:, QUAD * g + i, :], F(wv), start=True, stop=True)
                    last.then_inc(sem("attn_v_mm"), 1)
                pe.wait_ge(sem("attn_k"), past(tag, "attn_k") + GROUPS)
                n[2](pe)
                for g in range(GROUPS):
                    pe.wait_ge(sem("norm_xnT"), past(tag, "norm_xnT") + g + 1)
                    TE.matmul(bank(g), F(wq), quad(xnT, g), start=True, stop=True).then_inc(sem("attn_q_mm"), 1)
                pe.wait_ge(sem("attn_v"), past(tag, "attn_v") + GROUPS)
                for g in range(GROUPS):
                    pe.wait_ge(sem("attn_q"), past(tag, "attn_q") + g + 1)
                    for i in range(QUAD):
                        b = QUAD * g + i
                        last = TE.matmul(bank4(4 + g)[:, i, :], qT[:, b, :], kT[:, b, :], start=True, stop=True)
                    last.then_inc(sem("attn_logits"), 1)
                for g in range(GROUPS):
                    pe.wait_ge(sem("attn_exp"), past(tag, "attn_exp") + g + 1)
                    for i in range(QUAD):
                        last = TE.transpose(bank4(g)[:, i, :], attn[:, QUAD * g + i, :], ident)
                    last.then_inc(sem("attn_turned2"), 1)
                for g in range(GROUPS):
                    pe.wait_ge(sem("attn_attnT"), past(tag, "attn_attnT") + g + 1)
                    for i in range(QUAD):
                        b = QUAD * g + i
                        last = TE.matmul(bank4(4 + g)[:, i, :], attnT[:, b, :], vals[:, b, :], start=True, stop=True)
                    last.then_inc(sem("attn_out"), 1)

            def scalar(a):
                for g in range(GROUPS):
                    a.wait_ge(sem("attn_k_mm"), past(tag, "attn_k_mm") + g + 1)
                    if bk:
                        last = S.activation(quad(kT, g), bank4(g), ACT.Identity, bias=F(bk))
                    else:
                        last = S.copy(quad(kT, g), bank4(g))
                    last.then_inc(sem("attn_k"), 1)
                n[3](a)
                for g in range(GROUPS):
                    a.wait_ge(sem("attn_neg"), past(tag, "attn_neg") + g + 1)
                    for i in range(QUAD):
                        b = QUAD * g + i
                        src = attn[:, b, :] if causal else bank4(4 + g)[:, i, :]
                        last = S.activation(attn[:, b, :], src, ACT.Exp, bias=neg[:, b:b + 1], accum_out=total[:, b:b + 1])
                    last.then_inc(sem("attn_exp"), 1)

            def vector(v):
                v.sem_inc(sem("attn_start"), 1)
                v.wait_ge(sem("load_" + pack), 16)
                for g in range(GROUPS):
                    v.wait_ge(sem("attn_v_mm"), past(tag, "attn_v_mm") + g + 1)
                    if bv:
                        last = V.tensor_tensor(quad(vals, g), bank4(4 + g), spread(F(bv), 1, [P, QUAD, D]), ALU.add)
                    else:
                        last = V.tensor_copy(quad(vals, g), bank4(4 + g))
                    last.then_inc(sem("attn_v"), 1)
                n[0](v)
                for g in range(GROUPS):
                    v.wait_ge(sem("attn_q_mm"), past(tag, "attn_q_mm") + g + 1)
                    V.tensor_scalar(quad(qT, g), bank4(g), F(bq) if bq else 0.0, scale, ALU.add,
                                    ALU.mult).then_inc(sem("attn_q"), 1)
                for g in range(GROUPS):
                    v.wait_ge(sem("attn_logits"), past(tag, "attn_logits") + g + 1)
                    src = bank4(4 + g)
                    if causal:
                        src = quad(attn, g)
                        link(v, V.tensor_tensor(src, bank4(4 + g), spread(field["consts", "causal"], 1, [P, QUAD, T]), ALU.add))
                    V.tensor_reduce(neg[:, QUAD * g:QUAD * g + QUAD], src, AX.X, ALU.max,
                                    negate=True).then_inc(sem("attn_neg"), 1)
                for g in range(GROUPS):
                    v.wait_ge(sem("attn_turned2"), past(tag, "attn_turned2") + g + 1)
                    V.tensor_copy(quad(attnT, g), bank4(g)).then_inc(sem("attn_attnT"), 1)
                link(v, V.reciprocal(total, total))
                for g in range(GROUPS):
                    v.wait_ge(sem("attn_out"), past(tag, "attn_out") + g + 1)
                    for i in range(QUAD):
                        b = QUAD * g + i
                        last = V.scalar_tensor_tensor(x[:, b, :], bank4(4 + g)[:, i, :], total[:, b:b + 1], x[:, b, :],
                                                      ALU.mult, ALU.add)
                link(v, last)
            return vector, n[1], tensor, scalar

        def slotted(tag, cap, nb, gated, onehot, slots, hidden, silu, ring, turned_w, turned_y, taken, slotpos, weights,
                    up_bias, gate_bias, out_bias, channel_scale):
            per = E * cap
            parts = 4
            part = per // parts
            units = [(e, b0) for e in range(E) for b0 in range(0, B, nb)]
            cols = nb * cap
            nw = 2 if gated else 1
            s_ = lambda what: sem("slotted_" + what)
            hot = onehot.rearrange("p (b e c) -> p b e c", b=B, e=E)
            sl = slots.rearrange("p (b e c) -> p b e c", e=E, b=B)
            hid = hidden.rearrange("p (i f n) -> p i f n", i=2, f=CH1)

            def weights_of(e):
                w = ring[:, e % 2, :]
                up = w[:, 0:nw * HID1].rearrange("p (i n) -> p i n", i=nw)
                down = w[:, nw * HID1:nw * HID1 + CH1 * D].rearrange("p (f n) -> p f n", f=CH1)
                return up, down

            def sync(sp):
                for e in range(E):
                    if e >= 2:
                        sp.wait_ge(s_("down_mm"), past(tag, "slotted_down_mm") + (B // nb) * (e - 1))
                    sp.dma_start(ring[:, e % 2, :], dram[tag + "_experts"][e, :, :]).then_inc(s_(f"ring{e % 2}"), 16)

            def positions_tensor(pe):
                pe.wait_ge(s_("taken"), past(tag, "slotted_taken") + 1)
                TE.matmul(bank(6)[:, 0:B * E], field["consts", "before"], taken, start=True,
                          stop=True).then_inc(s_("before_mm"), 1)

            def tensor(pe):
                for b in range(B):
                    pe.wait_ge(s_("onehot"), past(tag, "slotted_onehot") + b // QUAD + 1)
                    if b >= 4:
                        pe.wait_ge(s_("slots"), past(tag, "slotted_slots") + b - 3)
                    TE.matmul(bank(b % 4)[:, 0:per], xn[:, b, :], hot[:, b, :, :], start=True,
                              stop=True).then_inc(s_("slots_mm"), 1)
                pe.wait_ge(s_("slots"), past(tag, "slotted_slots") + B)

                def down(u):
                    e, b0 = units[u]
                    pe.wait_ge(s_("hidden"), past(tag, "slotted_hidden") + CH1 * (u + 1))
                    if u >= 2:
                        pe.wait_ge(s_("y"), past(tag, "slotted_y") + u - 1)
                    for f in range(CH1):
                        last = TE.matmul(bank(4 + u % 2)[:, 0:cols], weights_of(e)[1][:, f, :], hid[:, u % 2, f, :],
                                         start=(f == 0), stop=(f == CH1 - 1))
                    last.then_inc(s_("down_mm"), 1)
                for u, (e, b0) in enumerate(units):
                    if b0 == 0:
                        pe.wait_ge(s_(f"ring{e % 2}"), past(tag, f"slotted_ring{e % 2}") + 16 * (e // 2 + 1))
                    for f in range(CH1):
                        k = CH1 * u + f
                        if k >= 2:
                            pe.wait_ge(s_("hidden"), past(tag, "slotted_hidden") + k - 1)
                        for i in range(nw):
                            last = TE.matmul(bank(2 * i + k % 2)[:, 0:cols], weights_of(e)[0][:, i, P * f:P * f + P],
                                             sl[:, b0:b0 + nb, e, :], start=True, stop=True)
                            if gated and i == 0:
                                last.then_inc(s_("gate_mm"), 1)
                        last.then_inc(s_("up_mm"), 1)
                    if u:
                        down(u - 1)
                down(len(units) - 1)
                pe.wait_ge(s_("weighted"), past(tag, "slotted_weighted") + 1)
                pe.wait_ge(s_("y"), past(tag, "slotted_y") + len(units))

                def turn(b):
                    if b >= 2:
                        pe.wait_ge(s_("turned_w"), past(tag, "slotted_turned_w") + b - 1)
                        pe.wait_ge(s_("turned_y"), past(tag, "slotted_turned_y") + b - 1)
                    for j in range(parts):
                        last = TE.transpose(bank4(b % 2)[0:part, j, :], hot[:, b, 2 * j:2 * j + 2, :], ident)
                    last.then_inc(s_("turn_w"), 1)
                    for j in range(parts):
                        last = TE.transpose(bank4(2 + b % 2)[0:part, j, :], sl[:, b, 2 * j:2 * j + 2, :], ident)
                    last.then_inc(s_("turn_y"), 1)
                turn(0)
                for b in range(B):
                    if b + 1 < B:
                        turn(b + 1)
                    pe.wait_ge(s_("turned_w"), past(tag, "slotted_turned_w") + b + 1)
                    pe.wait_ge(s_("turned_y"), past(tag, "slotted_turned_y") + b + 1)
                    for j in range(parts):
                        last = TE.matmul(bank4(4 + b // QUAD)[:, b % QUAD, :], turned_w[0:part, b % 2, j, :],
                                         turned_y[0:part, b % 2, j, :], start=(j == 0), stop=(j == parts - 1))
                    last.then_inc(s_("combined"), 1)

            def scalar(a):
                for b in range(B):
                    a.wait_ge(s_("slots_mm"), past(tag, "slotted_slots_mm") + b + 1)
                    src = bank(b % 4)[:, 0:per].rearrange("p (e c) -> p e c", e=E)
                    if channel_scale is None:
                        last = S.copy(sl[:, b, :, :], src)
                    else:
                        last = S.activation(sl[:, b, :, :], src, ACT.Identity, scale=channel_scale)
                    last.then_inc(s_("slots"), 1)

                for u, (e, b0) in enumerate(units):
                    for f in range(CH1):
                        k = CH1 * u + f
                        col = CH1 * e + f
                        if gated:
                            a.wait_ge(s_("gate_mm"), past(tag, "slotted_gate_mm") + k + 1)
                            if k >= 2:
                                a.wait_ge(s_("hidden"), past(tag, "slotted_hidden") + k - 1)
                            S.activation(silu[:, k % 2, 0:cols], bank(k % 2)[:, 0:cols], ACT.Silu,
                                         bias=gate_bias[:, col:col + 1]).then_inc(s_("silu"), 1)
                        else:
                            a.wait_ge(s_("up_mm"), past(tag, "slotted_up_mm") + k + 1)
                            S.activation(hid[:, u % 2, f, :], bank(k % 2)[:, 0:cols], ACT.Relu,
                                         bias=up_bias[:, col:col + 1]).then_inc(s_("hidden"), 1)
                for b in range(B):
                    a.wait_ge(s_("turn_w"), past(tag, "slotted_turn_w") + b + 1)
                    if b >= 2:
                        a.wait_ge(s_("combined"), past(tag, "slotted_combined") + b - 1)
                    S.copy(turned_w[0:part, b % 2, :, :], bank4(b % 2)[0:part, :, :]).then_inc(s_("turned_w"), 1)

            def vector(v):
                v.wait_ge(s_("before_mm"), past(tag, "slotted_before_mm") + 1)
                link(v, V.scalar_tensor_tensor(slotpos, bank(6)[:, 0:B * E], 1.0, taken, ALU.add, ALU.mult))
                link(v, V.tensor_scalar(slotpos, slotpos, -1.0, None, ALU.add))
                pos = slotpos.rearrange("p (b e) -> p b e", b=B)
                shape = [P, QUAD * E, cap]
                flat = onehot.rearrange("p (r c) -> p r c", c=cap)
                for g in range(GROUPS):
                    r = slice(QUAD * E * g, QUAD * E * (g + 1))
                    V.tensor_tensor(flat[:, r, :], spread(slotpos[:, r], 2, shape),
                                    spread(field["consts", "slot"][:, 0:cap], 1, shape), ALU.is_equal).then_inc(s_("onehot"), 1)
                for g in range(GROUPS):
                    r = slice(QUAD * E * g, QUAD * E * (g + 1))
                    v.wait_ge(s_("slots_mm"), past(tag, "slotted_slots_mm") + QUAD * (g + 1))
                    last = V.tensor_tensor(flat[:, r, :], flat[:, r, :], spread(weights[:, r], 2, shape), ALU.mult)
                last.then_inc(s_("weighted"), 1)

                def y(u):
                    e, b0 = units[u]
                    v.wait_ge(s_("down_mm"), past(tag, "slotted_down_mm") + u + 1)
                    V.tensor_scalar(sl[:, b0:b0 + nb, e, :], bank(4 + u % 2)[:, 0:cols].rearrange("p (b c) -> p b c", b=nb),
                                    out_bias[:, e:e + 1], None, ALU.add).then_inc(s_("y"), 1)
                for u, (e, b0) in enumerate(units):
                    if gated:
                        for f in range(CH1):
                            k = CH1 * u + f
                            col = CH1 * e + f
                            if u >= 2 and f == 0:
                                v.wait_ge(s_("down_mm"), past(tag, "slotted_down_mm") + u - 1)
                            v.wait_ge(s_("silu"), past(tag, "slotted_silu") + k + 1)
                            v.wait_ge(s_("up_mm"), past(tag, "slotted_up_mm") + k + 1)
                            V.scalar_tensor_tensor(hid[:, u % 2, f, :], bank(2 + k % 2)[:, 0:cols], up_bias[:, col:col + 1],
                                                   silu[:, k % 2, 0:cols], ALU.add, ALU.mult).then_inc(s_("hidden"), 1)
                    if u:
                        y(u - 1)
                y(len(units) - 1)
                for b in range(B):
                    v.wait_ge(s_("turn_y"), past(tag, "slotted_turn_y") + b + 1)
                    if b >= 2:
                        v.wait_ge(s_("combined"), past(tag, "slotted_combined") + b - 1)
                    V.tensor_copy(turned_y[0:part, b % 2, :, :], bank4(2 + b % 2)[0:part, :, :]).then_inc(s_("turned_y"), 1)
                for g in range(GROUPS):
                    v.wait_ge(s_("combined"), past(tag, "slotted_combined") + QUAD * (g + 1))
                    q = slice(QUAD * g, QUAD * g + QUAD)
                    last = V.tensor_tensor(x[:, q, :], bank4(4 + g), x[:, q, :], ALU.add)
                link(v, last)
            return sync, positions_tensor, tensor, scalar, vector

        def l1_experts():
            ta, tb = carve(arena_a), carve(arena_b)
            F = lambda name: field["l1f", name]
            C = lambda name: field["consts", name]
            hidden = ta(2 * CH1 * (B // 2) * CAP1)
            silu = ta(2 * (B // 2) * CAP1, "p (i n) -> p i n", i=2)
            ring = ta(2 * 3 * HID1, "p (i n) -> p i n", i=2)
            onehot = tb(B * E * CAP1)
            slots = tb(B * E * CAP1)
            score = tb(B * E, "p (b e) -> p b e", b=B)
            left = tb(B * E, "p (b e) -> p b e", b=B)
            chosen = tb(B * 2 * E, "p (b k e) -> p b k e", b=B, k=2)
            tmp = tb(B * 2 * E, "p (b k e) -> p b k e", b=B, k=2)
            best = tb(B)
            weight = tb(B * 2, "p (b k) -> p b k", b=B)
            second = tb(B)
            taken = tb(B * E)
            slotpos = tb(B * E)
            weights = tb(B * E)
            turned_w = hidden[:, 0:1024].rearrange("p (i j n) -> p i j n", i=2, j=4)
            turned_y = hidden[:, 1024:2048].rearrange("p (i j n) -> p i j n", i=2, j=4)
            square = slots[:, 0:B * D].rearrange("p (b d) -> p b d", b=B)
            n = norm("l1", rms=(square, F("lnw")))
            logits = bank(7)[:, 0:B * E].rearrange("p (b e) -> p b e", b=B)
            sync, positions, tensor_, scalar_, vector_ = slotted(
                "l1", CAP1, B // 2, True, onehot, slots, hidden, silu, ring, turned_w, turned_y, taken, slotpos, weights,
                F("b1b"), F("b1a"), F("b2"), F("lnw"))

            def tensor(pe):
                n[2](pe)
                pe.wait_ge(sem("load_l1f"), 16)
                for b in range(B):
                    pe.wait_ge(sem("norm_xnT"), past("l1", "norm_xnT") + b // QUAD + 1)
                    last = TE.matmul(logits[:, b, :], xnT[:, b, :], F("Wg"), start=True, stop=True)
                last.then_inc(sem("l1_logits"), 1)
                positions(pe)
                tensor_(pe)

            def scalar(a):
                a.wait_ge(sem("load_l1f"), 16)
                n[3](a)
                a.wait_ge(sem("l1_second"), 1)
                S.activation(second, second, ACT.Exp).then_inc(sem("l1_exp"), 1)
                scalar_(a)

            def vector(v):
                v.sem_inc(sem("l1_start"), 1)
                n[0](v)
                by8 = [P, B, E]
                prio = spread(C("prio"), 1, by8)
                v.wait_ge(sem("l1_logits"), 1)
                link(v, V.tensor_tensor(score, logits, spread(F("bg"), 1, by8), ALU.add))
                first_largest(v, chosen[:, :, 0, :], score, prio, best, by8)
                link(v, V.scalar_tensor_tensor(left, chosen[:, :, 0, :], -FAR, score, ALU.mult, ALU.add))
                first_largest(v, chosen[:, :, 1, :], left, prio, best, by8)
                V.tensor_tensor(taken.rearrange("p (b e) -> p b e", b=B), chosen[:, :, 0, :], chosen[:, :, 1, :],
                                ALU.add).then_inc(sem("slotted_taken"), 1)
                link(v, V.tensor_tensor(tmp, chosen, spread(score, 2, [P, B, 2, E]), ALU.mult))
                link(v, V.tensor_reduce(weight, tmp, AX.X, ALU.add))
                V.tensor_tensor(second, weight[:, :, 1], weight[:, :, 0], ALU.subtract).then_inc(sem("l1_second"), 1)
                v.wait_ge(sem("l1_exp"), 1)
                link(v, V.tensor_scalar(best, second, 1.0, None, ALU.add))
                link(v, V.reciprocal(weight[:, :, 0], best))
                link(v, V.tensor_tensor(weight[:, :, 1], second, weight[:, :, 0], ALU.mult))
                link(v, V.tensor_tensor(tmp, chosen, spread(weight, 3, [P, B, 2, E]), ALU.mult))
                link(v, V.tensor_tensor(weights.rearrange("p (b e) -> p b e", b=B), tmp[:, :, 0, :], tmp[:, :, 1, :], ALU.add))
                vector_(v)

            def start_sync(sp):
                sp.wait_ge(sem("l1_start"), 1)
                sync(sp)
            return vector, n[1], tensor, scalar, start_sync

        def l2_experts():
            ta, tb = carve(arena_a), carve(arena_b)
            F = lambda name: field["l2", name]
            C = lambda name: field["consts", name]
            H = HID2
            NM = M2 // P
            gather = ta(B * M2, "p (b m) -> p b m", b=B)
            scatter = ta(NM * B * T, "p (i b l) -> p i b l", i=NM, b=B)
            both = tb(B * 2 * H, "p (b i h) -> p b i h", b=B, i=2)
            zs = tb(B * H, "p (b h) -> p b h", b=B)
            zsT = tb(B // 2 * T, "p (u l) -> p u l", u=B // 2)
            shared = tb(B * D, "p (b d) -> p b d", b=B)
            sel = tb(2 * NM * E * H, "p (w i e h) -> p w i e h", w=2, i=NM, e=E)
            zm = tb(NM * E * H, "p (i e h) -> p i e h", i=NM, e=E)
            zmT = tb(NM * 4 * P, "p (i j m) -> p i j m", i=NM, j=4)
            rowsT = tb(M2)
            value = tb(NM * (D + 1), "p (i d) -> p i d", i=NM)
            keepmore = tb(B)
            idx = tb(2 * (M2 + NM), "p (w n) -> p w n", w=2)
            idxi = tb(2 * (M2 + NM), "p (w n) -> p w n", w=2).bitcast(I32)
            tmpi = tb(2 * (M2 + NM), "p (w n) -> p w n", w=2)
            at = tb(M2 + NM)
            same = tb(M2)
            first = tb(NM)
            st = tb(2 * B * 6, "p (w b c) -> p w b c", w=2, b=B)
            mv = tb(2 * B * 2, "p (w b c) -> p w b c", w=2, b=B)
            ve = tb(2 * B, "p (w b) -> p w b", w=2)
            rs = tb(2 * B, "p (w b) -> p w b", w=2)
            gate = tb(NM * (E + 1), "p (i e) -> p i e", i=NM)
            score = tb(NM * E, "p (i e) -> p i e", i=NM)
            onehot = tb(NM * E, "p (i e) -> p i e", i=NM)
            picked = tb(NM * E, "p (i e) -> p i e", i=NM)
            best = tb(NM)
            two = tb(NM * 2, "p (i w) -> p i w", i=NM)
            onehotT = tb(NM * P, "p (i m) -> p i m", i=NM)
            update = both.rearrange("p b i h -> p b (i h)")
            n = norm("l2f")
            s_ = lambda what: sem("l2f_" + what)

            def tensor(pe):
                n[2](pe)
                pe.wait_ge(sem("load_l2"), 16)
                for g in range(GROUPS):
                    pe.wait_ge(sem("norm_xnT"), past("l2f", "norm_xnT") + g + 1)
                    for i in range(QUAD):
                        last = TE.matmul(bank4(4 + g)[:, i, :], xnT[:, QUAD * g + i, :], F("sw12T"), start=True, stop=True)
                    last.then_inc(s_("both_mm"), 1)
                pe.wait_ge(s_("gather"), 1)
                for b in range(B):
                    last = TE.matmul(bank(0)[:, 0:M2], xn[:, b, :], gather[:, b, :], start=(b == 0), stop=(b == B - 1))
                last.then_inc(s_("rows_mm"), 1)
                pe.wait_ge(s_("rowsT"), 1)
                for i in range(NM):
                    last = TE.matmul(bank(1)[:, (E + 1) * i:(E + 1) * (i + 1)], rowsT[:, P * i:P * i + P], F("gateT"),
                                     start=True, stop=True)
                last.then_inc(s_("gate_mm"), 1)
                pe.wait_ge(s_("both"), GROUPS)
                for w, name in enumerate(("ew1T", "ew2T")):
                    for i in range(NM):
                        last = TE.matmul(bank(4 + 2 * w + i), rowsT[:, P * i:P * i + P], F(name), start=True, stop=True)
                    last.then_inc(s_("sel_mm"), 1)
                pe.wait_ge(s_("zs"), 1)
                for u in range(B // 2):
                    last = TE.transpose(bank4(2 + u // 4)[:, u % 4, :], zs[:, 2 * u:2 * u + 2, :], ident)
                last.then_inc(s_("zs_turned"), 1)
                pe.wait_ge(s_("zsT"), 1)
                pe.wait_ge(s_("gate"), 1)
                pe.wait_ge(s_("sel"), 2)
                for u in range(B // 2):
                    for i in range(2):
                        last = TE.matmul(bank4(4 * i + u // 4)[:, u % 4, :], zsT[H * i:H * i + H, u, :],
                                         F("sw3T")[H * i:H * i + H, :], start=True, stop=True)
                last.then_inc(s_("shared_mm"), 1)
                pe.wait_ge(s_("zm"), 1)
                for i in range(NM):
                    for j in range(4):
                        last = TE.transpose(bank4(2 + i)[:, j, :], zm[:, i, 2 * j:2 * j + 2, :], ident)
                    last.then_inc(s_("zm_turned"), 1)
                for i in range(NM):
                    last = TE.transpose(bank4(6)[0:E, i, :], onehot[:, i, :], ident)
                last.then_inc(s_("onehot_turned"), 1)
                pe.wait_ge(s_("zmT"), NM)
                pe.wait_ge(s_("onehotT"), 1)
                for i in range(NM):
                    for j in range(4):
                        TE.matmul(bank4(7)[:, i, :], zmT[:, i, j, :], F("ew3")[:, D * j:D * j + D], start=(j == 0), stop=False)
                    last = TE.matmul(bank4(7)[:, i, :], onehotT[0:E, i, :], F("eb3")[0:E, :], start=False, stop=True)
                last.then_inc(s_("expert_mm"), 1)
                pe.wait_ge(s_("value"), 1)
                pe.wait_ge(s_("shared"), 2)
                for b in range(B):
                    for i in range(NM):
                        last = TE.matmul(bank(b // 3)[:, (D + 1) * (b % 3):(D + 1) * (b % 3 + 1)], scatter[:, i, b, :],
                                         value[:, i, :], start=(i == 0), stop=(i == NM - 1))
                last.then_inc(s_("back"), 1)

            def gpsimd(g):
                n[1](g)
                for w in range(2):
                    g.wait_ge(s_(f"ve{w}"), 1)
                    nc.gpsimd.tensor_tensor(rs[:, w, :], ve[:, w, :], minushalf[:, :], ALU.pow).then_inc(s_(f"rs{w}"), 1)

            def scalar(a):
                n[3](a)
                for g in range(GROUPS):
                    a.wait_ge(s_("both"), g + 1)
                    q = slice(QUAD * g, QUAD * g + QUAD)
                    S.activation(both[:, q, 0, :], both[:, q, 0, :], ACT.Silu).then_inc(s_("silu"), 1)
                a.wait_ge(s_("sel"), 1)
                S.activation(sel[:, 0, :, :, :], sel[:, 0, :, :, :], ACT.Silu).then_inc(s_("sel_silu"), 1)
                a.wait_ge(s_("gate"), 1)
                S.activation(gate, gate, ACT.Sigmoid).then_inc(s_("sigmoid"), 1)
                for i in range(NM):
                    a.wait_ge(s_("zm_turned"), i + 1)
                    S.copy(zmT[:, i, :, :], bank4(2 + i)).then_inc(s_("zmT"), 1)
                a.wait_ge(s_("two"), 1)
                S.activation(two, two, ACT.Exp).then_inc(s_("exp"), 1)

            def normed(v, w, src, dst):
                for b in range(B):
                    last = V.bn_stats(st[:, w, b, :], src[:, b, :])
                link(v, last)
                for b in range(B):
                    last = V.bn_aggr(mv[:, w, b, :], st[:, w, b, :])
                link(v, last)
                V.tensor_scalar_add(ve[:, w, :], mv[:, w, :, 1], LN_EPS).then_inc(s_(f"ve{w}"), 1)
                v.wait_ge(s_(f"rs{w}"), 1)
                for b in range(B):
                    last = V.tensor_scalar(dst[:, b, :], src[:, b, :], mv[:, w, b, 0:1], rs[:, w, b:b + 1],
                                           ALU.subtract, ALU.mult)
                return last

            def vector(v):
                v.wait_ge(sem("load_index"), 16)
                link(v, V.tensor_copy(idx, index_sb[:, :, :]))
                for w, size in enumerate((B, T)):
                    link(v, V.tensor_scalar(tmpi[:, w, :], idx[:, w, :], 0.0, float(size), ALU.is_lt, ALU.mult))
                link(v, V.tensor_tensor(idx, idx, tmpi, ALU.add))
                for w, size in enumerate((B, T)):
                    link(v, V.tensor_scalar(tmpi[:, w, :], idx[:, w, :], 0.0, float(size - 1), ALU.max, ALU.min))
                link(v, V.tensor_tensor(tmpi, tmpi, idx, ALU.is_equal))
                link(v, V.tensor_tensor(tmpi[:, 0, :], tmpi[:, 0, :], tmpi[:, 1, :], ALU.mult))
                link(v, V.scalar_tensor_tensor(at, idx[:, 0, :], float(T), idx[:, 1, :], ALU.mult, ALU.add))
                link(v, V.scalar_tensor_tensor(at, at, 1.0, tmpi[:, 0, :], ALU.add, ALU.mult))
                link(v, V.tensor_scalar(at, at, -1.0, None, ALU.add))
                V.tensor_tensor(gather, spread(C("token"), 2, [P, B, M2]), spread(at[:, 0:M2], 1, [P, B, M2]),
                                ALU.is_equal).then_inc(s_("gather"), 1)
                for i in range(NM):
                    mine = at[:, M2 + i:M2 + i + 1]
                    link(v, V.tensor_scalar(scatter[:, i, :, :], C("tokenrow").rearrange("p (b l) -> p b l", b=B),
                                            mine, None, ALU.is_equal))
                    link(v, V.scalar_tensor_tensor(same, at[:, 0:M2], mine, C("earlier")[:, M2 * i:M2 * i + M2],
                                                   ALU.is_equal, ALU.mult))
                    link(v, V.tensor_reduce(first[:, i:i + 1], same, AX.X, ALU.max))
                link(v, V.tensor_scalar(first, first, -1.0, 1.0, ALU.mult, ALU.add))
                n[0](v)
                v.wait_ge(sem("load_l2"), 16)
                for g in range(GROUPS):
                    q = slice(QUAD * g, QUAD * g + QUAD)
                    v.wait_ge(s_("both_mm"), g + 1)
                    V.tensor_tensor(both[:, q, :, :].rearrange("p b i h -> p b (i h)"), bank4(4 + g),
                                    spread(F("sb12"), 1, [P, QUAD, 2 * H]), ALU.add).then_inc(s_("both"), 1)
                v.wait_ge(s_("rows_mm"), 1)
                V.tensor_copy(rowsT, bank(0)[:, 0:M2]).then_inc(s_("rowsT"), 1)
                v.wait_ge(s_("silu"), GROUPS)
                link(v, V.tensor_tensor(both[:, :, 0, :], both[:, :, 0, :], both[:, :, 1, :], ALU.mult))
                normed(v, 0, both[:, :, 0, :], zs).then_inc(s_("zs"), 1)
                v.wait_ge(s_("gate_mm"), 1)
                V.tensor_tensor(gate, bank(1)[:, 0:NM * (E + 1)].rearrange("p (i e) -> p i e", i=NM),
                                spread(F("gateb"), 1, [P, NM, E + 1]), ALU.add).then_inc(s_("gate"), 1)
                for w, name in enumerate(("eb1", "eb2")):
                    v.wait_ge(s_("sel_mm"), w + 1)
                    last = V.tensor_tensor(sel[:, w, :, :, :].rearrange("p i e h -> p i (e h)"), ps[:, 4 + 2 * w:6 + 2 * w, :],
                                           spread(F(name), 1, [P, NM, E * H]), ALU.add)
                    last.then_inc(s_("sel"), 1)
                v.wait_ge(s_("zs_turned"), 1)
                V.tensor_scalar(zsT, ps[:, 2:4, :].rearrange("p j (u l) -> p (j u) l", u=4), F("slng"), F("slnb"),
                                ALU.mult, ALU.add).then_inc(s_("zsT"), 1)
                v.wait_ge(s_("sel_silu"), 1)
                v.wait_ge(s_("sel"), 2)
                link(v, V.tensor_tensor(sel[:, 0, :, :, :], sel[:, 0, :, :, :], sel[:, 1, :, :, :], ALU.mult))
                rows16 = lambda ap: ap.rearrange("p i e h -> p (i e) h")
                link(v, normed(v, 1, rows16(sel[:, 0, :, :, :]), rows16(zm)))
                by = [P, NM, E]
                v.wait_ge(s_("sigmoid"), 1)
                link(v, V.tensor_tensor(score, gate[:, :, 1:E + 1], spread(F("expbias"), 1, by), ALU.add))
                first_largest(v, onehot, score, spread(C("prio"), 1, by), best, by)
                v.sem_inc(s_("onehot"), 1)
                link(v, V.tensor_tensor(picked, onehot, gate[:, :, 1:E + 1], ALU.mult))
                link(v, V.tensor_reduce(two[:, :, 1], picked, AX.X, ALU.add))
                link(v, V.tensor_copy(two[:, :, 0], gate[:, :, 0]))
                link(v, V.tensor_reduce(best, two, AX.X, ALU.max))
                V.tensor_tensor(two, two, spread(best, 2, [P, NM, 2]), ALU.subtract).then_inc(s_("two"), 1)
                full = [P, NM * E, H]
                link(v, V.tensor_tensor(rows16(zm), rows16(zm), spread(F("sellng"), 1, full), ALU.mult))
                link(v, V.tensor_tensor(rows16(zm), rows16(zm), spread(F("sellnb"), 1, full), ALU.add))
                V.tensor_tensor(rows16(zm), rows16(zm), spread(onehot.rearrange("p i e -> p (i e)"), 2, full),
                                ALU.mult).then_inc(s_("zm"), 1)
                v.wait_ge(s_("shared_mm"), 1)
                sh = shared.rearrange("p (u i) d -> p u i d", i=2)
                for i in range(2):
                    V.tensor_tensor(sh[:, :, i, :], ps[:, 4 * i:4 * i + 2, :].rearrange("p j (u d) -> p (j u) d", u=4),
                                    spread(F("sb3"), 1, [P, B // 2, D]), ALU.add).then_inc(s_("shared"), 1)
                v.wait_ge(s_("onehot_turned"), 1)
                V.tensor_copy(onehotT[0:E, :, :], bank4(6)[0:E, 0:NM, :]).then_inc(s_("onehotT"), 1)
                v.wait_ge(s_("exp"), 1)
                link(v, V.tensor_reduce(best, two, AX.X, ALU.add))
                link(v, V.reciprocal(best, best))
                link(v, V.tensor_tensor(two, two, spread(best, 2, [P, NM, 2]), ALU.mult))
                link(v, V.tensor_scalar(two[:, :, 0], two[:, :, 0], -1.0, None, ALU.add))
                link(v, V.tensor_tensor(two, two, spread(first, 2, [P, NM, 2]), ALU.mult))
                v.wait_ge(s_("expert_mm"), 1)
                V.tensor_copy(value[:, :, D:D + 1], two[:, :, 0:1])
                V.tensor_tensor(value[:, :, 0:D], bank4(7)[:, 0:NM, :], spread(two[:, :, 1], 2, [P, NM, D]),
                                ALU.mult).then_inc(s_("value"), 1)
                v.wait_ge(s_("back"), 1)
                back = [bank(b // 3)[:, (D + 1) * (b % 3):(D + 1) * (b % 3 + 1)] for b in range(B)]
                link(v, V.tensor_scalar(keepmore[:, 0:15].rearrange("p (j i) -> p j i", i=3), keepview(), 1.0, None, ALU.add))
                link(v, V.tensor_scalar(keepmore[:, 15:16], back[15][:, D:D + 1], 1.0, None, ALU.add))
                for b in range(B):
                    last = V.scalar_tensor_tensor(update[:, b, :], shared[:, b, :], keepmore[:, b:b + 1], back[b][:, 0:D],
                                                  ALU.mult, ALU.add)
                link(v, last)
                link(v, V.tensor_tensor(x[:, :, :], x[:, :, :], update, ALU.add))

            def keepview():
                return ps[:, 0:5, 0:3 * (D + 1)].rearrange("p j (i d) -> p j i d", i=3)[:, :, :, D]
            return vector, gpsimd, tensor, scalar

        def l3_attention():
            ta, tb = carve(arena_a), carve(arena_b)
            F = lambda name: field["l3", name]
            C9 = HEAD + 1
            PAIR = 2
            keys = ta(2 * PAIR * HEADS * T, "p (i b u g s) -> p i b u g s", i=2, b=PAIR, u=4, g=4)
            vals = tb(B * HEADS * C9, "p (b h c) -> p b h c", b=B, h=HEADS)
            probs = tb(3 * 4 * T, "p (i g s) -> p i g s", i=3, g=4)
            probsT = tb(3 * 4 * T, "p (i g l) -> p i g l", i=3, g=4)
            weighed = tb(2 * 4 * T, "p (i u l) -> p i u l", i=2, u=4)
            neg = tb(3 * 4, "p (i g) -> p i g", i=3)
            att = tb(B * D, "p (b d) -> p b d", b=B)
            attT = tb(B * D, "p (b l) -> p b l", b=B)
            inv = tb(2 * HEADS, "p (i h) -> p i h", i=2)
            scale = 1.0 / math.sqrt(HEAD)
            n = norm("l3x")
            K = 4 * B
            s_ = lambda what: sem("l3x_" + what)

            def tensor(pe):
                n[2](pe)
                pe.wait_ge(sem("load_l3"), 16)
                pe.wait_ge(s_("values"), spent("l3x_values") + 16)

                def score(k):
                    b, u = k // 4, k % 4
                    if b % PAIR == 0 and u == 0:
                        pe.wait_ge(s_(f"keys{b // PAIR % 2}"), spent(f"l3x_keys{b // PAIR % 2}") + 16 * HEADS * (b // (2 * PAIR) + 1))
                    if k < 4:
                        pe.wait_ge(sem("norm_xnT"), past("l3x", "norm_xnT") + GROUPS)
                    if k >= 3:
                        pe.wait_ge(s_("probs"), spent("l3x_probs") + k - 2)
                    TE.matmul(bank(k % 3), xnT[:, b, :], keys[:, b // PAIR % 2, b % PAIR, u, :, :], start=True,
                              stop=True).then_inc(s_("score"), 1)

                def turn(k):
                    pe.wait_ge(s_("probs"), spent("l3x_probs") + k + 1)
                    if k >= 3:
                        pe.wait_ge(s_("probsT"), spent("l3x_probsT") + k - 2)
                    for g in range(4):
                        last = TE.transpose(bank4(3 + k % 3)[:, g, :], probs[:, k % 3, g, :], ident)
                    last.then_inc(s_("turned"), 1)

                def weigh(k):
                    b, u = k // 4, k % 4
                    pe.wait_ge(s_("probsT"), spent("l3x_probsT") + k + 1)
                    if u == 0 and b >= 2:
                        pe.wait_ge(s_("att"), spent("l3x_att") + b - 1)
                    for g in range(4):
                        last = TE.matmul(bank4(6 + b % 2)[32 * g:32 * g + C9, u, :], vals[:, b, 4 * g + u, :],
                                         probsT[:, k % 3, g, :], start=True, stop=True)
                    last.then_inc(s_("weigh"), 1)

                def turn_back(b):
                    pe.wait_ge(s_("weighed"), spent("l3x_weighed") + b + 1)
                    for u in range(4):
                        last = TE.transpose(bank4(6 + b % 2)[:, u, :], weighed[:, b % 2, u, :], ident)
                    last.then_inc(s_("back"), 1)

                pe.wait_ge(s_("cleared"), spent("l3x_cleared") + 1)
                score(0)
                score(1)
                for k in range(K):
                    if k + 2 < K:
                        score(k + 2)
                    turn(k)
                    if k:
                        weigh(k - 1)
                    if k % 4 == 2 and k >= 4:
                        turn_back(k // 4 - 1)
                weigh(K - 1)
                turn_back(B - 1)
                for g in range(GROUPS):
                    pe.wait_ge(s_("att"), spent("l3x_att") + QUAD * (g + 1))
                    for i in range(QUAD):
                        last = TE.transpose(bank4(g)[:, i, :], att[:, QUAD * g + i, :], ident)
                    last.then_inc(s_("att_turned"), 1)
                pe.wait_ge(s_("att"), spent("l3x_att") + B)
                for g in range(GROUPS):
                    pe.wait_ge(s_("attT"), spent("l3x_attT") + g + 1)
                    for i in range(QUAD):
                        last = TE.matmul(bank4(4 + g)[:, i, :], attT[:, QUAD * g + i, :], F("wprojT"), start=True, stop=True)
                    last.then_inc(s_("out"), 1)

            def scalar(a):
                n[3](a)

                def copy_out(b):
                    a.wait_ge(s_("weigh"), spent("l3x_weigh") + 4 * (b + 1))
                    if b >= 2:
                        a.wait_ge(s_("back"), spent("l3x_back") + b - 1)
                    S.copy(weighed[:, b % 2, :, :], bank4(6 + b % 2)).then_inc(s_("weighed"), 1)
                for k in range(K):
                    a.wait_ge(s_("largest"), spent("l3x_largest") + k + 1)
                    if k >= 3:
                        a.wait_ge(s_("turned"), spent("l3x_turned") + k - 2)
                    for g in range(4):
                        last = S.activation(probs[:, k % 3, g, :], bank4(k % 3)[:, g, :], ACT.Exp,
                                            bias=neg[:, k % 3, g:g + 1], scale=scale)
                    last.then_inc(s_("probs"), 1)
                    if k % 4 == 2 and k >= 4:
                        copy_out(k // 4 - 1)
                copy_out(B - 1)
                for g in range(GROUPS):
                    a.wait_ge(s_("att_turned"), spent("l3x_att_turned") + g + 1)
                    S.copy(attT[:, QUAD * g:QUAD * g + QUAD, :], bank4(g)).then_inc(s_("attT"), 1)

            def vector(v):
                V.memset(arena_a[:, :], 0.0).then_inc(s_("start"), 1)
                V.memset(ps[:, 6:8, :], 0.0).then_inc(s_("cleared"), 1)
                n[0](v)
                v.wait_ge(sem("load_l3"), 16)

                def largest(k):
                    v.wait_ge(s_("score"), spent("l3x_score") + k + 1)
                    if k >= 3:
                        v.wait_ge(s_("probs"), spent("l3x_probs") + k - 2)
                    link(v, V.tensor_reduce(neg[:, k % 3, :], bank4(k % 3), AX.X, ALU.max))
                    V.tensor_scalar(neg[:, k % 3, :], neg[:, k % 3, :], -scale, None, ALU.mult).then_inc(s_("largest"), 1)

                def copy_turned(k):
                    v.wait_ge(s_("turned"), spent("l3x_turned") + k + 1)
                    if k >= 3:
                        v.wait_ge(s_("weigh"), spent("l3x_weigh") + k - 2)
                    V.tensor_copy(probsT[:, k % 3, :, :], bank4(3 + k % 3)).then_inc(s_("probsT"), 1)

                def divide(b):
                    v.wait_ge(s_("back"), spent("l3x_back") + b + 1)
                    back = bank(6 + b % 2).rearrange("p (u g c) -> p g u c", u=4, g=4)
                    link(v, V.reciprocal(inv[:, b % 2, :].rearrange("p (g u) -> p g u", g=4), back[:, :, :, HEAD]))
                    V.tensor_tensor(att[:, b, :].rearrange("p (g u c) -> p g u c", g=4, u=4), back[:, :, :, 0:HEAD],
                                    spread(inv[:, b % 2, :].rearrange("p (g u) -> p g u", g=4), 3, [P, 4, 4, HEAD]),
                                    ALU.mult).then_inc(s_("att"), 1)
                largest(0)
                largest(1)
                for k in range(K):
                    if k + 2 < K:
                        largest(k + 2)
                    copy_turned(k)
                    if k % 4 == 3 and k >= 4:
                        divide(k // 4 - 1)
                divide(B - 1)
                for g in range(GROUPS):
                    q = slice(QUAD * g, QUAD * g + QUAD)
                    last = V.tensor_tensor(x[:, q, :], x[:, q, :], spread(F("bproj"), 1, [P, QUAD, D]), ALU.add)
                link(v, last)
                for g in range(GROUPS):
                    q = slice(QUAD * g, QUAD * g + QUAD)
                    v.wait_ge(s_("out"), spent("l3x_out") + g + 1)
                    last = V.tensor_tensor(x[:, q, :], bank4(4 + g), x[:, q, :], ALU.add)
                link(v, last)

            def sync(sp):
                sp.wait_ge(s_("start"), spent("l3x_start") + 1)
                sp.dma_start(vals, dram["l3_values"].rearrange("p (b h c) -> p b h c", b=B, h=HEADS)).then_inc(s_("values"), 16)
                for r in range(B // PAIR):
                    if r >= 2:
                        sp.wait_ge(s_("score"), spent("l3x_score") + 4 * PAIR * (r - 1))
                    for h in range(HEADS):
                        rows_ = slice(HEAD * h, HEAD * h + HEAD)
                        sp.dma_start(keys[rows_, r % 2, :, h % 4, h // 4, :],
                                     dram["ctxT"][rows_, PAIR * r:PAIR * r + PAIR, :]).then_inc(s_(f"keys{r % 2}"), 16)
            return vector, n[1], tensor, scalar, sync

        def l3_experts():
            ta, tb = carve(arena_a), carve(arena_b)
            F = lambda name: field["l3", name]
            C = lambda name: field["consts", name]
            hidden = ta(2 * CH3 * B * CAP)
            ring = ta(2 * 2 * HID3, "p (i n) -> p i n", i=2)
            onehot = ta(B * E * CAP)
            slots = tb(B * E * CAP)
            route1 = tb(2 * CH3 * 512, "p (i f n) -> p i f n", i=2, f=CH3)
            route2 = tb(2 * CH3 * 512, "p (i f n) -> p i f n", i=2, f=CH3)
            score = tb(B * E, "p (b e) -> p b e", b=B)
            left = tb(B * E, "p (b e) -> p b e", b=B)
            chosen = tb(B * 2 * E, "p (b k e) -> p b k e", b=B, k=2)
            best = tb(B)
            taken = tb(B * E)
            slotpos = tb(B * E)
            weights = tb(B * E)
            turned_w = tb(1024, "p (i j n) -> p i j n", i=2, j=4)
            turned_y = tb(1024, "p (i j n) -> p i j n", i=2, j=4)
            n = norm("l3")
            s_ = lambda what: sem("l3f_" + what)
            logits = bank(7)[:, 0:B * E].rearrange("p (b e) -> p b e", b=B)
            sync, positions, tensor_, scalar_, vector_ = slotted(
                "l3", CAP, B, False, onehot, slots, hidden, None, ring, turned_w, turned_y, taken, slotpos, weights,
                F("eb1"), None, F("eb2"), None)

            def tensor(pe):
                n[2](pe)

                def first(g):
                    pe.wait_ge(sem("norm_xnT"), past("l3", "norm_xnT") + g + 1)
                    for f in range(CH3):
                        k = CH3 * g + f
                        if k >= 2:
                            pe.wait_ge(s_("route1"), spent("l3f_route1") + k - 1)
                        TE.matmul(bank(4 + k % 2), F("rW1")[:, P * f:P * f + P], xnT[:, QUAD * g:QUAD * g + QUAD, :],
                                  start=True, stop=True).then_inc(s_("first"), 1)

                def third(g):
                    pe.wait_ge(s_("route2"), spent("l3f_route2") + CH3 * (g + 1))
                    for i in range(QUAD):
                        for f in range(CH3):
                            last = TE.matmul(logits[:, QUAD * g + i, :], route2[:, g % 2, f, T * i:T * i + T],
                                             F("rW3")[:, E * f:E * f + E], start=(f == 0), stop=(f == CH3 - 1))
                    last.then_inc(s_("third"), 1)
                first(0)
                for g in range(GROUPS):
                    if g + 1 < GROUPS:
                        first(g + 1)
                    pe.wait_ge(s_("route1"), spent("l3f_route1") + CH3 * (g + 1))
                    for o in range(CH3):
                        k = CH3 * g + o
                        if k >= 2:
                            pe.wait_ge(s_("route2"), spent("l3f_route2") + k - 1)
                        else:
                            pe.wait_ge(sem("norm_xnT"), past("l3", "norm_xnT") + k + 1)
                        for f in range(CH3):
                            last = TE.matmul(bank(k % 2), F("rW2")[:, HID3 * f + P * o:HID3 * f + P * o + P],
                                             route1[:, g % 2, f, :], start=(f == 0), stop=(f == CH3 - 1))
                        last.then_inc(s_("second"), 1)
                    if g:
                        third(g - 1)
                third(GROUPS - 1)
                positions(pe)
                tensor_(pe)

            def scalar(a):
                n[3](a)

                def relu2(g):
                    for o in range(CH3):
                        a.wait_ge(s_("second"), spent("l3f_second") + CH3 * g + o + 1)
                        if g >= 2 and o == 0:
                            a.wait_ge(s_("third"), spent("l3f_third") + g - 1)
                        S.activation(route2[:, g % 2, o, :], bank((CH3 * g + o) % 2), ACT.Relu,
                                     bias=F("rb2")[:, o:o + 1]).then_inc(s_("route2"), 1)
                for g in range(GROUPS):
                    relu2(g)
                a.wait_ge(s_("centred"), spent("l3f_centred") + 1)
                S.activation(score, score, ACT.Exp).then_inc(s_("exp"), 1)
                scalar_(a)

            def vector(v):
                v.sem_inc(s_("start"), 1)
                n[0](v)
                for g in range(GROUPS):
                    for f in range(CH3):
                        k = CH3 * g + f
                        v.wait_ge(s_("first"), spent("l3f_first") + k + 1)
                        if g >= 2 and f == 0:
                            v.wait_ge(s_("second"), spent("l3f_second") + CH3 * (g - 1))
                        V.tensor_scalar(route1[:, g % 2, f, :], bank(4 + k % 2), F("rb1")[:, f:f + 1], 0.0, ALU.add,
                                        ALU.max).then_inc(s_("route1"), 1)
                v.wait_ge(s_("third"), spent("l3f_third") + GROUPS)
                by8 = [P, B, E]
                prio = spread(C("prio"), 1, by8)
                link(v, V.tensor_tensor(score, logits, spread(F("rb3"), 1, by8), ALU.add))
                link(v, V.tensor_reduce(best, score, AX.X, ALU.max))
                V.tensor_tensor(score, score, spread(best, 2, by8), ALU.subtract).then_inc(s_("centred"), 1)
                v.wait_ge(s_("exp"), spent("l3f_exp") + 1)
                link(v, V.tensor_reduce(best, score, AX.X, ALU.add))
                link(v, V.reciprocal(best, best))
                link(v, V.tensor_tensor(score, score, spread(best, 2, by8), ALU.mult))
                first_largest(v, chosen[:, :, 0, :], score, prio, best, by8)
                link(v, V.scalar_tensor_tensor(left, chosen[:, :, 0, :], -FAR, score, ALU.mult, ALU.add))
                first_largest(v, chosen[:, :, 1, :], left, prio, best, by8)
                by = lambda ap: ap.rearrange("p (b e) -> p b e", b=B)
                link(v, V.tensor_tensor(by(taken), chosen[:, :, 0, :], chosen[:, :, 1, :], ALU.add))
                v.sem_inc(sem("slotted_taken"), 1)
                link(v, V.tensor_tensor(by(weights), by(taken), score, ALU.mult))
                vector_(v)

            def start_sync(sp):
                sp.wait_ge(s_("start"), spent("l3f_start") + 1)
                sync(sp)
            return vector, n[1], tensor, scalar, start_sync

        phases = [l0_attention, l0_experts,
                  lambda: attention("l1x", "l1x", "Wq", "Wk", "Wv", "bq", "bk", "bv"), l1_experts,
                  lambda: attention("l2x", "l2", "WqT", "WqT", "WqT", causal=True),
                  l2_experts, l3_attention, l3_experts]
        phases = [p() for p in phases[:upto] if p]

        block = f.enter_context(nc.Block())

        @block.sync
        def _(sp):
            sp.dma_start(packed["fourier"][:, :], dram["fourier"]).then_inc(sem("load_fourier"), 16)
            sp.dma_start(ctx_tok[:, :, :], dram["ctx"].rearrange("b l d -> l b d")).then_inc(sem("load_ctx"), 16)
            sp.dma_start(ctxT[:, :, :], dram["ctxT"]).then_inc(sem("load_ctx"), 16)
            for pack in ("l0f", "l1x", "l1f", "l2", "l3"):
                sp.dma_start(packed[pack][:, :], dram[pack]).then_inc(sem("load_" + pack), 16)
            for p in phases:
                if len(p) > 4:
                    p[4](sp)
            sp.wait_ge(sem("done"), 1)
            sp.dma_start(out.rearrange("b l d -> l b d"), x[:, :, :]).then_inc(sem("stored"), 16)
            sp.wait_ge(sem("stored"), 16)

        @block.gpsimd
        def _(g):
            nc.gpsimd.memset(minushalf[:, :], -0.5).then_inc(sem("minushalf"), 1)
            g.wait_ge(sem("minushalf"), 1)
            for p in phases:
                p[1](g)

        @block.scalar
        def _(a):
            a.dma_start(x[:, :, :], dram["x"].rearrange("b l d -> l b d")).then_inc(sem("load_x"), 16)
            a.dma_start(index_sb[:, :, :], dram["index"].rearrange("p (w n) -> p w n", w=2)).then_inc(sem("load_index"), 16)
            a.dma_start(packed["consts"][:, :], dram["consts"]).then_inc(sem("load_consts"), 16)
            for p in phases:
                p[3](a)

        @block.vector
        def _(v):
            v.wait_ge(sem("load_consts"), 16)
            for p in phases:
                p[0](v)
            link(v, V.memset(wait_word[:, :], 0.0)) if False else None
            v.sem_inc(sem("done"), 1)

        @block.tensor
        def _(pe):
            for p in phases:
                p[2](pe)


def fourier_constants():
    n = T
    t = np.arange(n)
    half = n // 2
    fwd1, fwd2, inv1, inv2 = (np.zeros((n, n)) for _ in range(4))
    for j in range(half + 1):
        c = np.cos(2 * np.pi * j * t / n)
        s = np.sin(2 * np.pi * j * t / n)
        w = (1.0 if j in (0, half) else 2.0) / n
        fwd1[j], inv1[j] = c, w * c
        if 0 < j < half:
            fwd1[half + j], inv1[half + j] = -s, w * c
            fwd2[j], inv2[j] = -s, w * s
            fwd2[half + j], inv2[half + j] = c, -w * s
    dft = np.concatenate([fwd1.T, fwd2.T], axis=1)
    idft = np.concatenate([inv1, inv2], axis=1)
    return dft.astype(np.float32), idft.astype(np.float32)


def constants():
    p = np.arange(P)
    e = np.arange(E)
    dft, idft = fourier_constants()
    m = np.arange(M2)

    def rows(v):
        return np.tile(np.asarray(v, np.float32).reshape(1, -1), (P, 1))
    return {
        "dft": dft, "idft": idft, "ident": np.eye(P, dtype=np.float32),
        "blockmask": (p[:, None] // HEAD == np.arange(HEADS)[None]).astype(np.float32),
        "dmod": (p[:, None] % HEAD + T).astype(np.float32),
        "iota8": rows(np.arange(HEAD)), "prio": rows(E - e), "prio4": rows(4 - np.arange(4)),
        "lower": rows((e[None, :] <= e[:, None])),
        "rownum": (2 * (np.arange(B)[None, :, None] * T + p[:, None, None]) + np.arange(2)[None, None]).reshape(P, 2 * B).astype(np.float32),
        "ones": np.ones((P, P), np.float32),
        "before": (p[:, None] < p[None, :]).astype(np.float32),
        "causal": np.where(p[None, :] <= p[:, None], 0.0, -FAR).astype(np.float32),
        "slot": rows(np.arange(CAP1)),
        "token": (np.arange(B)[None] * T + p[:, None]).astype(np.float32),
        "tokenrow": rows(np.arange(B * T)),
        "earlier": np.concatenate([(m[None] < p[:, None]), (m[None] < P + p[:, None])], axis=1).astype(np.float32),
    }


def kernel(**inputs):
    import concourse.bacc as bacc
    from concourse.bass_utils import run_bass_kernel_spmd

    i = {k: np.asarray(v) for k, v in inputs.items()}

    def rows(v):
        return np.tile(v.reshape(1, -1), (P, 1))

    def col(v):
        return v.reshape(-1, P).T

    def tall(v):
        return np.concatenate([v, np.zeros((P - v.shape[0], v.shape[1]), v.dtype)])

    def twice(v):
        return np.concatenate([v, v])

    c = constants()
    fields = {
        ("fourier", "wk"): i["L0_xattn_wk"], ("fourier", "wq"): i["L0_xattn_wq"],
        ("fourier", "wv"): i["L0_xattn_wv"], ("fourier", "wo"): i["L0_xattn_wo"],
        ("l0f", "wgateT"): i["L0_ffn_w_gate"].T,
        ("l0f", "sw1T"): i["L0_ffn_sw1"].T, ("l0f", "sw3T"): i["L0_ffn_sw3"].T, ("l0f", "sw2T"): i["L0_ffn_sw2"].T,
        ("l0f", "ebias"): rows(i["L0_ffn_expert_bias"]),
        ("l0f", "w13"): np.concatenate([i["L0_ffn_w1"], i["L0_ffn_w3"]], axis=2).transpose(1, 0, 2).reshape(P, -1),
        ("l0f", "w2"): tall(i["L0_ffn_w2"].transpose(1, 0, 2).reshape(HID0, -1)),
        ("l1x", "Wq"): i["L1_xattn_Wq"], ("l1x", "Wk"): i["L1_xattn_Wk"], ("l1x", "Wv"): i["L1_xattn_Wv"],
        ("l1x", "bq"): col(i["L1_xattn_bq"]), ("l1x", "bk"): col(i["L1_xattn_bk"]), ("l1x", "bv"): rows(i["L1_xattn_bv"]),
        ("l1f", "lnw"): col(i["L1_ffn_ln_w"]), ("l1f", "Wg"): i["L1_ffn_Wg"], ("l1f", "bg"): rows(i["L1_ffn_bg"]),
        ("l1f", "b2"): col(i["L1_ffn_b2"]), ("l1f", "b1a"): col(i["L1_ffn_b1a"]), ("l1f", "b1b"): col(i["L1_ffn_b1b"]),
        ("l2", "WqT"): i["L2_xattn_Wq"].T,
        ("l2", "sw12T"): np.concatenate([i["L2_ffn_sw1"].T, i["L2_ffn_sw2"].T], axis=1),
        ("l2", "sb12"): rows(np.concatenate([i["L2_ffn_sb1"], i["L2_ffn_sb2"]])),
        ("l2", "sw3T"): twice(i["L2_ffn_sw3"].T), ("l2", "sb3"): rows(i["L2_ffn_sb3"]),
        ("l2", "slng"): twice(i["L2_ffn_s_ln_g"].reshape(-1, 1)), ("l2", "slnb"): twice(i["L2_ffn_s_ln_b"].reshape(-1, 1)),
        ("l2", "gateT"): np.concatenate([i["L2_ffn_sg_w"], i["L2_ffn_eg_w"]]).T,
        ("l2", "gateb"): rows(np.concatenate([i["L2_ffn_sg_b"], i["L2_ffn_eg_b"]])),
        ("l2", "expbias"): rows(i["L2_ffn_exp_bias"]),
        ("l2", "ew1T"): i["L2_ffn_ew1"].transpose(2, 0, 1).reshape(P, -1),
        ("l2", "ew2T"): i["L2_ffn_ew2"].transpose(2, 0, 1).reshape(P, -1),
        ("l2", "eb1"): rows(i["L2_ffn_eb1"]), ("l2", "eb2"): rows(i["L2_ffn_eb2"]),
        ("l2", "ew3"): i["L2_ffn_ew3"].transpose(0, 2, 1).reshape(E // 2, P, D).transpose(1, 0, 2).reshape(P, -1),
        ("l2", "eb3"): tall(i["L2_ffn_eb3"]),
        ("l2", "sellng"): rows(i["L2_ffn_sel_ln_g"]), ("l2", "sellnb"): rows(i["L2_ffn_sel_ln_b"]),
        ("l3", "wprojT"): i["L3_xattn_w_proj"].T, ("l3", "bproj"): rows(i["L3_xattn_b_proj"]),
        ("l3", "rW1"): i["L3_ffn_rW1"], ("l3", "rb1"): col(i["L3_ffn_rb1"]),
        ("l3", "rW2"): i["L3_ffn_rW2"].reshape(CH3, P, HID3).transpose(1, 0, 2).reshape(P, -1), ("l3", "rb2"): col(i["L3_ffn_rb2"]),
        ("l3", "rW3"): i["L3_ffn_rW3"].reshape(CH3, P, E).transpose(1, 0, 2).reshape(P, -1), ("l3", "rb3"): rows(i["L3_ffn_rb3"]),
        ("l3", "eb1"): col(i["L3_ffn_eb1"]), ("l3", "eb2"): col(i["L3_ffn_eb2"]),
    }
    arrays = {"x": i["x"], "ctx": i["ctx_1024"], "ctxT": i["ctx_1024"].transpose(2, 0, 1),
              "index": np.concatenate([v for w in ("b", "t") for v in (rows(i["L2_ffn_index_" + w]), col(i["L2_ffn_index_" + w]))],
                                      axis=1)}
    arrays["l1_experts"] = np.concatenate([
        i["L1_ffn_W1a"], i["L1_ffn_W1b"],
        i["L1_ffn_W2"].reshape(E, CH1, P, D).transpose(0, 2, 1, 3).reshape(E, P, -1)], axis=2)
    arrays["l3_experts"] = np.concatenate([
        i["L3_ffn_eW1"], i["L3_ffn_eW2"].reshape(E, CH3, P, D).transpose(0, 2, 1, 3).reshape(E, P, -1)], axis=2)
    vals = np.ones((T, B, HEADS, HEAD + 1), i["ctx_1024"].dtype)
    vals[..., 0:HEAD] = i["ctx_1024"].reshape(B, T, HEADS, HEAD).transpose(1, 0, 2, 3)
    arrays["l3_values"] = vals.reshape(P, -1)
    for pack, names in PACKS.items():
        arrays[pack] = np.concatenate([fields.get((pack, n), c.get(n)) for n, _ in names], axis=1)

    nc = bacc.Bacc("TRN2", target_bir_lowering=False, num_devices=1)
    feeds, dram = {}, {}
    for name, a in arrays.items():
        a = np.ascontiguousarray(a)
        feeds[f"in_{name}_dram"] = a
        dram[name] = nc.dram_tensor(f"in_{name}_dram", a.shape, mybir.dt.from_np(a.dtype), kind="ExternalInput").ap()
    out = nc.dram_tensor("out_0_dram", (B, T, D), F32, kind="ExternalOutput").ap()
    build(nc, dram, out, UPTO)
    r = run_bass_kernel_spmd(nc, [feeds], core_ids=[0])
    return r.results[0]["out_0_dram"]
```

```python
import math
from contextlib import ExitStack

import numpy as np

import concourse.bass as bass
from concourse import mybir

F32 = mybir.dt.float32
I32 = mybir.dt.int32
U32 = mybir.dt.uint32
ALU = mybir.AluOpType
ACT = mybir.ActivationFunctionType
AX = mybir.AxisListType

P = 128
B = 16
D = 128
T = 128
E = 8
QUAD = 4
GROUPS = B // QUAD
LN_EPS = 1e-5
RMS_EPS = float(np.finfo(np.float32).eps)
FAR = 1e30

CORR_TOP = int(math.floor(math.log(T)))
HEAD = 8
HEADS = D // HEAD
HID0 = 64
PAIRS = E * E
HID1 = 512
CH1 = HID1 // P
CAP1 = 52
RING1 = 3 * HID1 + 2 * CH1 + 1
HID2 = 64
M2 = 256
HID3 = 512
CH3 = HID3 // P
CAP = int(T / E * 1.25)
SLOTS = E * CAP
TILE = 32
UPTO = 8

PACKS = {
    "fourier": [("dft", 2 * T), ("wk", D), ("wq", D), ("idft", 2 * T), ("wv", D), ("wo", D), ("ident", P)],
    "consts": [("blockmask", HEADS), ("dmod", 1), ("iota8", HEAD), ("prio", E), ("prio4", 4), ("lower", E * E),
               ("rownum", 2 * B), ("ones", P), ("before", P), ("causal", P), ("slot", CAP1), ("token", B),
               ("tokenrow", B * T), ("earlier", 2 * M2)],
    "l0f": [("wgateT", TILE), ("sw1T", P), ("sw3T", P), ("sw2T", D), ("ebias", E), ("w13", E * 2 * HID0), ("w2", E * D)],
    "l1x": [("Wq", D), ("Wk", D), ("Wv", D), ("bq", 1), ("bk", 1), ("bv", D)],
    "l1f": [("lnw", 1), ("Wg", TILE), ("bg", E)],
    "l2": [("WqT", D), ("sw12T", 2 * HID2), ("sb12", 2 * HID2), ("sw3T", D), ("sb3", D), ("slng", 1), ("slnb", 1),
           ("gateT", E + 1), ("gateb", E + 1), ("expbias", E), ("ew1T", E * HID2), ("ew2T", E * HID2),
           ("eb1", E * HID2), ("eb2", E * HID2), ("ew3", E // 2 * D), ("eb3", D), ("sellng", HID2), ("sellnb", HID2)],
    "l3": [("wprojT", D), ("bproj", D), ("rb1", CH3), ("rb2", CH3), ("rW3", CH3 * TILE), ("rb3", E), ("rW1", HID3), ("rW2", CH3 * HID3)],
}


def pack_offsets(pack):
    at, out = 0, {}
    for name, n in PACKS[pack]:
        out[name] = (at, at + n)
        at += n
    return out, at


def build(nc, dram, out, upto):
    f = ExitStack()
    with f:
        sems = {}

        resting = [("l0x_" + n, c) for n, c in (
            ("khat_mm", B // 2), ("khat", B // 2), ("k_mm", 2 * GROUPS), ("k", 2 * GROUPS), ("u_mm", GROUPS), ("u", GROUPS),
            ("v_mm", GROUPS), ("v", GROUPS), ("qhat_mm", GROUPS), ("qhat", GROUPS), ("q_mm", GROUPS), ("prod", GROUPS),
            ("corr_mm", GROUPS), ("diff", 1), ("exp", 1), ("mix", GROUPS), ("mix_turned", GROUPS), ("mixed", GROUPS),
            ("out_mm", GROUPS))] + [("l0f_" + n, c) for n, c in (
                ("logits", 1), ("gate", GROUPS), ("up", GROUPS), ("gated", GROUPS), ("shared", GROUPS), ("added", GROUPS),
                ("counts", 1), ("local", 1), ("picked", 1), ("pair", 1), ("pair13_mm", 1), ("pair_turned", GROUPS),
                ("pairT", GROUPS), ("pair13", 1), ("pre_mm", 1), ("pre", 2), ("silu", GROUPS), ("silu2", 2), ("act", 1),
                ("sums_mm", 1), ("hidden", 1), ("hidden_turned", 1), ("hiddenT", 1), ("routed", 1), ("centred", 1))]
        heirs = ["l3x_" + n for n in ("values", "keys0", "keys1", "score", "probs", "turned", "probsT", "weigh", "weighed",
                                      "back", "att", "att_turned", "attT", "out", "cleared", "start", "largest")] + [
            "l3f_" + n for n in ("start", "first", "route1", "second", "route2", "third", "route3", "third_turned", "summed",
                                      "centred", "exp")] + [
            "rest_" + n for n in ("any", "any_mm", "flag", "weights", "gate", "up", "silu", "hidden", "down", "y", "turned",
                                  "added", "column")]
        inherits = dict(zip(heirs, resting))

        def spent(name):
            return inherits[name][1]

        def sem(name):
            if name in inherits:
                name = inherits[name][0]
            if name not in sems:
                sems[name] = f.enter_context(nc.semaphore(name))
            return sems[name]

        every = ("l0x", "l0f", "l1x", "l1", "l2x", "l2f", "l3x", "l3")
        adds = {"norm_" + what: [(tag, n * (2 if tag == "l1" and what in ("var", "rstd") else 1)) for tag in every
                                 if not (tag == "l0x" and what in ("turned", "xnT"))]
                for what, n in (("var", GROUPS), ("rstd", GROUPS), ("xn", GROUPS), ("turned", GROUPS), ("xnT", GROUPS))}
        for what in ("start", "k_mm", "v_mm", "k", "v", "q_mm", "q", "logits", "neg", "exp", "turned2", "attnT", "out"):
            adds["attn_" + what] = [("l1x", 1 if what == "start" else GROUPS), ("l2x", 1 if what == "start" else GROUPS)]
        for what, n1, n3 in (("taken", 1, 1), ("before_mm", 1, 1), ("onehot", GROUPS, GROUPS), ("slots_mm", B, B),
                             ("slots", B, B), ("gate_mm", 2 * E * CH1, 0), ("silu", 2 * E * CH1, 0),
                             ("up_mm", 2 * E * CH1, E * CH3), ("hidden", 2 * E * CH1, E * CH3), ("down_mm", 2 * E, E),
                             ("y", 2 * E, E), ("weighted", 1, 1), ("turn_w", B, B), ("turn_y", B, B), ("turned_w", B, B),
                             ("turned_y", B, B), ("combined", B, B), ("added", GROUPS, GROUPS), ("ring0", 8 * E, 4 * E), ("ring1", 8 * E, 4 * E), ("ring2", 0, 4 * E), ("ring3", 0, 4 * E)):
            adds["slotted_" + what] = [("l1", n1), ("l3", n3)]

        for what in ("mm", "copied"):
            adds["router_" + what] = [("l0f", 1), ("l1", 1)]

        def past(tag, name):
            tags = [t for t, _ in adds[name]]
            return sum(n for _, n in adds[name][:tags.index(tag)])

        def sb(name, shape, dt=F32):
            return f.enter_context(nc.sbuf_tensor(name, shape, dt))

        def spread(ap, axis, shape):
            return ap.unsqueeze(axis).to_broadcast(shape)

        ps = f.enter_context(nc.psum_tensor("ps", [P, 8, 512], F32))

        def bank(i):
            return ps[:, i, :]

        def bank4(i):
            return ps[:, i, :].rearrange("p (b c) -> p b c", b=QUAD)

        packed, field = {}, {}
        for pack in PACKS:
            offsets, width = pack_offsets(pack)
            packed[pack] = sb(f"pack_{pack}", [P, width])
            for name, (lo, hi) in offsets.items():
                field[pack, name] = packed[pack][:, lo:hi]
        x = sb("x", [P, B, D])
        xn = sb("xn", [P, B, D])
        xnT = sb("xnT", [P, B, T])
        ctx_tok = sb("ctx_tok", [P, B, D])
        ctxT = sb("ctxT", [P, B, T])
        stats = sb("stats", [P, B, 6])
        meanvar = sb("meanvar", [P, B, 2])
        vareps = sb("vareps", [P, B])
        rstd = sb("rstd", [P, B])
        rms_rstd = sb("rms_rstd", [P, B])
        minushalf = sb("minushalf", [P, B])
        row_at = sb("row_at", [P, M2 + M2 // P])
        row_first = sb("row_first", [P, M2 // P])
        zero = sb("zero", [P, 1])
        index_sb = sb("index_sb", [P, 2, M2 + M2 // P], I32)
        arena_a = sb("arena_a", [P, 8192])
        arena_b = sb("arena_b", [P, 15360])

        def carve(arena, start=0):
            at = [start]

            def take(n, pattern=None, **sizes):
                ap = arena[:, at[0]:at[0] + n]
                at[0] += n
                assert at[0] <= arena.shape[1], at[0]
                return ap.rearrange(pattern, **sizes) if pattern else ap
            return take

        ident = field["fourier", "ident"]
        chain = [0]

        def link(v, ins):
            chain[0] += 1
            ins.then_inc(sem("vector_chain"), 1)
            v.wait_ge(sem("vector_chain"), chain[0])

        V = nc.vector
        S = nc.scalar
        TE = nc.tensor

        measures, starts, ahead = {}, {}, {}

        def norm(tag, order=range(GROUPS), rms=None):
            order = list(order)

            def measure(v, g):
                q = slice(QUAD * g, QUAD * g + QUAD)
                for b in range(QUAD * g, QUAD * g + QUAD):
                    last = V.bn_stats(stats[:, b, :], x[:, b, :])
                link(v, last)
                for b in range(QUAD * g, QUAD * g + QUAD):
                    last = V.bn_aggr(meanvar[:, b, :], stats[:, b, :])
                link(v, last)
                V.tensor_scalar_add(vareps[:, q], meanvar[:, q, 1], LN_EPS).then_inc(sem("norm_var"), 1)
            measures[tag] = measure

            def vector(v):
                if rms:
                    v.wait_ge(sem("norm_rstd"), past(tag, "norm_rstd") + GROUPS)
                    link(v, V.tensor_tensor(vareps[:, :], rstd[:, :], rstd[:, :], ALU.mult))
                    link(v, V.tensor_tensor(vareps[:, :], vareps[:, :], meanvar[:, :, 1], ALU.mult))
                    for g in range(GROUPS):
                        q = slice(QUAD * g, QUAD * g + QUAD)
                        V.tensor_scalar_add(vareps[:, q], vareps[:, q], RMS_EPS).then_inc(sem("norm_var"), 1)
                for g in range(GROUPS):
                    q = slice(QUAD * g, QUAD * g + QUAD)
                    v.wait_ge(sem("norm_rstd"), past(tag, "norm_rstd") + (GROUPS if rms else 0) + order.index(g) + 1)
                    if rms:
                        link(v, V.tensor_tensor(rstd[:, q], rstd[:, q], rms_rstd[:, q], ALU.mult))
                    for b in range(QUAD * g, QUAD * g + QUAD):
                        last = V.tensor_scalar(xn[:, b, :], x[:, b, :], meanvar[:, b, 0:1], rstd[:, b:b + 1],
                                               ALU.subtract, ALU.mult)
                    last.then_inc(sem("norm_xn"), 1)

            def gpsimd(p):
                for i, dst in enumerate((rstd, rms_rstd) if rms else (rstd,)):
                    for j, g in enumerate(order):
                        q = slice(QUAD * g, QUAD * g + QUAD)
                        p.wait_ge(sem("norm_var"), past(tag, "norm_var") + GROUPS * i + j + 1)
                        nc.gpsimd.tensor_tensor(dst[:, q], vareps[:, q], minushalf[:, q], ALU.pow).then_inc(sem("norm_rstd"), 1)

            def tensor(pe):
                for g in range(GROUPS):
                    pe.wait_ge(sem("norm_xn"), past(tag, "norm_xn") + g + 1)
                    for i in range(QUAD):
                        last = TE.transpose(bank4(g)[:, i, :], xn[:, QUAD * g + i, :], ident)
                    last.then_inc(sem("norm_turned"), 1)

            def scalar(a):
                for g in range(GROUPS):
                    a.wait_ge(sem("norm_turned"), past(tag, "norm_turned") + g + 1)
                    S.activation(xnT[:, QUAD * g:QUAD * g + QUAD, :], bank4(g), ACT.Copy if not rms else ACT.Identity,
                                 scale=rms if rms else 1.0).then_inc(sem("norm_xnT"), 1)
            return vector, gpsimd, tensor, scalar

        def starting(v, following):
            if following in starts:
                v.sem_inc(starts[following], 1)

        def final(v, following, g, last):
            link(v, last)
            if following in measures:
                measures[following](v, g)

        def first_largest(v, onehot, score, prio, best, shape):
            link(v, V.tensor_reduce(best, score, AX.X, ALU.max))
            link(v, V.tensor_tensor(onehot, score, spread(best, len(shape) - 1, shape), ALU.is_equal))
            link(v, V.tensor_tensor(onehot, onehot, prio, ALU.mult))
            link(v, V.tensor_reduce(best, onehot, AX.X, ALU.max))
            link(v, V.tensor_tensor(onehot, onehot, spread(best, len(shape) - 1, shape), ALU.is_equal))

        def router(tag, weights, logitsT, done):
            logits = bank(6).rearrange("p (i g e) -> p g i e", i=QUAD, g=GROUPS)[:, :, :, 0:E]

            def route(pe):
                for g in range(GROUPS):
                    pe.wait_ge(sem("norm_xnT"), past(tag, "norm_xnT") + g + 1)
                    last = TE.matmul(bank(7)[TILE * g:TILE * g + TILE, :], weights, xnT[:, QUAD * g:QUAD * g + QUAD, :],
                                     start=True, stop=True)
                last.then_inc(sem("router_mm"), 1)

            def turn(pe):
                pe.wait_ge(sem("router_copied"), past(tag, "router_copied") + 1)
                for i in range(QUAD):
                    last = TE.transpose(bank4(6)[:, i, :], logitsT[:, T * i:T * i + T], ident)
                last.then_inc(sem(done), 1)

            def copy(a):
                a.wait_ge(sem("router_mm"), past(tag, "router_mm") + 1)
                S.copy(logitsT, bank(7)).then_inc(sem("router_copied"), 1)
            return logits, route, turn, copy

        def l0_attention():
            ta, tb = carve(arena_a), carve(arena_b)
            k_hat = ta(B * 2 * T, "p (b f) -> p b f", b=B)
            k1 = ta(B * D, "p (b d) -> p b d", b=B)
            k2 = ta(B * D, "p (b d) -> p b d", b=B)
            q_hat = tb(B * T, "p (b f) -> p b f", b=B)
            values = tb(B * D, "p (b o) -> p b o", b=B)
            prod1 = tb(B * D, "p (b d) -> p b d", b=B)
            prod2 = tb(B * D, "p (b d) -> p b d", b=B)
            mix_T = prod1
            mix = prod2
            top = tb(B * 8, "p (b k) -> p b k", b=B)
            where = tb(B * 8, "p (b k) -> p b k", b=B).bitcast(U32)
            wsoft = tb(B * CORR_TOP, "p (b k) -> p b k", b=B)
            wsum = tb(B)
            shift = tb(B * CORR_TOP, "p (b k) -> p b k", b=B)
            shift_i = tb(B * CORR_TOP, "p (b k) -> p b k", b=B).bitcast(I32)
            hit = tb(B * CORR_TOP * HEAD, "p (b k r) -> p b k r", b=B, k=CORR_TOP)
            mix8 = tb(B * HEAD, "p (b r) -> p b r", b=B)
            F = lambda n: field["fourier", n]
            C = lambda n: field["consts", n]

            def tensor(pe):
                pe.wait_ge(sem("load_fourier"), 16)
                pe.wait_ge(sem("load_ctx"), 32)
                for u in range(B // 2):
                    if u >= 4:
                        pe.wait_ge(sem("l0x_khat"), u - 3)
                    for i in range(2):
                        last = TE.matmul(bank(u % 4)[:, 256 * i:256 * i + 256], ctx_tok[:, 2 * u + i, :], F("dft"),
                                         start=True, stop=True)
                    last.then_inc(sem("l0x_khat_mm"), 1)
                for h in range(2):
                    for g in range(GROUPS):
                        pe.wait_ge(sem("l0x_khat"), 2 * g + 2)
                        if h:
                            pe.wait_ge(sem("l0x_k"), g + 1)
                        for i in range(QUAD):
                            last = TE.matmul(bank4(4 + g)[:, i, :], k_hat[:, QUAD * g + i, T * h:T * h + T], F("wk"),
                                             start=True, stop=True)
                        last.then_inc(sem("l0x_k_mm"), 1)
                pe.wait_ge(sem("l0x_khat"), B // 2)
                for g in range(GROUPS):
                    for i in range(QUAD):
                        last = TE.matmul(bank4(g)[:, i, :], ctx_tok[:, QUAD * g + i, :], F("wo"), start=True, stop=True)
                    last.then_inc(sem("l0x_u_mm"), 1)
                for g in range(GROUPS):
                    pe.wait_ge(sem("l0x_u"), g + 1)
                    last = TE.matmul(bank(g), F("wv"), q_hat[:, QUAD * g:QUAD * g + QUAD, :], start=True, stop=True)
                    last.then_inc(sem("l0x_v_mm"), 1)
                for g in range(GROUPS):
                    pe.wait_ge(sem("norm_xn"), past("l0x", "norm_xn") + g + 1)
                    pe.wait_ge(sem("l0x_k"), GROUPS + g + 1)
                    for i in range(QUAD):
                        last = TE.matmul(bank4(4 + g)[:, i, :], xn[:, QUAD * g + i, :], F("dft")[:, 0:T],
                                         start=True, stop=True)
                    last.then_inc(sem("l0x_qhat_mm"), 1)
                for g in range(GROUPS):
                    pe.wait_ge(sem("l0x_qhat"), g + 1)
                    pe.wait_ge(sem("l0x_v"), g + 1)
                    for i in range(QUAD):
                        last = TE.matmul(bank4(g)[:, i, :], q_hat[:, QUAD * g + i, :], F("wq"), start=True, stop=True)
                    last.then_inc(sem("l0x_q_mm"), 1)
                for g in range(GROUPS):
                    pe.wait_ge(sem("l0x_prod"), g + 1)
                    for i in range(QUAD):
                        b = QUAD * g + i
                        TE.matmul(bank4(4 + g)[:, i, :], prod1[:, b, :], F("idft")[:, 0:T], start=True, stop=False)
                        last = TE.matmul(bank4(4 + g)[:, i, :], prod2[:, b, :], F("idft")[:, T:2 * T],
                                         start=False, stop=True)
                    last.then_inc(sem("l0x_corr_mm"), 1)
                for g in range(GROUPS):
                    pe.wait_ge(sem("l0x_mix"), g + 1)
                    for i in range(QUAD):
                        last = TE.transpose(bank4(g)[:, i, :], mix_T[:, QUAD * g + i, :], ident)
                    last.then_inc(sem("l0x_mix_turned"), 1)
                for g in range(GROUPS):
                    pe.wait_ge(sem("l0x_mixed"), g + 1)
                    for i in range(QUAD):
                        b = QUAD * g + i
                        last = TE.matmul(bank4(4 + g)[:, i, :], mix[:, b, :], values[:, b, :], start=True, stop=True)
                    last.then_inc(sem("l0x_out_mm"), 1)

            def scalar(a):
                for u in range(B // 2):
                    a.wait_ge(sem("l0x_khat_mm"), u + 1)
                    S.copy(k_hat[:, 2 * u:2 * u + 2, :], bank(u % 4).rearrange("p (b f) -> p b f", b=2)
                           ).then_inc(sem("l0x_khat"), 1)
                for g in range(GROUPS):
                    a.wait_ge(sem("l0x_u_mm"), g + 1)
                    S.copy(q_hat[:, QUAD * g:QUAD * g + QUAD, :], bank4(g)).then_inc(sem("l0x_u"), 1)
                for g in range(GROUPS):
                    a.wait_ge(sem("l0x_v_mm"), g + 1)
                    S.copy(values[:, QUAD * g:QUAD * g + QUAD, :], bank4(g)).then_inc(sem("l0x_v"), 1)
                a.wait_ge(sem("l0x_v_mm"), GROUPS)
                for g in range(GROUPS):
                    a.wait_ge(sem("l0x_qhat_mm"), g + 1)
                    S.copy(q_hat[:, QUAD * g:QUAD * g + QUAD, :], bank4(4 + g)).then_inc(sem("l0x_qhat"), 1)
                a.wait_ge(sem("l0x_diff"), 1)
                S.activation(wsoft, wsoft, ACT.Exp).then_inc(sem("l0x_exp"), 1)
                for g in range(GROUPS):
                    a.wait_ge(sem("l0x_mix_turned"), g + 1)
                    S.copy(mix[:, QUAD * g:QUAD * g + QUAD, :].rearrange("p b (r h) -> p b h r", h=HEADS),
                           bank4(g).rearrange("p b (h r) -> p b h r", h=HEADS)).then_inc(sem("l0x_mixed"), 1)

            def vector(v):
                for h, dst in enumerate((k1, k2)):
                    for g in range(GROUPS):
                        v.wait_ge(sem("l0x_k_mm"), GROUPS * h + g + 1)
                        V.tensor_copy(dst[:, QUAD * g:QUAD * g + QUAD, :], bank4(4 + g)).then_inc(sem("l0x_k"), 1)
                v.wait_ge(sem("load_x"), 16)
                for g in range(GROUPS):
                    measures["l0x"](v, g)
                norm_l0x[0](v)
                v.wait_ge(sem("l0x_k"), 2 * GROUPS)
                for g in range(GROUPS):
                    s = slice(QUAD * g, QUAD * g + QUAD)
                    v.wait_ge(sem("l0x_q_mm"), g + 1)
                    V.tensor_tensor(prod1[:, s, :], bank4(g), k1[:, s, :], ALU.mult)
                    V.tensor_tensor(prod2[:, s, :], bank4(g), k2[:, s, :], ALU.mult).then_inc(sem("l0x_prod"), 1)
                for g in range(GROUPS):
                    v.wait_ge(sem("l0x_corr_mm"), g + 1)
                    for i in range(QUAD):
                        b = QUAD * g + i
                        last = V.max(top[:, b, :], bank4(4 + g)[:, i, :])
                    link(v, last)
                    for i in range(QUAD):
                        b = QUAD * g + i
                        last = V.max_index(where[:, b, :], top[:, b, :], bank4(4 + g)[:, i, :])
                link(v, last)
                four = [P, B, CORR_TOP]
                V.tensor_tensor(wsoft, top[:, :, 0:CORR_TOP], top[:, :, 0:1].to_broadcast(four),
                                ALU.subtract).then_inc(sem("l0x_diff"), 1)
                link(v, V.tensor_copy(shift, where[:, :, 0:CORR_TOP]))
                link(v, V.tensor_scalar(shift_i, shift, -1.0, C("dmod"), ALU.mult, ALU.add))
                link(v, V.tensor_scalar(shift_i, shift_i, HEAD - 1, None, ALU.bitwise_and))
                link(v, V.tensor_copy(shift, shift_i))
                full = [P, B, CORR_TOP, HEAD]
                link(v, V.tensor_tensor(hit, spread(shift, 3, full),
                                        C("iota8").unsqueeze(1).unsqueeze(1).to_broadcast(full), ALU.is_equal))
                v.wait_ge(sem("l0x_exp"), 1)
                link(v, V.tensor_reduce(wsum, wsoft, AX.X, ALU.add))
                link(v, V.reciprocal(wsum, wsum))
                link(v, V.tensor_tensor(wsoft, wsoft, spread(wsum, 2, four), ALU.mult))
                link(v, V.tensor_tensor(hit, hit, spread(wsoft, 3, full), ALU.mult))
                link(v, V.tensor_reduce(mix8, hit.rearrange("p b k r -> p b r k"), AX.X, ALU.add))
                for g in range(GROUPS):
                    s = slice(QUAD * g, QUAD * g + QUAD)
                    shape = [P, QUAD, HEADS, HEAD]
                    V.tensor_tensor(mix_T[:, s, :].rearrange("p b (h r) -> p b h r", h=HEADS),
                                    spread(mix8[:, s, :], 2, shape),
                                    C("blockmask").unsqueeze(1).unsqueeze(3).to_broadcast(shape),
                                    ALU.mult).then_inc(sem("l0x_mix"), 1)
                for g in range(GROUPS):
                    s = slice(QUAD * g, QUAD * g + QUAD)
                    v.wait_ge(sem("l0x_out_mm"), g + 1)
                    final(v, "l0f", g, V.tensor_tensor(x[:, s, :], bank4(4 + g), x[:, s, :], ALU.add))
            norm_l0x = norm("l0x")
            return vector, norm_l0x[1], tensor, scalar

        def l0_experts():
            ta, tb = carve(arena_a), carve(arena_b)
            F = lambda n: field["l0f", n]
            C = lambda n: field["consts", n]
            gated = ta(B * T, "p (b l) -> p b l", b=B)
            pairT = ta(B * T, "p (b r) -> p b r", b=B)
            silu = ta(2 * 512, "p (i c) -> p i c", i=2)
            picked = ta(E * P, "p (g k e h) -> p g k e h", g=E, k=2, e=E)
            pair13 = ta(3 * HID0, "p (i h) -> p i h", i=3)
            logitsT = ta(512)
            sums = ta(HID0)
            hiddenT = ta(PAIRS)
            pair = tb(B * 2 * PAIRS, "p (r e g) -> p r e g", r=2 * B, e=E)
            pre = tb(2 * B * HID0, "p (b k h) -> p b k h", k=2, b=B)
            act = tb(2 * B * HID0, "p (b k h) -> p b k h", k=2, b=B)
            score = tb(B * E, "p (b e) -> p b e", b=B)
            biased = tb(B * E, "p (b e) -> p b e", b=B)
            group = tb(B * 4, "p (b e) -> p b e", b=B)
            hot4 = tb(B * 4, "p (b e) -> p b e", b=B)
            keep4 = tb(B * 4, "p (b e) -> p b e", b=B)
            best = tb(B)
            chosen = tb(B * 2 * E, "p (b k e) -> p b k e", b=B, k=2)
            tmp = tb(B * 2 * E, "p (b k e) -> p b k e", b=B, k=2)
            weight = tb(B * 2, "p (b k) -> p b k", b=B)
            local = tb(E)
            ends = tb(E)
            low = tb(E * E, "p (e c) -> p e c", e=E)
            reached = tb(2 * B * (E + 1), "p (r e) -> p r e", r=2 * B)
            member = tb(2 * B * E, "p (r e) -> p r e", r=2 * B)
            by8 = [P, B, E]
            by4 = [P, B, 4]
            n = norm("l0f")
            logits, route, turn_logits, copy_logits = router("l0f", F("wgateT"), logitsT, "l0f_logits")

            def tensor(pe):
                n[2](pe)
                pe.wait_ge(sem("load_l0f"), 16)
                route(pe)
                def down(g):
                    pe.wait_ge(sem("l0f_gated"), g + 1)
                    if g >= 2:
                        pe.wait_ge(sem("l0f_added"), g - 1)
                    for i in range(QUAD):
                        last = TE.matmul(bank4(4 + g % 2)[:, i, :], gated[:, QUAD * g + i, :], F("sw2T"),
                                         start=True, stop=True)
                    last.then_inc(sem("l0f_shared"), 1)
                for g in range(GROUPS):
                    if g >= 2:
                        pe.wait_ge(sem("l0f_gated"), g - 1)
                    xb = xnT[:, QUAD * g:QUAD * g + QUAD, :]
                    TE.matmul(bank(g % 2), F("sw1T"), xb, start=True, stop=True).then_inc(sem("l0f_gate"), 1)
                    TE.matmul(bank(2 + g % 2), F("sw3T"), xb, start=True, stop=True).then_inc(sem("l0f_up"), 1)
                    if g == 0:
                        turn_logits(pe)
                    if g:
                        down(g - 1)
                down(GROUPS - 1)
                pe.wait_ge(sem("l0f_local"), 1)
                TE.matmul(bank(7)[:, 256:256 + E], C("ones"), local, start=True, stop=True).then_inc(sem("l0f_counts"), 1)
                pe.wait_ge(sem("l0f_picked"), 1)
                for g in range(E):
                    last = TE.matmul(bank(6)[:, 0:2 * HID0], picked[:, g, :, :, :],
                                     F("w13")[:, 2 * HID0 * g:2 * HID0 * (g + 1)], start=(g == 0), stop=(g == E - 1))
                last.then_inc(sem("l0f_pair13_mm"), 1)
                pe.wait_ge(sem("l0f_pair"), 1)
                for g in range(GROUPS):
                    if g < 2:
                        pe.wait_ge(sem("l0f_gated"), GROUPS)
                    for i in range(QUAD):
                        last = TE.transpose(bank4(g)[:, i, :], pair[:, 2 * (QUAD * g + i):2 * (QUAD * g + i) + 2, :, :],
                                            ident)
                    last.then_inc(sem("l0f_pair_turned"), 1)
                pe.wait_ge(sem("l0f_pair13"), 1)
                pe.wait_ge(sem("l0f_pairT"), GROUPS)
                pe.wait_ge(sem("l0f_added"), GROUPS)
                for b in range(B):
                    last = TE.matmul(bank4(4 + b // QUAD)[:, b % QUAD, :], pairT[:, b, :], pair13[:, 0:2, :],
                                     start=True, stop=True)
                last.then_inc(sem("l0f_pre_mm"), 1)
                pe.wait_ge(sem("l0f_act"), 1)
                for k in range(2):
                    for b in range(B):
                        last = TE.matmul(bank(0)[0:PAIRS, 0:HID0], pair[:, 2 * b + k, :, :], act[:, b, k, :],
                                         start=(k == 0 and b == 0), stop=(k == 1 and b == B - 1))
                last.then_inc(sem("l0f_sums_mm"), 1)
                pe.wait_ge(sem("l0f_hidden"), 1)
                TE.transpose(bank(1)[0:HID0, 0:PAIRS], sums[0:PAIRS, :], ident[0:PAIRS, 0:PAIRS]).then_inc(sem("l0f_hidden_turned"), 1)
                pe.wait_ge(sem("l0f_hiddenT"), 1)
                hT = hiddenT[0:HID0, :].rearrange("p (e g) -> p g e", e=E)
                for g in range(E):
                    last = TE.matmul(bank(2)[0:E, 0:D], hT[:, g, :], F("w2")[0:HID0, D * g:D * g + D],
                                     start=(g == 0), stop=(g == E - 1))
                last.then_inc(sem("l0f_routed"), 1)

            def scalar(a):
                n[3](a)
                copy_logits(a)
                a.wait_ge(sem("l0f_centred"), 1)
                S.activation(score, score, ACT.Exp).then_inc(sem("l0f_exp"), 1)
                for g in range(GROUPS):
                    a.wait_ge(sem("l0f_gate"), g + 1)
                    if g >= 2:
                        a.wait_ge(sem("l0f_gated"), g - 1)
                    S.activation(silu[:, g % 2, :], bank(g % 2), ACT.Silu).then_inc(sem("l0f_silu"), 1)
                for g in range(GROUPS):
                    a.wait_ge(sem("l0f_pair_turned"), g + 1)
                    S.copy(pairT[:, QUAD * g:QUAD * g + QUAD, :], bank4(g)).then_inc(sem("l0f_pairT"), 1)
                for k in range(2):
                    a.wait_ge(sem("l0f_pre"), k + 1)
                    S.activation(act[:, 8 * k:8 * k + 8, :, :], pre[:, 8 * k:8 * k + 8, :, :], ACT.Silu).then_inc(sem("l0f_silu2"), 1)

            def vector(v):
                n[0](v)
                v.wait_ge(sem("load_l0f"), 16)
                link(v, V.memset(pair13, 0.0))
                link(v, V.memset(picked, 0.0))
                v.wait_ge(sem("norm_xnT"), past("l0f", "norm_xnT") + 1)
                for g in range(E):
                    last = V.tensor_copy(picked[:, g, :, :, g], spread(xnT[:, 0, 0:E], 1, [P, 2, E]))
                last.then_inc(sem("l0f_picked"), 1)
                v.wait_ge(sem("l0f_logits"), 1)
                link(v, V.tensor_copy(score.rearrange("p (g i) e -> p g i e", g=GROUPS), logits))
                link(v, V.tensor_reduce(best, score, AX.X, ALU.max))
                V.tensor_tensor(score, score, spread(best, 2, by8), ALU.subtract).then_inc(sem("l0f_centred"), 1)
                def shared(g):
                    v.wait_ge(sem("l0f_silu"), g + 1)
                    v.wait_ge(sem("l0f_up"), g + 1)
                    V.tensor_tensor(gated[:, QUAD * g:QUAD * g + QUAD, :],
                                    silu[:, g % 2, :].rearrange("p (b l) -> p b l", b=QUAD),
                                    bank4(2 + g % 2), ALU.mult).then_inc(sem("l0f_gated"), 1)
                def shared_add(g):
                    v.wait_ge(sem("l0f_shared"), g + 1)
                    s = slice(QUAD * g, QUAD * g + QUAD)
                    V.tensor_tensor(x[:, s, :], bank4(4 + g % 2), x[:, s, :], ALU.add).then_inc(sem("l0f_added"), 1)

                def measured(g):
                    if "l1x" in measures:
                        measures["l1x"](v, g)
                v.wait_ge(sem("l0f_exp"), 1)
                link(v, V.tensor_reduce(best, score, AX.X, ALU.add))
                link(v, V.reciprocal(best, best))
                link(v, V.tensor_tensor(score, score, spread(best, 2, by8), ALU.mult))
                link(v, V.tensor_tensor(biased, score, spread(F("ebias"), 1, by8), ALU.add))
                pairs = biased.rearrange("p b (g i) -> p b g i", i=2)
                link(v, V.tensor_tensor(group, pairs[:, :, :, 0], pairs[:, :, :, 1], ALU.add))
                prio4 = spread(C("prio4"), 1, by4)
                prio = spread(C("prio"), 1, by8)
                first_largest(v, keep4, group, prio4, best, by4)
                link(v, V.scalar_tensor_tensor(group, keep4, -FAR, group, ALU.mult, ALU.add))
                first_largest(v, hot4, group, prio4, best, by4)
                link(v, V.tensor_tensor(keep4, keep4, hot4, ALU.add))
                link(v, V.tensor_scalar(keep4, keep4, -1.0, FAR, ALU.add, ALU.mult))
                link(v, V.tensor_tensor(pairs, pairs, spread(keep4, 3, [P, B, 4, 2]), ALU.add))
                shared(0)
                for k in range(2):
                    first_largest(v, chosen[:, :, k, :], biased, prio, best, by8)
                    if k == 0:
                        link(v, V.scalar_tensor_tensor(biased, chosen[:, :, k, :], -FAR, biased, ALU.mult, ALU.add))
                    shared(1 + k)
                    shared_add(k)
                link(v, V.tensor_tensor(tmp, chosen, spread(score, 2, [P, B, 2, E]), ALU.mult))
                link(v, V.tensor_reduce(weight, tmp, AX.X, ALU.add))
                V.tensor_reduce(local, chosen.rearrange("p b k e -> p e b k"), AX.XY, ALU.add).then_inc(sem("l0f_local"), 1)
                shared(3)
                shared_add(2)
                shared_add(3)
                v.wait_ge(sem("l0f_counts"), 1)
                link(v, V.tensor_tensor(low, C("lower").rearrange("p (e c) -> p e c", e=E),
                                        spread(bank(7)[:, 256:256 + E], 1, [P, E, E]), ALU.mult))
                link(v, V.tensor_reduce(ends, low, AX.X, ALU.add))
                rows9 = [P, 2 * B, E]
                V.memset(reached[:, :, 0], 1.0)
                link(v, V.tensor_tensor(reached[:, :, 1:E + 1], spread(C("rownum"), 2, rows9),
                                        spread(ends, 1, rows9), ALU.is_ge))
                link(v, V.tensor_tensor(member, reached[:, :, 0:E], reached[:, :, 1:E + 1], ALU.subtract))
                full = [P, 2 * B, E, E]
                V.tensor_tensor(pair, spread(chosen.rearrange("p b k e -> p (b k) e"), 3, full),
                                spread(member, 2, full), ALU.mult).then_inc(sem("l0f_pair"), 1)
                v.wait_ge(sem("l0f_pair13_mm"), 1)
                for k in range(2):
                    V.tensor_copy(pair13[PAIRS * k:PAIRS * k + PAIRS, k, :], bank(6)[PAIRS * k:PAIRS * k + PAIRS, 0:HID0])
                V.tensor_copy(pair13[:, 2, :], bank(6)[:, HID0:2 * HID0]).then_inc(sem("l0f_pair13"), 1)
                v.wait_ge(sem("l0f_pre_mm"), 1)
                flat3 = lambda ap: ap.rearrange("p b k h -> p (b k) h")
                weighting = lambda r: spread(weight.rearrange("p b k -> p (b k)")[:, 2 * r.start:2 * r.stop], 2, [P, B, HID0])
                halves = [slice(8 * k, 8 * k + 8) for k in range(2)]
                for k, r in enumerate(halves):
                    V.tensor_tensor(flat3(pre[:, r, :, :]), ps[:, 4 + 2 * k:6 + 2 * k, :].rearrange("p c (b h) -> p (c b) h", b=8),
                                    weighting(r), ALU.mult).then_inc(sem("l0f_pre"), 1)
                for k, r in enumerate(halves):
                    v.wait_ge(sem("l0f_silu2"), k + 1)
                    last = V.tensor_tensor(flat3(act[:, r, :, :]), flat3(act[:, r, :, :]), weighting(r), ALU.mult)
                last.then_inc(sem("l0f_act"), 1)
                v.wait_ge(sem("l0f_added"), GROUPS)
                for g in range(1, GROUPS):
                    measured(g)
                v.wait_ge(sem("l0f_sums_mm"), 1)
                V.tensor_tensor(sums[0:PAIRS, :], bank(0)[0:PAIRS, 0:HID0], pair13[0:PAIRS, 2, :],
                                ALU.mult).then_inc(sem("l0f_hidden"), 1)
                v.wait_ge(sem("l0f_hidden_turned"), 1)
                V.tensor_copy(hiddenT[0:HID0, :], bank(1)[0:HID0, 0:PAIRS]).then_inc(sem("l0f_hiddenT"), 1)
                v.wait_ge(sem("l0f_routed"), 1)
                link(v, V.tensor_tensor(x[0:E, 0, :], bank(2)[0:E, 0:D], x[0:E, 0, :], ALU.add))
                starting(v, "l1x")
                measured(0)
            return vector, n[1], tensor, scalar

        def attention(tag, pack, wq, wk, wv, bq=None, bk=None, bv=None, causal=False):
            tb = carve(arena_b)
            qT = tb(B * T, "p (b l) -> p b l", b=B)
            attn = tb(B * T, "p (b l) -> p b l", b=B)
            attnT = tb(B * T, "p (b l) -> p b l", b=B)
            kT = tb(B * T, "p (b l) -> p b l", b=B)
            vals = tb(B * D, "p (b d) -> p b d", b=B)
            neg = tb(B)
            total = tb(B)
            F = lambda name: field[pack, name]
            scale = 1.0 / math.sqrt(D)
            following = {"l1x": "l1", "l2x": "l2f"}[tag]
            n = norm(tag, (1, 2, 3, 0) if tag == "l1x" else range(GROUPS))
            starts[tag] = sem("attn_start")
            quad = lambda ap, g: ap[:, QUAD * g:QUAD * g + QUAD, :]

            def tensor(pe):
                pe.wait_ge(sem("load_" + pack), 16)
                pe.wait_ge(sem("attn_start"), past(tag, "attn_start") + 1)
                for g in range(GROUPS):
                    TE.matmul(bank(g), F(wk), quad(ctxT, g), start=True, stop=True).then_inc(sem("attn_k_mm"), 1)
                    for i in range(QUAD):
                        last = TE.matmul(bank4(4 + g)[:, i, :], ctxT[:, QUAD * g + i, :], F(wv), start=True, stop=True)
                    last.then_inc(sem("attn_v_mm"), 1)
                pe.wait_ge(sem("attn_k"), past(tag, "attn_k") + GROUPS)
                n[2](pe)
                for g in range(GROUPS):
                    pe.wait_ge(sem("norm_xnT"), past(tag, "norm_xnT") + g + 1)
                    TE.matmul(bank(g), F(wq), quad(xnT, g), start=True, stop=True).then_inc(sem("attn_q_mm"), 1)
                pe.wait_ge(sem("attn_v"), past(tag, "attn_v") + GROUPS)
                for g in range(GROUPS):
                    pe.wait_ge(sem("attn_q"), past(tag, "attn_q") + g + 1)
                    for i in range(QUAD):
                        b = QUAD * g + i
                        last = TE.matmul(bank4(4 + g)[:, i, :], qT[:, b, :], kT[:, b, :], start=True, stop=True)
                    last.then_inc(sem("attn_logits"), 1)
                for g in range(GROUPS):
                    pe.wait_ge(sem("attn_exp"), past(tag, "attn_exp") + g + 1)
                    for i in range(QUAD):
                        last = TE.transpose(bank4(g)[:, i, :], attn[:, QUAD * g + i, :], ident)
                    last.then_inc(sem("attn_turned2"), 1)
                for g in range(GROUPS):
                    pe.wait_ge(sem("attn_attnT"), past(tag, "attn_attnT") + g + 1)
                    for i in range(QUAD):
                        b = QUAD * g + i
                        last = TE.matmul(bank4(4 + g)[:, i, :], attnT[:, b, :], vals[:, b, :], start=True, stop=True)
                    last.then_inc(sem("attn_out"), 1)

            def scalar(a):
                for g in range(GROUPS):
                    a.wait_ge(sem("attn_k_mm"), past(tag, "attn_k_mm") + g + 1)
                    if bk:
                        last = S.activation(quad(kT, g), bank4(g), ACT.Identity, bias=F(bk))
                    else:
                        last = S.copy(quad(kT, g), bank4(g))
                    last.then_inc(sem("attn_k"), 1)
                n[3](a)
                for g in range(GROUPS):
                    a.wait_ge(sem("attn_neg"), past(tag, "attn_neg") + g + 1)
                    for i in range(QUAD):
                        b = QUAD * g + i
                        src = attn[:, b, :] if causal else bank4(4 + g)[:, i, :]
                        last = S.activation(attn[:, b, :], src, ACT.Exp, bias=neg[:, b:b + 1], accum_out=total[:, b:b + 1])
                    last.then_inc(sem("attn_exp"), 1)

            def vector(v):
                n[0](v)
                v.wait_ge(sem("load_" + pack), 16)
                for g in range(GROUPS):
                    v.wait_ge(sem("attn_v_mm"), past(tag, "attn_v_mm") + g + 1)
                    if bv:
                        last = V.tensor_tensor(quad(vals, g), bank4(4 + g), spread(F(bv), 1, [P, QUAD, D]), ALU.add)
                    else:
                        last = V.tensor_copy(quad(vals, g), bank4(4 + g))
                    last.then_inc(sem("attn_v"), 1)
                for g in range(GROUPS):
                    v.wait_ge(sem("attn_q_mm"), past(tag, "attn_q_mm") + g + 1)
                    V.tensor_scalar(quad(qT, g), bank4(g), F(bq) if bq else 0.0, scale, ALU.add,
                                    ALU.mult).then_inc(sem("attn_q"), 1)
                for g in range(GROUPS):
                    v.wait_ge(sem("attn_logits"), past(tag, "attn_logits") + g + 1)
                    src = bank4(4 + g)
                    if causal:
                        src = quad(attn, g)
                        link(v, V.tensor_tensor(src, bank4(4 + g), spread(field["consts", "causal"], 1, [P, QUAD, T]), ALU.add))
                    V.tensor_reduce(neg[:, QUAD * g:QUAD * g + QUAD], src, AX.X, ALU.max,
                                    negate=True).then_inc(sem("attn_neg"), 1)
                if causal and "gather" in ahead:
                    ahead["gather"](v)
                for g in range(GROUPS):
                    v.wait_ge(sem("attn_turned2"), past(tag, "attn_turned2") + g + 1)
                    V.tensor_copy(quad(attnT, g), bank4(g)).then_inc(sem("attn_attnT"), 1)
                link(v, V.reciprocal(total, total))
                for g in range(GROUPS):
                    v.wait_ge(sem("attn_out"), past(tag, "attn_out") + g + 1)
                    for i in range(QUAD):
                        b = QUAD * g + i
                        last = V.scalar_tensor_tensor(x[:, b, :], bank4(4 + g)[:, i, :], total[:, b:b + 1], x[:, b, :],
                                                      ALU.mult, ALU.add)
                    final(v, following, g, last)

            def gpsimd(p):
                n[1](p)
                if causal and "scatter" in ahead:
                    ahead["scatter"](p)
            return vector, gpsimd, tensor, scalar

        def slotted(tag, cap, nb, gated, onehot, slots, hidden, silu, ring, turned_w, turned_y, taken, slotpos, weights,
                    channel_scale, left_over=None, any_left=None):
            per = E * cap
            parts = -(-per // P)
            of = E // parts
            part = per // parts
            rows = max(part, 96)
            units = [(e, b0) for e in range(E) for b0 in range(0, B, nb)]
            cols = nb * cap
            nw = 2 if gated else 1
            depth = len(ring)
            s_ = lambda what: sem("slotted_" + what)
            hot = onehot.rearrange("p (b e c) -> p b e c", b=B, e=E)
            sl = slots.rearrange("p (b e c) -> p b e c", e=E, b=B)
            hid = hidden.rearrange("p (i f n) -> p i f n", i=2, f=CH1)

            def weights_of(e):
                w = ring[e % depth]
                up = w[:, 0:nw * HID1].rearrange("p (i n) -> p i n", i=nw)
                down = w[:, nw * HID1:nw * HID1 + CH1 * D].rearrange("p (f n) -> p f n", f=CH1)
                bias = w[:, nw * HID1 + CH1 * D:]
                return up, down, [bias[:, CH1 * i:CH1 * i + CH1] for i in range(nw)], bias[:, CH1 * nw:CH1 * nw + 1]

            def sync(sp):
                for e in range(E):
                    if e >= depth:
                        sp.wait_ge(s_("y"), past(tag, "slotted_y") + (B // nb) * (e - depth + 1))
                    elif e == 2:
                        sp.wait_ge(s_("taken"), past(tag, "slotted_taken") + 1)
                    sp.dma_start(ring[e % depth], dram[tag + "_experts"][e, :, :]).then_inc(s_(f"ring{e % depth}"), 16)

            def positions_tensor(pe):
                pe.wait_ge(s_("taken"), past(tag, "slotted_taken") + 1)
                TE.matmul(bank(6)[:, 0:B * E], field["consts", "before"], taken, start=True,
                          stop=True).then_inc(s_("before_mm"), 1)

            def tensor(pe):
                for b in range(B):
                    pe.wait_ge(s_("onehot"), past(tag, "slotted_onehot") + b // QUAD + 1)
                    if b >= 4:
                        pe.wait_ge(s_("slots"), past(tag, "slotted_slots") + b - 3)
                    TE.matmul(bank(b % 4)[:, 0:per], xn[:, b, :], hot[:, b, :, :], start=True,
                              stop=True).then_inc(s_("slots_mm"), 1)
                    if left_over and b == B - 1:
                        pe.wait_ge(sem("rest_any"), spent("rest_any") + 1)
                        TE.matmul(bank(6)[:, 256:257], field["consts", "ones"], any_left, start=True,
                                  stop=True).then_inc(sem("rest_any_mm"), 1)
                pe.wait_ge(s_("slots"), past(tag, "slotted_slots") + B)

                def down(u):
                    e, b0 = units[u]
                    pe.wait_ge(s_("hidden"), past(tag, "slotted_hidden") + CH1 * (u + 1))
                    if u >= 2:
                        pe.wait_ge(s_("y"), past(tag, "slotted_y") + u - 1)
                    for f in range(CH1):
                        last = TE.matmul(bank(4 + u % 2)[:, 0:cols], weights_of(e)[1][:, f, :], hid[:, u % 2, f, :],
                                         start=(f == 0), stop=(f == CH1 - 1))
                    last.then_inc(s_("down_mm"), 1)
                for u, (e, b0) in enumerate(units):
                    if b0 == 0:
                        pe.wait_ge(s_(f"ring{e % depth}"), past(tag, f"slotted_ring{e % depth}") + 16 * (e // depth + 1))
                    for f in range(CH1):
                        k = CH1 * u + f
                        if k >= 2:
                            pe.wait_ge(s_("hidden"), past(tag, "slotted_hidden") + k - 1)
                        for i in range(nw):
                            last = TE.matmul(bank(2 * i + k % 2)[:, 0:cols], weights_of(e)[0][:, i, P * f:P * f + P],
                                             sl[:, b0:b0 + nb, e, :], start=True, stop=True)
                            if gated and i == 0:
                                last.then_inc(s_("gate_mm"), 1)
                        last.then_inc(s_("up_mm"), 1)
                    if u:
                        down(u - 1)
                down(len(units) - 1)
                pe.wait_ge(s_("weighted"), past(tag, "slotted_weighted") + 1)
                pe.wait_ge(s_("y"), past(tag, "slotted_y") + len(units))

                def turn(b):
                    if b >= 2:
                        pe.wait_ge(s_("turned_w"), past(tag, "slotted_turned_w") + b - 1)
                        pe.wait_ge(s_("turned_y"), past(tag, "slotted_turned_y") + b - 1)
                    for j in range(parts):
                        last = TE.transpose(bank4(b % 2)[0:part, j, :], hot[:, b, of * j:of * j + of, :], ident)
                    last.then_inc(s_("turn_w"), 1)
                    for j in range(parts):
                        last = TE.transpose(bank4(2 + b % 2)[0:part, j, :], sl[:, b, of * j:of * j + of, :], ident)
                    last.then_inc(s_("turn_y"), 1)
                turn(0)
                for b in range(B):
                    if b + 1 < B:
                        turn(b + 1)
                    pe.wait_ge(s_("turned_w"), past(tag, "slotted_turned_w") + b + 1)
                    pe.wait_ge(s_("turned_y"), past(tag, "slotted_turned_y") + b + 1)
                    for j in range(parts):
                        last = TE.matmul(bank4(4 + b // QUAD)[:, b % QUAD, :], turned_w[0:rows, b % 2, j, :],
                                         turned_y[0:rows, b % 2, j, :], start=(j == 0), stop=(j == parts - 1))
                    last.then_inc(s_("combined"), 1)

            def scalar(a):
                for b in range(B):
                    a.wait_ge(s_("slots_mm"), past(tag, "slotted_slots_mm") + b + 1)
                    src = bank(b % 4)[:, 0:per].rearrange("p (e c) -> p e c", e=E)
                    if channel_scale is None:
                        last = S.copy(sl[:, b, :, :], src)
                    else:
                        last = S.activation(sl[:, b, :, :], src, ACT.Identity, scale=channel_scale)
                    last.then_inc(s_("slots"), 1)

                for u, (e, b0) in enumerate(units):
                    for f in range(CH1):
                        k = CH1 * u + f
                        if gated:
                            a.wait_ge(s_("gate_mm"), past(tag, "slotted_gate_mm") + k + 1)
                            if k >= 2:
                                a.wait_ge(s_("hidden"), past(tag, "slotted_hidden") + k - 1)
                            S.activation(silu[:, k % 2, 0:cols], bank(k % 2)[:, 0:cols], ACT.Silu,
                                         bias=weights_of(e)[2][0][:, f:f + 1]).then_inc(s_("silu"), 1)
                        else:
                            a.wait_ge(s_("up_mm"), past(tag, "slotted_up_mm") + k + 1)
                            S.activation(hid[:, u % 2, f, :], bank(k % 2)[:, 0:cols], ACT.Relu,
                                         bias=weights_of(e)[2][0][:, f:f + 1]).then_inc(s_("hidden"), 1)
                for b in range(B):
                    a.wait_ge(s_("turn_w"), past(tag, "slotted_turn_w") + b + 1)
                    if b >= 2:
                        a.wait_ge(s_("combined"), past(tag, "slotted_combined") + b - 1)
                    S.copy(turned_w[0:part, b % 2, :, :], bank4(b % 2)[0:part, 0:parts, :]).then_inc(s_("turned_w"), 1)

            def vector(v):
                if rows > part:
                    for turned in (turned_w, turned_y):
                        link(v, V.memset(turned[64:96, :, :, :], 0.0))
                v.wait_ge(s_("before_mm"), past(tag, "slotted_before_mm") + 1)
                link(v, V.scalar_tensor_tensor(slotpos, bank(6)[:, 0:B * E], 1.0, taken, ALU.add, ALU.mult))
                link(v, V.tensor_scalar(slotpos, slotpos, -1.0, None, ALU.add))
                pos = slotpos.rearrange("p (b e) -> p b e", b=B)
                shape = [P, QUAD * E, cap]
                flat = onehot.rearrange("p (r c) -> p r c", c=cap)
                for g in range(GROUPS):
                    r = slice(QUAD * E * g, QUAD * E * (g + 1))
                    V.tensor_tensor(flat[:, r, :], spread(slotpos[:, r], 2, shape),
                                    spread(field["consts", "slot"][:, 0:cap], 1, shape), ALU.is_equal).then_inc(s_("onehot"), 1)
                if left_over:
                    left_over(v)
                for g in range(GROUPS):
                    r = slice(QUAD * E * g, QUAD * E * (g + 1))
                    v.wait_ge(s_("slots_mm"), past(tag, "slotted_slots_mm") + QUAD * (g + 1))
                    last = V.tensor_tensor(flat[:, r, :], flat[:, r, :], spread(weights[:, r], 2, shape), ALU.mult)
                last.then_inc(s_("weighted"), 1)

                def y(u):
                    e, b0 = units[u]
                    v.wait_ge(s_("down_mm"), past(tag, "slotted_down_mm") + u + 1)
                    V.tensor_scalar(sl[:, b0:b0 + nb, e, :], bank(4 + u % 2)[:, 0:cols].rearrange("p (b c) -> p b c", b=nb),
                                    weights_of(e)[3], None, ALU.add).then_inc(s_("y"), 1)
                for u, (e, b0) in enumerate(units):
                    if gated:
                        for f in range(CH1):
                            k = CH1 * u + f
                            if u >= 2 and f == 0:
                                v.wait_ge(s_("down_mm"), past(tag, "slotted_down_mm") + u - 1)
                            v.wait_ge(s_("silu"), past(tag, "slotted_silu") + k + 1)
                            v.wait_ge(s_("up_mm"), past(tag, "slotted_up_mm") + k + 1)
                            V.scalar_tensor_tensor(hid[:, u % 2, f, :], bank(2 + k % 2)[:, 0:cols], weights_of(e)[2][1][:, f:f + 1],
                                                   silu[:, k % 2, 0:cols], ALU.add, ALU.mult).then_inc(s_("hidden"), 1)
                    if u:
                        y(u - 1)
                y(len(units) - 1)
                for b in range(B):
                    v.wait_ge(s_("turn_y"), past(tag, "slotted_turn_y") + b + 1)
                    if b >= 2:
                        v.wait_ge(s_("combined"), past(tag, "slotted_combined") + b - 1)
                    V.tensor_copy(turned_y[0:part, b % 2, :, :], bank4(2 + b % 2)[0:part, 0:parts, :]).then_inc(s_("turned_y"), 1)
                for g in range(GROUPS):
                    v.wait_ge(s_("combined"), past(tag, "slotted_combined") + QUAD * (g + 1))
                    q = slice(QUAD * g, QUAD * g + QUAD)
                    V.tensor_tensor(x[:, q, :], bank4(4 + g), x[:, q, :], ALU.add).then_inc(s_("added"), 1)
            return sync, positions_tensor, tensor, scalar, vector

        def l1_experts():
            ta, tb = carve(arena_a), carve(arena_b)
            F = lambda name: field["l1f", name]
            C = lambda name: field["consts", name]
            hidden = ta(2 * CH1 * (B // 2) * CAP1)
            silu = ta(2 * (B // 2) * CAP1, "p (i n) -> p i n", i=2)
            ring = ta(2 * RING1, "p (i n) -> p i n", i=2)
            onehot = tb(B * E * CAP1)
            slots = tb(B * E * CAP1)
            score = tb(B * E, "p (b e) -> p b e", b=B)
            left = tb(B * E, "p (b e) -> p b e", b=B)
            chosen = tb(B * 2 * E, "p (b k e) -> p b k e", b=B, k=2)
            tmp = tb(B * 2 * E, "p (b k e) -> p b k e", b=B, k=2)
            best = tb(B)
            weight = tb(B * 2, "p (b k) -> p b k", b=B)
            second = tb(B)
            taken = tb(B * E)
            slotpos = tb(B * E)
            weights = tb(B * E)
            excess = tb(B * E)
            any_left = tb(1)
            flag = tb(1).bitcast(I32)
            column = tb(B)
            turned_w = hidden[:, 0:1024].rearrange("p (i j n) -> p i j n", i=2, j=4)
            turned_y = hidden[:, 1024:2048].rearrange("p (i j n) -> p i j n", i=2, j=4)
            dense_h = hidden[:, 0:CH1 * 512].rearrange("p (f n) -> p f n", f=CH1)
            dense_y = slots[:, 0:512]
            dense_silu = slots[:, 512:1024]
            n = norm("l1", rms=F("lnw"))
            logits, route, turn_logits, copy_logits = router("l1", F("Wg"), hidden[:, 0:512], "l1_logits")
            sync, positions, tensor_, scalar_, vector_ = slotted(
                "l1", CAP1, B // 2, True, onehot, slots, hidden, silu, [ring[:, 0, :], ring[:, 1, :]], turned_w, turned_y, taken, slotpos, weights,
                F("lnw"), lambda v: left_over(v), any_left)

            def left_over(v):
                link(v, V.tensor_scalar(excess, slotpos, float(CAP1), None, ALU.is_ge))
                V.tensor_reduce(any_left, excess, AX.X, ALU.max).then_inc(sem("rest_any"), 1)
                link(v, V.tensor_tensor(excess, excess, weights, ALU.mult))
                v.wait_ge(sem("rest_any_mm"), spent("rest_any_mm") + 1)
                V.tensor_scalar(flag, bank(6)[:, 256:257], 0.0, None, ALU.is_gt).then_inc(sem("rest_flag"), 1)

            def tensor(pe):
                n[2](pe)
                pe.wait_ge(sem("load_l1f"), 16)
                route(pe)
                turn_logits(pe)
                positions(pe)
                tensor_(pe)
                with second_pass(pe):
                    with pe.Fori(0, E) as e:
                        pe.wait_ge(sem("rest_weights"), spent("rest_weights") + 16 * e + 16)
                        for g in range(GROUPS):
                            unit = GROUPS * e + g
                            for f in range(CH1):
                                pe.wait_ge(sem("rest_hidden"), spent("rest_hidden") + CH1 * unit + f)
                                TE.matmul(bank(0), ring[:, 0, P * f:P * f + P], xnT[:, QUAD * g:QUAD * g + QUAD, :],
                                          start=True, stop=True).then_inc(sem("rest_gate"), 1)
                                TE.matmul(bank(1), ring[:, 0, HID1 + P * f:HID1 + P * f + P],
                                          xnT[:, QUAD * g:QUAD * g + QUAD, :], start=True, stop=True).then_inc(sem("rest_up"), 1)
                            pe.wait_ge(sem("rest_hidden"), spent("rest_hidden") + CH1 * unit + CH1)
                            pe.wait_ge(sem("rest_y"), spent("rest_y") + unit)
                            for f in range(CH1):
                                last = TE.matmul(bank(2), ring[:, 0, 2 * HID1 + D * f:2 * HID1 + D * f + D], dense_h[:, f, :],
                                                 start=(f == 0), stop=(f == CH1 - 1))
                            last.then_inc(sem("rest_down"), 1)
                            pe.wait_ge(sem("rest_y"), spent("rest_y") + unit + 1)
                            pe.wait_ge(sem("rest_added"), spent("rest_added") + unit)
                            for i in range(QUAD):
                                last = TE.transpose(bank4(3)[:, i, :], dense_y[:, T * i:T * i + T], ident)
                            last.then_inc(sem("rest_turned"), 1)

            def second_pass(eng):
                eng.wait_ge(sem("rest_flag"), spent("rest_flag") + 1)
                return eng.If(eng.value_load(flag[0:1, 0:1], min_val=0, max_val=1) > 0)

            def scalar(a):
                a.wait_ge(sem("load_l1f"), 16)
                n[3](a)
                copy_logits(a)
                a.wait_ge(sem("l1_second"), 1)
                S.activation(second, second, ACT.Exp).then_inc(sem("l1_exp"), 1)
                scalar_(a)
                with second_pass(a):
                    with a.Fori(0, E * GROUPS) as unit:
                        for f in range(CH1):
                            a.wait_ge(sem("rest_gate"), spent("rest_gate") + CH1 * unit + f + 1)
                            a.wait_ge(sem("rest_hidden"), spent("rest_hidden") + CH1 * unit + f)
                            S.activation(dense_silu, bank(0), ACT.Silu,
                                         bias=ring[:, 0, 3 * HID1 + f:3 * HID1 + f + 1]).then_inc(sem("rest_silu"), 1)

            def vector(v):
                v.sem_inc(sem("l1_start"), 1)
                n[0](v)
                by8 = [P, B, E]
                prio = spread(C("prio"), 1, by8)
                v.wait_ge(sem("l1_logits"), 1)
                link(v, V.tensor_copy(score.rearrange("p (g i) e -> p g i e", g=GROUPS), logits))
                link(v, V.tensor_tensor(score, score, spread(F("bg"), 1, by8), ALU.add))
                first_largest(v, chosen[:, :, 0, :], score, prio, best, by8)
                link(v, V.scalar_tensor_tensor(left, chosen[:, :, 0, :], -FAR, score, ALU.mult, ALU.add))
                first_largest(v, chosen[:, :, 1, :], left, prio, best, by8)
                V.tensor_tensor(taken.rearrange("p (b e) -> p b e", b=B), chosen[:, :, 0, :], chosen[:, :, 1, :],
                                ALU.add).then_inc(sem("slotted_taken"), 1)
                link(v, V.tensor_tensor(tmp, chosen, spread(score, 2, [P, B, 2, E]), ALU.mult))
                link(v, V.tensor_reduce(weight, tmp, AX.X, ALU.add))
                V.tensor_tensor(second, weight[:, :, 1], weight[:, :, 0], ALU.subtract).then_inc(sem("l1_second"), 1)
                v.wait_ge(sem("l1_exp"), 1)
                link(v, V.tensor_scalar(best, second, 1.0, None, ALU.add))
                link(v, V.reciprocal(weight[:, :, 0], best))
                link(v, V.tensor_tensor(weight[:, :, 1], second, weight[:, :, 0], ALU.mult))
                link(v, V.tensor_tensor(tmp, chosen, spread(weight, 3, [P, B, 2, E]), ALU.mult))
                link(v, V.tensor_tensor(weights.rearrange("p (b e) -> p b e", b=B), tmp[:, :, 0, :], tmp[:, :, 1, :], ALU.add))
                vector_(v)
                v.wait_ge(sem("slotted_added"), past("l1", "slotted_added") + GROUPS)
                with second_pass(v):
                    with v.Fori(0, E) as e:
                        v.wait_ge(sem("rest_added"), spent("rest_added") + GROUPS * e)
                        V.tensor_copy(column, excess.rearrange("p (b e) -> p b e", b=B)[:, :, bass.ds(e, 1)]).then_inc(sem("rest_column"), 1)
                        v.wait_ge(sem("rest_column"), spent("rest_column") + e + 1)
                        for g in range(GROUPS):
                            unit = GROUPS * e + g
                            v.wait_ge(sem("rest_down"), spent("rest_down") + unit)
                            for f in range(CH1):
                                n_ = CH1 * unit + f + 1
                                v.wait_ge(sem("rest_silu"), spent("rest_silu") + n_)
                                v.wait_ge(sem("rest_up"), spent("rest_up") + n_)
                                b1b = 3 * HID1 + CH1 + f
                                V.scalar_tensor_tensor(dense_h[:, f, :], bank(1), ring[:, 0, b1b:b1b + 1], dense_silu,
                                                       ALU.add, ALU.mult).then_inc(sem("rest_hidden"), 1)
                            v.wait_ge(sem("rest_down"), spent("rest_down") + unit + 1)
                            v.wait_ge(sem("rest_turned"), spent("rest_turned") + unit)
                            V.tensor_scalar(dense_y, bank(2), ring[:, 0, RING1 - 1:RING1], None,
                                            ALU.add).then_inc(sem("rest_y"), 1)
                            v.wait_ge(sem("rest_turned"), spent("rest_turned") + unit + 1)
                            v.wait_ge(sem("rest_added"), spent("rest_added") + unit)
                            for i in range(QUAD):
                                b = QUAD * g + i
                                last = V.scalar_tensor_tensor(x[:, b, :], bank4(3)[:, i, :], column[:, b:b + 1], x[:, b, :],
                                                              ALU.mult, ALU.add)
                            last.then_inc(sem("rest_added"), 1)
                    v.wait_ge(sem("rest_added"), spent("rest_added") + E * GROUPS)
                starting(v, "l2x")
                for g in range(GROUPS if "l2x" in measures else 0):
                    measures["l2x"](v, g)

            def start_sync(sp):
                sp.wait_ge(sem("l1_start"), 1)
                sync(sp)
                sp.wait_ge(sem("slotted_combined"), past("l1", "slotted_combined") + B)
                with second_pass(sp):
                    with sp.Fori(0, E) as e:
                        sp.wait_ge(sem("rest_added"), spent("rest_added") + GROUPS * e)
                        sp.dma_start(ring[:, 0, :], dram["l1_experts"][bass.ds(e, 1), :, :].rearrange("e p n -> (e p) n")
                                     ).then_inc(sem("rest_weights"), 16)
            return vector, n[1], tensor, scalar, start_sync

        def l2_experts():
            ta, tb = carve(arena_a), carve(arena_b)
            F = lambda name: field["l2", name]
            C = lambda name: field["consts", name]
            H = HID2
            NM = M2 // P
            gather = ta(B * M2, "p (b m) -> p b m", b=B)
            scatter = ta(NM * B * T, "p (i b l) -> p i b l", i=NM, b=B)
            both = tb(B * 2 * H, "p (b i h) -> p b i h", b=B, i=2)
            zs = tb(B * H, "p (b h) -> p b h", b=B)
            zsT = tb(B // 2 * T, "p (u l) -> p u l", u=B // 2)
            shared = tb(B * D, "p (b d) -> p b d", b=B)
            sel = tb(2 * NM * E * H, "p (w i e h) -> p w i e h", w=2, i=NM, e=E)
            zm = tb(NM * E * H, "p (i e h) -> p i e h", i=NM, e=E)
            zmT = tb(NM * 4 * P, "p (i j m) -> p i j m", i=NM, j=4)
            rowsT = tb(M2)
            value = tb(NM * (D + 1), "p (i d) -> p i d", i=NM)
            keepmore = tb(B)
            st = tb(2 * B * 6, "p (w b c) -> p w b c", w=2, b=B)
            mv = tb(2 * B * 2, "p (w b c) -> p w b c", w=2, b=B)
            ve = tb(2 * B, "p (w b) -> p w b", w=2)
            rs = tb(2 * B, "p (w b) -> p w b", w=2)
            gate = tb(NM * (E + 1), "p (i e) -> p i e", i=NM)
            score = tb(NM * E, "p (i e) -> p i e", i=NM)
            onehot = tb(NM * E, "p (i e) -> p i e", i=NM)
            picked = tb(NM * E, "p (i e) -> p i e", i=NM)
            best = tb(NM)
            two = tb(NM * 2, "p (i w) -> p i w", i=NM)
            onehotT = tb(NM * P, "p (i m) -> p i m", i=NM)
            update = both.rearrange("p b i h -> p b (i h)")
            n = norm("l2f")
            s_ = lambda what: sem("l2f_" + what)

            def index_ahead(v):
                tc = carve(arena_b, 13312)
                idx = tc(2 * (M2 + NM), "p (w n) -> p w n", w=2)
                inside = tc(2 * (M2 + NM), "p (w n) -> p w n", w=2)
                same = tc(M2)
                at = row_at[:, :]
                v.wait_ge(sem("load_index"), 16)
                link(v, V.tensor_copy(idx, index_sb[:, :, :]))
                for w, size in enumerate((B, T)):
                    link(v, V.tensor_scalar(inside[:, w, :], idx[:, w, :], 0.0, float(size), ALU.is_lt, ALU.mult))
                link(v, V.tensor_tensor(idx, idx, inside, ALU.add))
                for w, size in enumerate((B, T)):
                    link(v, V.tensor_scalar(inside[:, w, :], idx[:, w, :], 0.0, float(size - 1), ALU.max, ALU.min))
                link(v, V.tensor_tensor(inside, inside, idx, ALU.is_equal))
                link(v, V.tensor_tensor(inside[:, 0, :], inside[:, 0, :], inside[:, 1, :], ALU.mult))
                link(v, V.scalar_tensor_tensor(at, idx[:, 0, :], float(T), idx[:, 1, :], ALU.mult, ALU.add))
                link(v, V.scalar_tensor_tensor(at, at, 1.0, inside[:, 0, :], ALU.add, ALU.mult))
                link(v, V.tensor_scalar(at, at, -1.0, None, ALU.add))
                v.wait_ge(sem("load_consts"), 16)
                for i in range(NM):
                    link(v, V.scalar_tensor_tensor(same, at[:, 0:M2], at[:, M2 + i:M2 + i + 1],
                                                   C("earlier")[:, M2 * i:M2 * i + M2], ALU.is_equal, ALU.mult))
                    link(v, V.tensor_reduce(row_first[:, i:i + 1], same, AX.X, ALU.max))
                link(v, V.tensor_scalar(row_first[:, :], row_first[:, :], -1.0, 1.0, ALU.mult, ALU.add))
                v.sem_inc(s_("index"), 1)

            def gather_ahead(v):
                V.tensor_tensor(gather, spread(C("token"), 2, [P, B, M2]), spread(row_at[:, 0:M2], 1, [P, B, M2]),
                                ALU.is_equal).then_inc(s_("gather"), 1)

            def scatter_ahead(p):
                p.wait_ge(s_("index"), 1)
                p.wait_ge(sem("attn_start"), 2)
                for i in range(NM):
                    nc.gpsimd.tensor_scalar(scatter[:, i, :, :], C("tokenrow").rearrange("p (b l) -> p b l", b=B),
                                            row_at[:, M2 + i:M2 + i + 1], None, ALU.is_equal).then_inc(s_("scatter"), 1)
            ahead["index"], ahead["gather"], ahead["scatter"] = index_ahead, gather_ahead, scatter_ahead

            def tensor(pe):
                n[2](pe)
                pe.wait_ge(sem("load_l2"), 16)
                for g in range(GROUPS):
                    pe.wait_ge(sem("norm_xnT"), past("l2f", "norm_xnT") + g + 1)
                    for i in range(QUAD):
                        last = TE.matmul(bank4(4 + g)[:, i, :], xnT[:, QUAD * g + i, :], F("sw12T"), start=True, stop=True)
                    last.then_inc(s_("both_mm"), 1)
                pe.wait_ge(s_("gather"), 1)
                for b in range(B):
                    last = TE.matmul(bank(0)[:, 0:M2], xn[:, b, :], gather[:, b, :], start=(b == 0), stop=(b == B - 1))
                last.then_inc(s_("rows_mm"), 1)
                pe.wait_ge(s_("rowsT"), 1)
                for i in range(NM):
                    last = TE.matmul(bank(1)[:, (E + 1) * i:(E + 1) * (i + 1)], rowsT[:, P * i:P * i + P], F("gateT"),
                                     start=True, stop=True)
                last.then_inc(s_("gate_mm"), 1)
                pe.wait_ge(s_("both"), GROUPS)
                for w, name in enumerate(("ew1T", "ew2T")):
                    for i in range(NM):
                        last = TE.matmul(bank(4 + 2 * w + i), rowsT[:, P * i:P * i + P], F(name), start=True, stop=True)
                    last.then_inc(s_("sel_mm"), 1)
                pe.wait_ge(s_("zs"), 1)
                for u in range(B // 2):
                    last = TE.transpose(bank4(2 + u // 4)[:, u % 4, :], zs[:, 2 * u:2 * u + 2, :], ident)
                last.then_inc(s_("zs_turned"), 1)
                pe.wait_ge(s_("zsT"), 1)
                pe.wait_ge(s_("gate"), 1)
                pe.wait_ge(s_("sel"), 2)
                for u in range(B // 2):
                    for i in range(2):
                        last = TE.matmul(bank4(4 * i + u // 4)[:, u % 4, :], zsT[H * i:H * i + H, u, :],
                                         F("sw3T")[H * i:H * i + H, :], start=True, stop=True)
                last.then_inc(s_("shared_mm"), 1)
                pe.wait_ge(s_("zm"), 1)
                for i in range(NM):
                    for j in range(4):
                        last = TE.transpose(bank4(2 + i)[:, j, :], zm[:, i, 2 * j:2 * j + 2, :], ident)
                    last.then_inc(s_("zm_turned"), 1)
                for i in range(NM):
                    last = TE.transpose(bank4(6)[0:E, i, :], onehot[:, i, :], ident)
                last.then_inc(s_("onehot_turned"), 1)
                pe.wait_ge(s_("zmT"), NM)
                pe.wait_ge(s_("onehotT"), 1)
                for i in range(NM):
                    for j in range(4):
                        TE.matmul(bank4(7)[:, i, :], zmT[:, i, j, :], F("ew3")[:, D * j:D * j + D], start=(j == 0), stop=False)
                    last = TE.matmul(bank4(7)[:, i, :], onehotT[0:E, i, :], F("eb3")[0:E, :], start=False, stop=True)
                last.then_inc(s_("expert_mm"), 1)
                pe.wait_ge(s_("scatter"), NM)
                pe.wait_ge(s_("value"), 1)
                pe.wait_ge(s_("shared"), 2)
                for b in range(B):
                    for i in range(NM):
                        last = TE.matmul(bank(b // 3)[:, (D + 1) * (b % 3):(D + 1) * (b % 3 + 1)], scatter[:, i, b, :],
                                         value[:, i, :], start=(i == 0), stop=(i == NM - 1))
                last.then_inc(s_("back"), 1)

            def gpsimd(g):
                n[1](g)
                for w in range(2):
                    g.wait_ge(s_(f"ve{w}"), 1)
                    nc.gpsimd.tensor_tensor(rs[:, w, :], ve[:, w, :], minushalf[:, :], ALU.pow).then_inc(s_(f"rs{w}"), 1)

            def scalar(a):
                n[3](a)
                for g in range(GROUPS):
                    a.wait_ge(s_("both"), g + 1)
                    q = slice(QUAD * g, QUAD * g + QUAD)
                    S.activation(both[:, q, 0, :], both[:, q, 0, :], ACT.Silu).then_inc(s_("silu"), 1)
                if "keys" in ahead:
                    a.wait_ge(sem("filled"), 2)
                    a.wait_ge(s_("rows_mm"), 1)
                    ahead["keys"](a, 0)
                a.wait_ge(s_("sel"), 1)
                S.activation(sel[:, 0, :, :, :], sel[:, 0, :, :, :], ACT.Silu).then_inc(s_("sel_silu"), 1)
                a.wait_ge(s_("gate"), 1)
                S.activation(gate, gate, ACT.Sigmoid).then_inc(s_("sigmoid"), 1)
                for i in range(NM):
                    a.wait_ge(s_("zm_turned"), i + 1)
                    S.copy(zmT[:, i, :, :], bank4(2 + i)).then_inc(s_("zmT"), 1)
                a.wait_ge(s_("two"), 1)
                S.activation(two, two, ACT.Exp).then_inc(s_("exp"), 1)
                if "keys" in ahead:
                    a.wait_ge(s_("back"), 1)
                    ahead["keys"](a, 1)

            def normed(v, w, src, dst):
                for b in range(B):
                    last = V.bn_stats(st[:, w, b, :], src[:, b, :])
                link(v, last)
                for b in range(B):
                    last = V.bn_aggr(mv[:, w, b, :], st[:, w, b, :])
                link(v, last)
                V.tensor_scalar_add(ve[:, w, :], mv[:, w, :, 1], LN_EPS).then_inc(s_(f"ve{w}"), 1)
                v.wait_ge(s_(f"rs{w}"), 1)
                for b in range(B):
                    last = V.tensor_scalar(dst[:, b, :], src[:, b, :], mv[:, w, b, 0:1], rs[:, w, b:b + 1],
                                           ALU.subtract, ALU.mult)
                return last

            def vector(v):
                n[0](v)
                v.wait_ge(sem("load_l2"), 16)
                for g in range(GROUPS):
                    q = slice(QUAD * g, QUAD * g + QUAD)
                    v.wait_ge(s_("both_mm"), g + 1)
                    V.tensor_tensor(both[:, q, :, :].rearrange("p b i h -> p b (i h)"), bank4(4 + g),
                                    spread(F("sb12"), 1, [P, QUAD, 2 * H]), ALU.add).then_inc(s_("both"), 1)
                v.wait_ge(s_("rows_mm"), 1)
                V.tensor_copy(rowsT, bank(0)[:, 0:M2]).then_inc(s_("rowsT"), 1)
                v.wait_ge(s_("silu"), GROUPS)
                link(v, V.tensor_tensor(both[:, :, 0, :], both[:, :, 0, :], both[:, :, 1, :], ALU.mult))
                normed(v, 0, both[:, :, 0, :], zs).then_inc(s_("zs"), 1)
                v.wait_ge(s_("gate_mm"), 1)
                V.tensor_tensor(gate, bank(1)[:, 0:NM * (E + 1)].rearrange("p (i e) -> p i e", i=NM),
                                spread(F("gateb"), 1, [P, NM, E + 1]), ALU.add).then_inc(s_("gate"), 1)
                for w, name in enumerate(("eb1", "eb2")):
                    v.wait_ge(s_("sel_mm"), w + 1)
                    last = V.tensor_tensor(sel[:, w, :, :, :].rearrange("p i e h -> p i (e h)"), ps[:, 4 + 2 * w:6 + 2 * w, :],
                                           spread(F(name), 1, [P, NM, E * H]), ALU.add)
                    last.then_inc(s_("sel"), 1)
                v.wait_ge(s_("zs_turned"), 1)
                V.tensor_scalar(zsT, ps[:, 2:4, :].rearrange("p j (u l) -> p (j u) l", u=4), F("slng"), F("slnb"),
                                ALU.mult, ALU.add).then_inc(s_("zsT"), 1)
                v.wait_ge(s_("sel_silu"), 1)
                v.wait_ge(s_("sel"), 2)
                link(v, V.tensor_tensor(sel[:, 0, :, :, :], sel[:, 0, :, :, :], sel[:, 1, :, :, :], ALU.mult))
                rows16 = lambda ap: ap.rearrange("p i e h -> p (i e) h")
                link(v, normed(v, 1, rows16(sel[:, 0, :, :, :]), rows16(zm)))
                by = [P, NM, E]
                v.wait_ge(s_("sigmoid"), 1)
                link(v, V.tensor_tensor(score, gate[:, :, 1:E + 1], spread(F("expbias"), 1, by), ALU.add))
                first_largest(v, onehot, score, spread(C("prio"), 1, by), best, by)
                v.sem_inc(s_("onehot"), 1)
                link(v, V.tensor_tensor(picked, onehot, gate[:, :, 1:E + 1], ALU.mult))
                link(v, V.tensor_reduce(two[:, :, 1], picked, AX.X, ALU.add))
                link(v, V.tensor_copy(two[:, :, 0], gate[:, :, 0]))
                link(v, V.tensor_reduce(best, two, AX.X, ALU.max))
                V.tensor_tensor(two, two, spread(best, 2, [P, NM, 2]), ALU.subtract).then_inc(s_("two"), 1)
                full = [P, NM * E, H]
                link(v, V.tensor_tensor(rows16(zm), rows16(zm), spread(F("sellng"), 1, full), ALU.mult))
                link(v, V.tensor_tensor(rows16(zm), rows16(zm), spread(F("sellnb"), 1, full), ALU.add))
                V.tensor_tensor(rows16(zm), rows16(zm), spread(onehot.rearrange("p i e -> p (i e)"), 2, full),
                                ALU.mult).then_inc(s_("zm"), 1)
                v.wait_ge(s_("shared_mm"), 1)
                sh = shared.rearrange("p (u i) d -> p u i d", i=2)
                for i in range(2):
                    V.tensor_tensor(sh[:, :, i, :], ps[:, 4 * i:4 * i + 2, :].rearrange("p j (u d) -> p (j u) d", u=4),
                                    spread(F("sb3"), 1, [P, B // 2, D]), ALU.add).then_inc(s_("shared"), 1)
                v.wait_ge(s_("onehot_turned"), 1)
                V.tensor_copy(onehotT[0:E, :, :], bank4(6)[0:E, 0:NM, :]).then_inc(s_("onehotT"), 1)
                v.wait_ge(s_("exp"), 1)
                link(v, V.tensor_reduce(best, two, AX.X, ALU.add))
                link(v, V.reciprocal(best, best))
                link(v, V.tensor_tensor(two, two, spread(best, 2, [P, NM, 2]), ALU.mult))
                link(v, V.tensor_scalar(two[:, :, 0], two[:, :, 0], -1.0, None, ALU.add))
                link(v, V.tensor_tensor(two, two, spread(row_first[:, :], 2, [P, NM, 2]), ALU.mult))
                v.wait_ge(s_("expert_mm"), 1)
                V.tensor_copy(value[:, :, D:D + 1], two[:, :, 0:1])
                V.tensor_tensor(value[:, :, 0:D], bank4(7)[:, 0:NM, :], spread(two[:, :, 1], 2, [P, NM, D]),
                                ALU.mult).then_inc(s_("value"), 1)
                v.wait_ge(s_("back"), 1)
                back = [bank(b // 3)[:, (D + 1) * (b % 3):(D + 1) * (b % 3 + 1)] for b in range(B)]
                link(v, V.tensor_scalar(keepmore[:, 0:15].rearrange("p (j i) -> p j i", i=3), keepview(), 1.0, None, ALU.add))
                link(v, V.tensor_scalar(keepmore[:, 15:16], back[15][:, D:D + 1], 1.0, None, ALU.add))
                def weigh_shared(g):
                    for b in range(QUAD * g, QUAD * g + QUAD):
                        last = V.scalar_tensor_tensor(update[:, b, :], shared[:, b, :], keepmore[:, b:b + 1],
                                                      back[b][:, 0:D], ALU.mult, ALU.add)
                    return last
                for g in range(GROUPS):
                    q = slice(QUAD * g, QUAD * g + QUAD)
                    link(v, weigh_shared(g))
                    final(v, "l3x", g, V.tensor_tensor(x[:, q, :], x[:, q, :], update[:, q, :], ALU.add))

            def keepview():
                return ps[:, 0:5, 0:3 * (D + 1)].rearrange("p j (i d) -> p j i d", i=3)[:, :, :, D]
            return vector, gpsimd, tensor, scalar

        def l3_attention():
            ta, tb = carve(arena_a), carve(arena_b)
            F = lambda name: field["l3", name]
            C9 = HEAD + 1
            PAIR = 2
            keys = ta(2 * PAIR * HEADS * T, "p (i b u g s) -> p i b u g s", i=2, b=PAIR, u=4, g=4)
            vals = tb(B * HEADS * C9, "p (b h c) -> p b h c", b=B, h=HEADS)
            probs = tb(3 * 4 * T, "p (i g s) -> p i g s", i=3, g=4)
            probsT = tb(3 * 4 * T, "p (i g l) -> p i g l", i=3, g=4)
            weighed = tb(2 * 4 * T, "p (i u l) -> p i u l", i=2, u=4)
            neg = tb(3 * 4, "p (i g) -> p i g", i=3)
            att = tb(B * D, "p (b d) -> p b d", b=B)
            attT = tb(B * D, "p (b l) -> p b l", b=B)
            inv = tb(2 * HEADS, "p (i h) -> p i h", i=2)
            scale = 1.0 / math.sqrt(HEAD)
            n = norm("l3x")
            K = 4 * B
            s_ = lambda what: sem("l3x_" + what)

            def tensor(pe):
                n[2](pe)
                pe.wait_ge(sem("load_l3"), 16)
                pe.wait_ge(s_("values"), spent("l3x_values") + 16)

                def score(k):
                    b, u = k // 4, k % 4
                    if b % PAIR == 0 and u == 0:
                        pe.wait_ge(s_(f"keys{b // PAIR % 2}"), spent(f"l3x_keys{b // PAIR % 2}") + 16 * HEADS * (b // (2 * PAIR) + 1))
                    if k < 4:
                        pe.wait_ge(sem("norm_xnT"), past("l3x", "norm_xnT") + GROUPS)
                    if k >= 3:
                        pe.wait_ge(s_("probs"), spent("l3x_probs") + k - 2)
                    TE.matmul(bank(k % 3), xnT[:, b, :], keys[:, b // PAIR % 2, b % PAIR, u, :, :], start=True,
                              stop=True).then_inc(s_("score"), 1)

                def turn(k):
                    pe.wait_ge(s_("probs"), spent("l3x_probs") + k + 1)
                    if k >= 3:
                        pe.wait_ge(s_("probsT"), spent("l3x_probsT") + k - 2)
                    for g in range(4):
                        last = TE.transpose(bank4(3 + k % 3)[:, g, :], probs[:, k % 3, g, :], ident)
                    last.then_inc(s_("turned"), 1)

                def weigh(k):
                    b, u = k // 4, k % 4
                    pe.wait_ge(s_("probsT"), spent("l3x_probsT") + k + 1)
                    if u == 0 and b >= 2:
                        pe.wait_ge(s_("att"), spent("l3x_att") + b - 1)
                    for g in range(4):
                        last = TE.matmul(bank4(6 + b % 2)[32 * g:32 * g + C9, u, :], vals[:, b, 4 * g + u, :],
                                         probsT[:, k % 3, g, :], start=True, stop=True)
                    last.then_inc(s_("weigh"), 1)

                def turn_back(b):
                    pe.wait_ge(s_("weighed"), spent("l3x_weighed") + b + 1)
                    for u in range(4):
                        last = TE.transpose(bank4(6 + b % 2)[:, u, :], weighed[:, b % 2, u, :], ident)
                    last.then_inc(s_("back"), 1)

                pe.wait_ge(s_("cleared"), spent("l3x_cleared") + 2)
                score(0)
                score(1)
                for k in range(K):
                    if k + 2 < K:
                        score(k + 2)
                    turn(k)
                    if k:
                        weigh(k - 1)
                    if k % 4 == 2 and k >= 4:
                        turn_back(k // 4 - 1)
                weigh(K - 1)
                turn_back(B - 1)
                for g in range(GROUPS):
                    pe.wait_ge(s_("att"), spent("l3x_att") + QUAD * (g + 1))
                    for i in range(QUAD):
                        last = TE.transpose(bank4(g)[:, i, :], att[:, QUAD * g + i, :], ident)
                    last.then_inc(s_("att_turned"), 1)
                pe.wait_ge(s_("att"), spent("l3x_att") + B)
                for g in range(GROUPS):
                    pe.wait_ge(s_("attT"), spent("l3x_attT") + g + 1)
                    for i in range(QUAD):
                        last = TE.matmul(bank4(4 + g)[:, i, :], attT[:, QUAD * g + i, :], F("wprojT"), start=True, stop=True)
                    last.then_inc(s_("out"), 1)

            def scalar(a):
                n[3](a)

                def copy_out(b):
                    a.wait_ge(s_("weigh"), spent("l3x_weigh") + 4 * (b + 1))
                    if b >= 2:
                        a.wait_ge(s_("back"), spent("l3x_back") + b - 1)
                    S.copy(weighed[:, b % 2, :, :], bank4(6 + b % 2)).then_inc(s_("weighed"), 1)
                for k in range(K):
                    a.wait_ge(s_("largest"), spent("l3x_largest") + k + 1)
                    if k >= 3:
                        a.wait_ge(s_("turned"), spent("l3x_turned") + k - 2)
                    for g in range(4):
                        last = S.activation(probs[:, k % 3, g, :], bank4(k % 3)[:, g, :], ACT.Exp,
                                            bias=neg[:, k % 3, g:g + 1], scale=scale)
                    last.then_inc(s_("probs"), 1)
                    if k % 4 == 2 and k >= 4:
                        copy_out(k // 4 - 1)
                copy_out(B - 1)
                for g in range(GROUPS):
                    a.wait_ge(s_("att_turned"), spent("l3x_att_turned") + g + 1)
                    S.copy(attT[:, QUAD * g:QUAD * g + QUAD, :], bank4(g)).then_inc(s_("attT"), 1)

            def vector(v):
                v.sem_inc(s_("cleared"), 1)
                n[0](v)
                V.memset(ps[:, 6:8, :], 0.0).then_inc(s_("cleared"), 1)
                v.wait_ge(sem("load_l3"), 16)

                def largest(k):
                    v.wait_ge(s_("score"), spent("l3x_score") + k + 1)
                    if k >= 3:
                        v.wait_ge(s_("probs"), spent("l3x_probs") + k - 2)
                    link(v, V.tensor_reduce(neg[:, k % 3, :], bank4(k % 3), AX.X, ALU.max))
                    V.tensor_scalar(neg[:, k % 3, :], neg[:, k % 3, :], -scale, None, ALU.mult).then_inc(s_("largest"), 1)

                def copy_turned(k):
                    v.wait_ge(s_("turned"), spent("l3x_turned") + k + 1)
                    if k >= 3:
                        v.wait_ge(s_("weigh"), spent("l3x_weigh") + k - 2)
                    V.tensor_copy(probsT[:, k % 3, :, :], bank4(3 + k % 3)).then_inc(s_("probsT"), 1)

                def divide(b):
                    v.wait_ge(s_("back"), spent("l3x_back") + b + 1)
                    back = bank(6 + b % 2).rearrange("p (u g c) -> p g u c", u=4, g=4)
                    link(v, V.reciprocal(inv[:, b % 2, :].rearrange("p (g u) -> p g u", g=4), back[:, :, :, HEAD]))
                    V.tensor_tensor(att[:, b, :].rearrange("p (g u c) -> p g u c", g=4, u=4), back[:, :, :, 0:HEAD],
                                    spread(inv[:, b % 2, :].rearrange("p (g u) -> p g u", g=4), 3, [P, 4, 4, HEAD]),
                                    ALU.mult).then_inc(s_("att"), 1)
                largest(0)
                largest(1)
                for k in range(K):
                    if k + 2 < K:
                        largest(k + 2)
                    copy_turned(k)
                    if k % 4 == 3 and k >= 4:
                        divide(k // 4 - 1)
                divide(B - 1)
                for g in range(GROUPS):
                    q = slice(QUAD * g, QUAD * g + QUAD)
                    last = V.tensor_tensor(x[:, q, :], x[:, q, :], spread(F("bproj"), 1, [P, QUAD, D]), ALU.add)
                link(v, last)
                for g in range(GROUPS):
                    q = slice(QUAD * g, QUAD * g + QUAD)
                    v.wait_ge(s_("out"), spent("l3x_out") + g + 1)
                    final(v, "l3", g, V.tensor_tensor(x[:, q, :], bank4(4 + g), x[:, q, :], ALU.add))

            def clear_keys(a, half):
                flat = keys.rearrange("p i b u g s -> p i (b u g s)")[:, half, :]
                for i in range(2):
                    n_ = PAIR * HEADS * T // 2
                    S.activation(flat[:, n_ * i:n_ * i + n_], zero[:, 0:1].to_broadcast([P, n_]),
                                 ACT.Copy).then_inc(s_("start"), 1)
            ahead["keys"] = clear_keys

            def load_keys(sp, r):
                for h in range(HEADS):
                    rows_ = slice(HEAD * h, HEAD * h + HEAD)
                    sp.dma_start(keys[rows_, r % 2, :, h % 4, h // 4, :],
                                 dram["ctxT"][rows_, PAIR * r:PAIR * r + PAIR, :]).then_inc(s_(f"keys{r % 2}"), 16)

            def sync(sp):
                sp.wait_ge(s_("start"), spent("l3x_start") + 2)
                load_keys(sp, 0)
                sp.wait_ge(s_("cleared"), spent("l3x_cleared") + 1)
                sp.dma_start(vals, dram["l3_values"].rearrange("p (b h c) -> p b h c", b=B, h=HEADS)).then_inc(s_("values"), 16)
                sp.wait_ge(s_("start"), spent("l3x_start") + 4)
                for r in range(1, B // PAIR):
                    if r >= 2:
                        sp.wait_ge(s_("score"), spent("l3x_score") + 4 * PAIR * (r - 1))
                    load_keys(sp, r)
            return vector, n[1], tensor, scalar, sync

        def l3_experts():
            ta, tb = carve(arena_a), carve(arena_b)
            F = lambda name: field["l3", name]
            C = lambda name: field["consts", name]
            hidden = ta(2 * CH3 * B * CAP)
            ring3 = HID3 + CH3 * D + CH3 + 1
            ring = [ta(ring3) for _ in range(2)]
            onehot = ta(B * E * CAP)
            slots = tb(B * E * CAP)
            route1 = tb(2 * CH3 * 512, "p (i f n) -> p i f n", i=2, f=CH3)
            route2 = tb(2 * CH3 * 512, "p (i f n) -> p i f n", i=2, f=CH3)
            ring += [route1.rearrange("p i f n -> p (i f n)")[:, ring3 * i:ring3 * i + ring3] for i in range(2)]
            score = tb(B * E, "p (b e) -> p b e", b=B)
            left = tb(B * E, "p (b e) -> p b e", b=B)
            chosen = tb(B * 2 * E, "p (b k e) -> p b k e", b=B, k=2)
            best = tb(B)
            taken = tb(B * E)
            slotpos = tb(B * E)
            weights = tb(B * E)
            turned_w = tb(4 * T, "p (i j n) -> p i j n", i=2, j=2)
            turned_y = tb(4 * D, "p (i j n) -> p i j n", i=2, j=2)
            route3 = tb(2 * 512, "p (i n) -> p i n", i=2)
            n = norm("l3")
            s_ = lambda what: sem("l3f_" + what)
            sync, positions, tensor_, scalar_, vector_ = slotted(
                "l3", CAP, B, False, onehot, slots, hidden, None, ring, turned_w, turned_y, taken, slotpos, weights,
                None)

            def tensor(pe):
                n[2](pe)

                def first(g):
                    pe.wait_ge(sem("norm_xnT"), past("l3", "norm_xnT") + g + 1)
                    for f in range(CH3):
                        k = CH3 * g + f
                        if k >= 2:
                            pe.wait_ge(s_("route1"), spent("l3f_route1") + k - 1)
                        TE.matmul(bank(4 + k % 2), F("rW1")[:, P * f:P * f + P], xnT[:, QUAD * g:QUAD * g + QUAD, :],
                                  start=True, stop=True).then_inc(s_("first"), 1)

                def third(g):
                    pe.wait_ge(s_("route2"), spent("l3f_route2") + CH3 * (g + 1))
                    if g >= 2:
                        pe.wait_ge(s_("route3"), spent("l3f_route3") + g - 1)
                    for f in range(CH3):
                        last = TE.matmul(bank(2 + g % 2)[TILE * f:TILE * f + TILE, :], F("rW3")[:, TILE * f:TILE * f + TILE],
                                         route2[:, g % 2, f, :], start=True, stop=True)
                    last.then_inc(s_("third"), 1)

                def turn_third(g):
                    pe.wait_ge(s_("route3"), spent("l3f_route3") + g + 1)
                    if g >= 2:
                        pe.wait_ge(s_("summed"), spent("l3f_summed") + g - 1)
                    for i in range(QUAD):
                        last = TE.transpose(bank4(6 + g % 2)[:, i, :], route3[:, g % 2, T * i:T * i + T], ident)
                    last.then_inc(s_("third_turned"), 1)
                first(0)
                for g in range(GROUPS):
                    if g + 1 < GROUPS:
                        first(g + 1)
                    pe.wait_ge(s_("route1"), spent("l3f_route1") + CH3 * (g + 1))
                    for o in range(CH3):
                        k = CH3 * g + o
                        if k >= 2:
                            pe.wait_ge(s_("route2"), spent("l3f_route2") + k - 1)
                        else:
                            pe.wait_ge(sem("norm_xnT"), past("l3", "norm_xnT") + k + 1)
                        for f in range(CH3):
                            last = TE.matmul(bank(k % 2), F("rW2")[:, HID3 * f + P * o:HID3 * f + P * o + P],
                                             route1[:, g % 2, f, :], start=(f == 0), stop=(f == CH3 - 1))
                        last.then_inc(s_("second"), 1)
                    if g >= 2:
                        turn_third(g - 2)
                    if g:
                        third(g - 1)
                turn_third(GROUPS - 2)
                third(GROUPS - 1)
                turn_third(GROUPS - 1)
                positions(pe)
                tensor_(pe)

            def scalar(a):
                n[3](a)

                def relu2(g):
                    for o in range(CH3):
                        a.wait_ge(s_("second"), spent("l3f_second") + CH3 * g + o + 1)
                        if g >= 2 and o == 0:
                            a.wait_ge(s_("third"), spent("l3f_third") + g - 1)
                        S.activation(route2[:, g % 2, o, :], bank((CH3 * g + o) % 2), ACT.Relu,
                                     bias=F("rb2")[:, o:o + 1]).then_inc(s_("route2"), 1)

                def copy3(g):
                    a.wait_ge(s_("third"), spent("l3f_third") + g + 1)
                    if g >= 2:
                        a.wait_ge(s_("third_turned"), spent("l3f_third_turned") + g - 1)
                    S.copy(route3[:, g % 2, :], bank(2 + g % 2)).then_inc(s_("route3"), 1)
                for g in range(GROUPS):
                    relu2(g)
                    if g:
                        copy3(g - 1)
                copy3(GROUPS - 1)
                a.wait_ge(s_("centred"), spent("l3f_centred") + 1)
                S.activation(score, score, ACT.Exp).then_inc(s_("exp"), 1)
                scalar_(a)

            def vector(v):
                v.sem_inc(s_("start"), 1)
                n[0](v)

                def sum_third(g):
                    v.wait_ge(s_("third_turned"), spent("l3f_third_turned") + g + 1)
                    chunks = bank(6 + g % 2).rearrange("p (i f e) -> p i e f", i=QUAD, f=CH3)[:, :, 0:E, :]
                    V.tensor_reduce(score[:, QUAD * g:QUAD * g + QUAD, :], chunks, AX.X, ALU.add).then_inc(s_("summed"), 1)
                for g in range(GROUPS):
                    for f in range(CH3):
                        k = CH3 * g + f
                        v.wait_ge(s_("first"), spent("l3f_first") + k + 1)
                        if g >= 2 and f == 0:
                            v.wait_ge(s_("second"), spent("l3f_second") + CH3 * (g - 1))
                        V.tensor_scalar(route1[:, g % 2, f, :], bank(4 + k % 2), F("rb1")[:, f:f + 1], 0.0, ALU.add,
                                        ALU.max).then_inc(s_("route1"), 1)
                    if g >= 3:
                        sum_third(g - 3)
                for g in range(GROUPS - 3, GROUPS):
                    sum_third(g)
                v.wait_ge(s_("summed"), spent("l3f_summed") + GROUPS)
                by8 = [P, B, E]
                prio = spread(C("prio"), 1, by8)
                link(v, V.tensor_tensor(score, score, spread(F("rb3"), 1, by8), ALU.add))
                link(v, V.tensor_reduce(best, score, AX.X, ALU.max))
                V.tensor_tensor(score, score, spread(best, 2, by8), ALU.subtract).then_inc(s_("centred"), 1)
                v.wait_ge(s_("exp"), spent("l3f_exp") + 1)
                link(v, V.tensor_reduce(best, score, AX.X, ALU.add))
                link(v, V.reciprocal(best, best))
                link(v, V.tensor_tensor(score, score, spread(best, 2, by8), ALU.mult))
                first_largest(v, chosen[:, :, 0, :], score, prio, best, by8)
                link(v, V.scalar_tensor_tensor(left, chosen[:, :, 0, :], -FAR, score, ALU.mult, ALU.add))
                first_largest(v, chosen[:, :, 1, :], left, prio, best, by8)
                by = lambda ap: ap.rearrange("p (b e) -> p b e", b=B)
                link(v, V.tensor_tensor(by(taken), chosen[:, :, 0, :], chosen[:, :, 1, :], ALU.add))
                v.sem_inc(sem("slotted_taken"), 1)
                link(v, V.tensor_tensor(by(weights), by(taken), score, ALU.mult))
                vector_(v)

            def start_sync(sp):
                sp.wait_ge(s_("start"), spent("l3f_start") + 1)
                sync(sp)
            return vector, n[1], tensor, scalar, start_sync

        phases = [l0_attention, l0_experts,
                  lambda: attention("l1x", "l1x", "Wq", "Wk", "Wv", "bq", "bk", "bv"), l1_experts,
                  lambda: attention("l2x", "l2", "WqT", "WqT", "WqT", causal=True),
                  l2_experts, l3_attention, l3_experts]
        phases = [p() for p in phases[:upto] if p]

        block = f.enter_context(nc.Block())

        @block.sync
        def _(sp):
            sp.dma_start(packed["fourier"][:, :], dram["fourier"]).then_inc(sem("load_fourier"), 16)
            sp.dma_start(ctx_tok[:, :, :], dram["ctx"].rearrange("b l d -> l b d")).then_inc(sem("load_ctx"), 16)
            sp.dma_start(ctxT[:, :, :], dram["ctxT"]).then_inc(sem("load_ctx"), 16)
            for pack in ("l0f", "l1x", "l1f", "l2", "l3"):
                sp.dma_start(packed[pack][:, :], dram[pack]).then_inc(sem("load_" + pack), 16)
            for p in phases:
                if len(p) > 4:
                    p[4](sp)
            full = upto == 8
            for g in range(GROUPS):
                q = slice(QUAD * g, QUAD * g + QUAD)
                if full:
                    sp.wait_ge(sem("slotted_added"), past("l3", "slotted_added") + g + 1)
                else:
                    sp.wait_ge(sem("done"), 1)
                sp.dma_start(out[q, :, :].rearrange("b l d -> l b d"), x[:, q, :]).then_inc(sem("stored"), 16)
            sp.wait_ge(sem("stored"), 16 * GROUPS)

        @block.gpsimd
        def _(g):
            nc.gpsimd.memset(minushalf[:, :], -0.5).then_inc(sem("filled"), 1)
            nc.gpsimd.memset(zero[:, :], 0.0).then_inc(sem("filled"), 1)
            g.wait_ge(sem("filled"), 2)
            for p in phases:
                p[1](g)

        @block.scalar
        def _(a):
            a.dma_start(x[:, :, :], dram["x"].rearrange("b l d -> l b d")).then_inc(sem("load_x"), 16)
            a.dma_start(index_sb[:, :, :], dram["index"].rearrange("p (w n) -> p w n", w=2)).then_inc(sem("load_index"), 16)
            a.dma_start(packed["consts"][:, :], dram["consts"]).then_inc(sem("load_consts"), 16)
            for p in phases:
                p[3](a)

        @block.vector
        def _(v):
            if "index" in ahead:
                ahead["index"](v)
            v.wait_ge(sem("load_consts"), 16)
            for p in phases:
                p[0](v)
            if upto < 8:
                v.sem_inc(sem("done"), 1)

        @block.tensor
        def _(pe):
            for p in phases:
                p[2](pe)


def fourier_constants():
    n = T
    t = np.arange(n)
    half = n // 2
    fwd1, fwd2, inv1, inv2 = (np.zeros((n, n)) for _ in range(4))
    for j in range(half + 1):
        c = np.cos(2 * np.pi * j * t / n)
        s = np.sin(2 * np.pi * j * t / n)
        w = (1.0 if j in (0, half) else 2.0) / n
        fwd1[j], inv1[j] = c, w * c
        if 0 < j < half:
            fwd1[half + j], inv1[half + j] = -s, w * c
            fwd2[j], inv2[j] = -s, w * s
            fwd2[half + j], inv2[half + j] = c, -w * s
    dft = np.concatenate([fwd1.T, fwd2.T], axis=1)
    idft = np.concatenate([inv1, inv2], axis=1)
    return dft.astype(np.float32), idft.astype(np.float32)


def constants():
    p = np.arange(P)
    e = np.arange(E)
    dft, idft = fourier_constants()
    m = np.arange(M2)

    def rows(v):
        return np.tile(np.asarray(v, np.float32).reshape(1, -1), (P, 1))
    return {
        "dft": dft, "idft": idft, "ident": np.eye(P, dtype=np.float32),
        "blockmask": (p[:, None] // HEAD == np.arange(HEADS)[None]).astype(np.float32),
        "dmod": (p[:, None] % HEAD + T).astype(np.float32),
        "iota8": rows(np.arange(HEAD)), "prio": rows(E - e), "prio4": rows(4 - np.arange(4)),
        "lower": rows((e[None, :] <= e[:, None])),
        "rownum": (2 * (np.arange(B)[None, :, None] * T + p[:, None, None]) + np.arange(2)[None, None]).reshape(P, 2 * B).astype(np.float32),
        "ones": np.ones((P, P), np.float32),
        "before": (p[:, None] < p[None, :]).astype(np.float32),
        "causal": np.where(p[None, :] <= p[:, None], 0.0, -FAR).astype(np.float32),
        "slot": rows(np.arange(CAP1)),
        "token": (np.arange(B)[None] * T + p[:, None]).astype(np.float32),
        "tokenrow": rows(np.arange(B * T)),
        "earlier": np.concatenate([(m[None] < p[:, None]), (m[None] < P + p[:, None])], axis=1).astype(np.float32),
    }


def kernel(**inputs):
    import concourse.bacc as bacc
    from concourse.bass_utils import run_bass_kernel_spmd

    i = {k: np.asarray(v) for k, v in inputs.items()}

    def rows(v):
        return np.tile(v.reshape(1, -1), (P, 1))

    def col(v):
        return v.reshape(-1, P).T

    def cols(v):
        return v.reshape(E, -1, P).transpose(0, 2, 1)

    def tall(v):
        return np.concatenate([v, np.zeros((P - v.shape[0], v.shape[1]), v.dtype)])

    def tile32(v):
        return np.concatenate([v, np.zeros(v.shape[:-1] + (TILE - v.shape[-1],), v.dtype)], axis=-1)

    def twice(v):
        return np.concatenate([v, v])

    c = constants()
    fields = {
        ("fourier", "wk"): i["L0_xattn_wk"], ("fourier", "wq"): i["L0_xattn_wq"],
        ("fourier", "wv"): i["L0_xattn_wv"], ("fourier", "wo"): i["L0_xattn_wo"],
        ("l0f", "wgateT"): tile32(i["L0_ffn_w_gate"].T),
        ("l0f", "sw1T"): i["L0_ffn_sw1"].T, ("l0f", "sw3T"): i["L0_ffn_sw3"].T, ("l0f", "sw2T"): i["L0_ffn_sw2"].T,
        ("l0f", "ebias"): rows(i["L0_ffn_expert_bias"]),
        ("l0f", "w13"): np.concatenate([i["L0_ffn_w1"], i["L0_ffn_w3"]], axis=2).transpose(1, 0, 2).reshape(P, -1),
        ("l0f", "w2"): tall(i["L0_ffn_w2"].transpose(1, 0, 2).reshape(HID0, -1)),
        ("l1x", "Wq"): i["L1_xattn_Wq"], ("l1x", "Wk"): i["L1_xattn_Wk"], ("l1x", "Wv"): i["L1_xattn_Wv"],
        ("l1x", "bq"): col(i["L1_xattn_bq"]), ("l1x", "bk"): col(i["L1_xattn_bk"]), ("l1x", "bv"): rows(i["L1_xattn_bv"]),
        ("l1f", "lnw"): col(i["L1_ffn_ln_w"]), ("l1f", "Wg"): tile32(i["L1_ffn_Wg"]), ("l1f", "bg"): rows(i["L1_ffn_bg"]),
        ("l2", "WqT"): i["L2_xattn_Wq"].T,
        ("l2", "sw12T"): np.concatenate([i["L2_ffn_sw1"].T, i["L2_ffn_sw2"].T], axis=1),
        ("l2", "sb12"): rows(np.concatenate([i["L2_ffn_sb1"], i["L2_ffn_sb2"]])),
        ("l2", "sw3T"): twice(i["L2_ffn_sw3"].T), ("l2", "sb3"): rows(i["L2_ffn_sb3"]),
        ("l2", "slng"): twice(i["L2_ffn_s_ln_g"].reshape(-1, 1)), ("l2", "slnb"): twice(i["L2_ffn_s_ln_b"].reshape(-1, 1)),
        ("l2", "gateT"): np.concatenate([i["L2_ffn_sg_w"], i["L2_ffn_eg_w"]]).T,
        ("l2", "gateb"): rows(np.concatenate([i["L2_ffn_sg_b"], i["L2_ffn_eg_b"]])),
        ("l2", "expbias"): rows(i["L2_ffn_exp_bias"]),
        ("l2", "ew1T"): i["L2_ffn_ew1"].transpose(2, 0, 1).reshape(P, -1),
        ("l2", "ew2T"): i["L2_ffn_ew2"].transpose(2, 0, 1).reshape(P, -1),
        ("l2", "eb1"): rows(i["L2_ffn_eb1"]), ("l2", "eb2"): rows(i["L2_ffn_eb2"]),
        ("l2", "ew3"): i["L2_ffn_ew3"].transpose(0, 2, 1).reshape(E // 2, P, D).transpose(1, 0, 2).reshape(P, -1),
        ("l2", "eb3"): tall(i["L2_ffn_eb3"]),
        ("l2", "sellng"): rows(i["L2_ffn_sel_ln_g"]), ("l2", "sellnb"): rows(i["L2_ffn_sel_ln_b"]),
        ("l3", "wprojT"): i["L3_xattn_w_proj"].T, ("l3", "bproj"): rows(i["L3_xattn_b_proj"]),
        ("l3", "rW1"): i["L3_ffn_rW1"], ("l3", "rb1"): col(i["L3_ffn_rb1"]),
        ("l3", "rW2"): i["L3_ffn_rW2"].reshape(CH3, P, HID3).transpose(1, 0, 2).reshape(P, -1), ("l3", "rb2"): col(i["L3_ffn_rb2"]),
        ("l3", "rW3"): tile32(i["L3_ffn_rW3"].reshape(CH3, P, E)).transpose(1, 0, 2).reshape(P, -1), ("l3", "rb3"): rows(i["L3_ffn_rb3"]),
    }
    arrays = {"x": i["x"], "ctx": i["ctx_1024"], "ctxT": i["ctx_1024"].transpose(2, 0, 1),
              "index": np.concatenate([v for w in ("b", "t") for v in (rows(i["L2_ffn_index_" + w]), col(i["L2_ffn_index_" + w]))],
                                      axis=1)}
    arrays["l1_experts"] = np.concatenate([
        i["L1_ffn_W1a"], i["L1_ffn_W1b"],
        i["L1_ffn_W2"].reshape(E, CH1, P, D).transpose(0, 2, 1, 3).reshape(E, P, -1),
        cols(i["L1_ffn_b1a"]), cols(i["L1_ffn_b1b"]), cols(i["L1_ffn_b2"])], axis=2)
    arrays["l3_experts"] = np.concatenate([
        i["L3_ffn_eW1"], i["L3_ffn_eW2"].reshape(E, CH3, P, D).transpose(0, 2, 1, 3).reshape(E, P, -1),
        cols(i["L3_ffn_eb1"]), cols(i["L3_ffn_eb2"])], axis=2)
    vals = np.ones((T, B, HEADS, HEAD + 1), i["ctx_1024"].dtype)
    vals[..., 0:HEAD] = i["ctx_1024"].reshape(B, T, HEADS, HEAD).transpose(1, 0, 2, 3)
    arrays["l3_values"] = vals.reshape(P, -1)
    for pack, names in PACKS.items():
        arrays[pack] = np.concatenate([fields.get((pack, n), c.get(n)) for n, _ in names], axis=1)

    nc = bacc.Bacc("TRN2", target_bir_lowering=False, num_devices=1)
    feeds, dram = {}, {}
    for name, a in arrays.items():
        a = np.ascontiguousarray(a)
        feeds[f"in_{name}_dram"] = a
        dram[name] = nc.dram_tensor(f"in_{name}_dram", a.shape, mybir.dt.from_np(a.dtype), kind="ExternalInput").ap()
    out = nc.dram_tensor("out_0_dram", (B, T, D), F32, kind="ExternalOutput").ap()
    build(nc, dram, out, UPTO)
    r = run_bass_kernel_spmd(nc, [feeds], core_ids=[0])
    return r.results[0]["out_0_dram"]
```

```python
import math
from contextlib import ExitStack

import numpy as np

import concourse.bass as bass
from concourse import mybir

F32 = mybir.dt.float32
I32 = mybir.dt.int32
U32 = mybir.dt.uint32
ALU = mybir.AluOpType
ACT = mybir.ActivationFunctionType
AX = mybir.AxisListType

P = 128
B = 16
D = 128
T = 128
E = 8
QUAD = 4
GROUPS = B // QUAD
LN_EPS = 1e-5
RMS_EPS = float(np.finfo(np.float32).eps)
FAR = 1e30

CORR_TOP = int(math.floor(math.log(T)))
HEAD = 8
HEADS = D // HEAD
HID0 = 64
PAIRS = E * E
HID1 = 512
CH1 = HID1 // P
CAP1 = 52
RING1 = 3 * HID1 + 2 * CH1 + 1
HID2 = 64
M2 = 256
HID3 = 512
CH3 = HID3 // P
CAP = int(T / E * 1.25)
TILE = 32
WARM = {"l0f": (2, 1, 1, 1), "l1x": (0, 1, 0, 0), "l1": (2, 1, 1, 0), "l2x": (0, 0, 0, 0), "l2f": (2, 1, 1, 1), "l3x": (2, 2, 2, 0),
        "l3": (2, 2, 2, 2), "mix": 7, "act": 2, "takenl1": 3, "takenl3": 7, "onehotl1": 3, "onehotl3": 2, "zs": 6}

PACKS = {
    "fourier": [("dft", 2 * T), ("wk", D), ("wq", D), ("idft", 2 * T), ("wv", D), ("wo", D), ("ident", P)],
    "consts": [("blockmask", HEADS), ("dmod", 1), ("iota8", HEAD), ("prio", E), ("prio4", 4), ("lower", E * E),
               ("rownum", 2 * B), ("ones", P), ("before", P), ("causal", P), ("slot", CAP1), ("token", B),
               ("tokenrow", B * T), ("earlier", 2 * M2)],
    "l0f": [("wgateT", TILE), ("sw1T", P), ("sw3T", P), ("sw2T", D), ("ebias", E), ("w13", E * 2 * HID0), ("w2", E * D)],
    "l1x": [("Wq", D), ("Wk", D), ("Wv", D), ("bq", 1), ("bk", 1), ("bv", D)],
    "l1f": [("lnw", 1), ("Wg", TILE), ("bg", E)],
    "l2": [("WqT", D), ("sw12T", 2 * HID2), ("sb12", 2 * HID2), ("sw3T", 2 * D), ("sb3", D), ("slng", 1), ("slnb", 1),
           ("gateT", E + 1), ("gateb", E + 1), ("expbias", E), ("ew1T", E * HID2), ("ew2T", E * HID2),
           ("eb12", 2 * HID2), ("ew3", E // 2 * D), ("eb3", D), ("sellng", HID2), ("sellnb", HID2)],
    "l3": [("wprojT", D), ("bproj", D), ("rb1", CH3), ("rb2", CH3), ("rW3", CH3 * TILE), ("rb3", E), ("rW1", HID3), ("rW2", CH3 * HID3)],
}


def pack_offsets(pack):
    at, out = 0, {}
    for name, n in PACKS[pack]:
        out[name] = (at, at + n)
        at += n
    return out, at


def build(nc, dram, out):
    f = ExitStack()
    with f:
        sems = {}

        resting = [("l0x_" + n, c) for n, c in (
            ("keys_mm", GROUPS), ("keys", GROUPS), ("k_mm", 2 * GROUPS), ("k", GROUPS), ("u_mm", GROUPS), ("u", GROUPS),
            ("v_mm", GROUPS), ("v", GROUPS), ("qhat_mm", GROUPS), ("qhat", GROUPS), ("q_mm", GROUPS), ("prod", GROUPS),
            ("corr_mm", GROUPS), ("diff", 1), ("exp", 1), ("mix", GROUPS), ("mix_turned", GROUPS), ("mixed", GROUPS),
            ("out_mm", GROUPS))] + [("l0f_" + n, c) for n, c in (
                ("logits", 1), ("gate", GROUPS), ("up", GROUPS), ("gated", GROUPS), ("shared", GROUPS), ("added", GROUPS),
                ("counts", 1), ("local", 1), ("picked", 1), ("pair", GROUPS), ("pair13_mm", 1), ("pair_turned", GROUPS),
                ("pairT", GROUPS), ("pair13", 1), ("pre_mm", 2), ("pre", 2), ("silu", GROUPS), ("silu2", 2), ("act", 2),
                ("sums_mm", 1), ("hidden", 1), ("hidden_turned", 1), ("hiddenT", 1), ("routed", 1), ("centred", 1))]
        heirs = ["l3x_" + n for n in ("values", "keys0", "keys1", "score", "probs", "turned", "probsT", "weigh", "weighed",
                                      "back", "att", "att_turned", "attT", "out", "cleared", "start", "largest")] + [
            "l3f_" + n for n in ("start", "first", "route1", "second", "route2", "third", "route3", "third_turned", "summed",
                                      "centred", "exp")] + [
            "rest_" + n for n in ("any", "any_mm", "flag", "weights", "gate", "up", "silu", "hidden", "down", "y", "turned",
                                  "added", "column")]
        inherits = dict(zip(heirs, resting))

        def spent(name):
            return inherits[name][1]

        def sem(name):
            if name in inherits:
                name = inherits[name][0]
            if name not in sems:
                sems[name] = f.enter_context(nc.semaphore(name))
            return sems[name]

        every = ("l0x", "l0f", "l1x", "l1", "l2x", "l2f", "l3x", "l3")
        adds = {"norm_" + what: [(tag, n) for tag in every
                                 if not (tag == "l0x" and what in ("turned", "xnT", "shift", "xn_scalar"))]
                for what, n in (("var", GROUPS), ("rstd", GROUPS), ("xn", GROUPS), ("shift", GROUPS),
                             ("xn_scalar", GROUPS), ("turned", GROUPS), ("xnT", GROUPS))}
        for what in ("start", "k_mm", "v_mm", "k", "v", "q_mm", "q", "logits", "neg", "exp", "turned2", "attnT", "out"):
            adds["attn_" + what] = [("l1x", 1 if what == "start" else GROUPS), ("l2x", 1 if what == "start" else GROUPS)]
        for what, n1, n3 in (("taken", 1, 1), ("before_mm", 1, 1), ("onehot", B // 2, B // 2), ("slots_mm", B, B),
                             ("slots", B, B), ("gate_mm", 2 * E * CH1, 0), ("silu", 2 * E * CH1, 0),
                             ("up_mm", 2 * E * CH1, E * CH3), ("hidden", 2 * E * CH1, E * CH3), ("down_mm", 2 * E, E),
                             ("y", 2 * E, E), ("weighted", E, E // 2), ("turn_w", B, B), ("turn_y", B, B), ("turned_w", B, B),
                             ("turned_y", B, B), ("combined", B, B), ("added", GROUPS, GROUPS), ("ring0", 8 * E, 4 * E), ("ring1", 8 * E, 4 * E), ("ring2", 0, 4 * E), ("ring3", 0, 4 * E)):
            adds["slotted_" + what] = [("l1", n1), ("l3", n3)]

        for what in ("mm", "copied"):
            adds["router_" + what] = [("l0f", 1), ("l1", 1)]

        def past(tag, name):
            tags = [t for t, _ in adds[name]]
            return sum(n for _, n in adds[name][:tags.index(tag)])

        def sb(name, shape, dt=F32):
            return f.enter_context(nc.sbuf_tensor(name, shape, dt))

        def spread(ap, axis, shape):
            return ap.unsqueeze(axis).to_broadcast(shape)

        ps = f.enter_context(nc.psum_tensor("ps", [P, 8, 512], F32))

        def bank(i):
            return ps[:, i, :]

        def bank4(i):
            return ps[:, i, :].rearrange("p (b c) -> p b c", b=QUAD)

        packed, field = {}, {}
        for pack in PACKS:
            offsets, width = pack_offsets(pack)
            packed[pack] = sb(f"pack_{pack}", [P, width])
            for name, (lo, hi) in offsets.items():
                field[pack, name] = packed[pack][:, lo:hi]
        x = sb("x", [P, B, D])
        xn = sb("xn", [P, B, D])
        xnT = sb("xnT", [P, B, T])
        ctx_tok = sb("ctx_tok", [P, B, D])
        ctxT = sb("ctxT", [P, B, T])
        stats = sb("stats", [P, B, 6])
        meanvar = sb("meanvar", [P, B, 2])
        vareps = sb("vareps", [P, B])
        rstd = sb("rstd", [P, B])
        shift = sb("shift", [P, B])
        minushalf = sb("minushalf", [P, B])
        row_at = sb("row_at", [P, M2 + M2 // P])
        row_first = sb("row_first", [P, M2 // P])
        zero = sb("zero", [P, 1])
        index_sb = sb("index_sb", [P, 2, M2 + M2 // P], I32)
        arena_a = sb("arena_a", [P, 8192])
        arena_b = sb("arena_b", [P, 15360])

        def carve(arena, start=0):
            at = [start]

            def take(n, pattern=None, **sizes):
                ap = arena[:, at[0]:at[0] + n]
                at[0] += n
                assert at[0] <= arena.shape[1], at[0]
                return ap.rearrange(pattern, **sizes) if pattern else ap
            return take

        ident = field["fourier", "ident"]
        chain = [0]

        def link(v, ins):
            chain[0] += 1
            ins.then_inc(sem("vector_chain"), 1)
            v.wait_ge(sem("vector_chain"), chain[0])

        V = nc.vector
        S = nc.scalar
        TE = nc.tensor

        def keep_warm(pe, n, free):
            for _ in range(n):
                TE.matmul(bank(free), ident, packed["fourier"][:, 0:512], start=True, stop=True)

        measures, starts, ahead = {}, {}, {}

        def norm(tag, order=range(GROUPS), rms=None, scale=1.0):
            order = list(order)

            applied = []
            ours = QUAD // 2 if tag != "l0x" else QUAD

            def measure(v, g, overlap=False):
                q = slice(QUAD * g, QUAD * g + QUAD)
                for b in range(QUAD * g, QUAD * g + QUAD):
                    last = V.bn_stats(stats[:, b, :], x[:, b, :])
                chain[0] += 1
                last.then_inc(sem("vector_chain"), 1)
                settled = chain[0]
                if overlap and g:
                    apply(v, g - 1)
                v.wait_ge(sem("vector_chain"), settled)
                for b in range(QUAD * g, QUAD * g + QUAD):
                    last = V.bn_aggr(meanvar[:, b, :], stats[:, b, :])
                link(v, last)
                V.tensor_scalar(vareps[:, q], meanvar[:, q, 1], 1.0 + RMS_EPS if rms else 1.0,
                                LN_EPS * (RMS_EPS if rms else 1.0), ALU.mult, ALU.add).then_inc(sem("norm_var"), 1)
            measures[tag] = measure

            def apply(v, g):
                applied.append(g)
                q = slice(QUAD * g, QUAD * g + QUAD)
                v.wait_ge(sem("norm_rstd"), past(tag, "norm_rstd") + order.index(g) + 1)
                if ours < QUAD:
                    V.scalar_tensor_tensor(shift[:, q], meanvar[:, q, 0], -1.0, rstd[:, q], ALU.mult,
                                           ALU.mult).then_inc(sem("norm_shift"), 1)
                for b in range(QUAD * g, QUAD * g + ours):
                    last = V.tensor_scalar(xn[:, b, :], x[:, b, :], meanvar[:, b, 0:1], rstd[:, b:b + 1],
                                           ALU.subtract, ALU.mult)
                last.then_inc(sem("norm_xn"), 1)

            def vector(v):
                for g in range(GROUPS):
                    if g not in applied:
                        apply(v, g)

            def gpsimd(p):
                for j, g in enumerate(order):
                    q = slice(QUAD * g, QUAD * g + QUAD)
                    p.wait_ge(sem("norm_var"), past(tag, "norm_var") + j + 1)
                    nc.gpsimd.tensor_tensor(rstd[:, q], vareps[:, q], minushalf[:, q], ALU.pow).then_inc(sem("norm_rstd"), 1)

            def tensor(pe, before_last=None, behind=None):
                for g in range(GROUPS):
                    if before_last and g == GROUPS - 1:
                        before_last()
                    keep_warm(pe, WARM[tag][g], 7 if tag == "l3x" else 3)
                    pe.wait_ge(sem("norm_xn"), past(tag, "norm_xn") + g + 1)
                    pe.wait_ge(sem("norm_xn_scalar"), past(tag, "norm_xn_scalar") + g + 1)
                    for i in range(QUAD):
                        last = TE.transpose(bank4(g)[:, i, :], xn[:, QUAD * g + i, :], ident)
                    last.then_inc(sem("norm_turned"), 1)
                    if behind and g:
                        behind(g - 1)
                if behind:
                    behind(GROUPS - 1)

            def scalar(a):
                def theirs(g):
                    a.wait_ge(sem("norm_shift"), past(tag, "norm_shift") + g + 1)
                    for b in range(QUAD * g + ours, QUAD * g + QUAD):
                        last = S.activation(xn[:, b, :], x[:, b, :], ACT.Identity, bias=shift[:, b:b + 1],
                                            scale=rstd[:, b:b + 1])
                    last.then_inc(sem("norm_xn_scalar"), 1)
                theirs(0)
                for g in range(GROUPS):
                    if g + 1 < GROUPS:
                        theirs(g + 1)
                    a.wait_ge(sem("norm_turned"), past(tag, "norm_turned") + g + 1)
                    S.activation(xnT[:, QUAD * g:QUAD * g + QUAD, :], bank4(g), ACT.Copy if not rms else ACT.Identity,
                                 scale=rms if rms else scale).then_inc(sem("norm_xnT"), 1)
            return vector, gpsimd, tensor, scalar

        def starting(v, following):
            v.sem_inc(starts[following], 1)

        def final(v, following, g, last):
            link(v, last)
            measures[following](v, g, overlap=True)

        def first_largest(v, onehot, score, prio, best, shape):
            link(v, V.tensor_reduce(best, score, AX.X, ALU.max))
            link(v, V.tensor_tensor(onehot, score, spread(best, len(shape) - 1, shape), ALU.is_equal))
            link(v, V.tensor_tensor(onehot, onehot, prio, ALU.mult))
            link(v, V.tensor_reduce(best, onehot, AX.X, ALU.max))
            link(v, V.tensor_tensor(onehot, onehot, spread(best, len(shape) - 1, shape), ALU.is_equal))

        def router(tag, weights, logitsT, done):
            logits = bank(6).rearrange("p (i g e) -> p g i e", i=QUAD, g=GROUPS)[:, :, :, 0:E]

            def route(pe, g):
                pe.wait_ge(sem("norm_xnT"), past(tag, "norm_xnT") + g + 1)
                last = TE.matmul(bank(4)[TILE * g:TILE * g + TILE, :], weights, xnT[:, QUAD * g:QUAD * g + QUAD, :],
                                 start=True, stop=True)
                if g == GROUPS - 1:
                    last.then_inc(sem("router_mm"), 1)

            def turn(pe):
                pe.wait_ge(sem("router_copied"), past(tag, "router_copied") + 1)
                for i in range(QUAD):
                    last = TE.transpose(bank4(6)[:, i, :], logitsT[:, T * i:T * i + T], ident)
                last.then_inc(sem(done), 1)

            def copy(a):
                a.wait_ge(sem("router_mm"), past(tag, "router_mm") + 1)
                S.copy(logitsT, bank(4)).then_inc(sem("router_copied"), 1)
            return logits, route, turn, copy

        def l0_attention():
            ta, tb = carve(arena_a), carve(arena_b)
            k_time = ta(B * D, "p (b d) -> p b d", b=B)
            k1 = ta(B * D, "p (b d) -> p b d", b=B)
            k2 = ta(B * D, "p (b d) -> p b d", b=B)
            q_hat = tb(B * T, "p (b f) -> p b f", b=B)
            values = tb(B * D, "p (b o) -> p b o", b=B)
            prod1 = tb(B * D, "p (b d) -> p b d", b=B)
            prod2 = tb(B * D, "p (b d) -> p b d", b=B)
            mix_T = prod1
            mix = prod2
            top = tb(B * 8, "p (b k) -> p b k", b=B)
            where = tb(B * 8, "p (b k) -> p b k", b=B).bitcast(U32)
            wsoft = tb(B * CORR_TOP, "p (b k) -> p b k", b=B)
            wsum = tb(B)
            shift = tb(B * CORR_TOP, "p (b k) -> p b k", b=B)
            shift_i = tb(B * CORR_TOP, "p (b k) -> p b k", b=B).bitcast(I32)
            hit = tb(B * CORR_TOP * HEAD, "p (b k r) -> p b k r", b=B, k=CORR_TOP)
            mix8 = tb(B * HEAD, "p (b r) -> p b r", b=B)
            F = lambda n: field["fourier", n]
            C = lambda n: field["consts", n]

            def tensor(pe):
                pe.wait_ge(sem("load_first"), 32)
                for g in range(GROUPS):
                    if g == 1:
                        pe.wait_ge(sem("load_ctxT"), 16)
                    for i in range(QUAD):
                        last = TE.matmul(bank4(g)[:, i, :], ctxT[:, QUAD * g + i, :], F("wk"), start=True, stop=True)
                    last.then_inc(sem("l0x_keys_mm"), 1)
                for h in range(2):
                    for g in range(GROUPS):
                        pe.wait_ge(sem("l0x_keys"), g + 1)
                        if h:
                            pe.wait_ge(sem("l0x_k_scalar"), g + 1)
                        TE.matmul(bank(4 + g), F("dft")[:, T * h:T * h + T], k_time[:, QUAD * g:QUAD * g + QUAD, :],
                                  start=True, stop=True).then_inc(sem("l0x_k_mm"), 1)
                pe.wait_ge(sem("load_ctx"), 16)
                pe.wait_ge(sem("load_fourier"), 16)
                for g in range(GROUPS):
                    for i in range(QUAD):
                        last = TE.matmul(bank4(g)[:, i, :], ctx_tok[:, QUAD * g + i, :], F("wo"), start=True, stop=True)
                    last.then_inc(sem("l0x_u_mm"), 1)
                for g in range(GROUPS):
                    pe.wait_ge(sem("l0x_u"), g + 1)
                    last = TE.matmul(bank(g), F("wv"), q_hat[:, QUAD * g:QUAD * g + QUAD, :], start=True, stop=True)
                    last.then_inc(sem("l0x_v_mm"), 1)
                for g in range(GROUPS):
                    pe.wait_ge(sem("norm_xn"), past("l0x", "norm_xn") + g + 1)
                    pe.wait_ge(sem("l0x_k"), g + 1)
                    for i in range(QUAD):
                        last = TE.matmul(bank4(4 + g)[:, i, :], xn[:, QUAD * g + i, :], F("dft")[:, 0:T],
                                         start=True, stop=True)
                    last.then_inc(sem("l0x_qhat_mm"), 1)
                for g in range(GROUPS):
                    pe.wait_ge(sem("l0x_qhat"), g + 1)
                    pe.wait_ge(sem("l0x_v"), g + 1)
                    for i in range(QUAD):
                        last = TE.matmul(bank4(g)[:, i, :], q_hat[:, QUAD * g + i, :], F("wq"), start=True, stop=True)
                    last.then_inc(sem("l0x_q_mm"), 1)
                for g in range(GROUPS):
                    pe.wait_ge(sem("l0x_prod"), g + 1)
                    for i in range(QUAD):
                        b = QUAD * g + i
                        TE.matmul(bank4(4 + g)[:, i, :], prod1[:, b, :], F("idft")[:, 0:T], start=True, stop=False)
                        last = TE.matmul(bank4(4 + g)[:, i, :], prod2[:, b, :], F("idft")[:, T:2 * T],
                                         start=False, stop=True)
                    last.then_inc(sem("l0x_corr_mm"), 1)
                keep_warm(pe, WARM["mix"], 3)
                for g in range(GROUPS):
                    pe.wait_ge(sem("l0x_mix"), g + 1)
                    for i in range(QUAD):
                        last = TE.transpose(bank4(g)[:, i, :], mix_T[:, QUAD * g + i, :], ident)
                    last.then_inc(sem("l0x_mix_turned"), 1)
                for g in range(GROUPS):
                    pe.wait_ge(sem("l0x_mixed"), g + 1)
                    for i in range(QUAD):
                        b = QUAD * g + i
                        last = TE.matmul(bank4(4 + g)[:, i, :], mix[:, b, :], values[:, b, :], start=True, stop=True)
                    last.then_inc(sem("l0x_out_mm"), 1)

            def scalar(a):
                for g in range(GROUPS):
                    a.wait_ge(sem("l0x_keys_mm"), g + 1)
                    S.copy(k_time[:, QUAD * g:QUAD * g + QUAD, :], bank4(g)).then_inc(sem("l0x_keys"), 1)
                for g in range(GROUPS):
                    a.wait_ge(sem("l0x_k_mm"), g + 1)
                    S.copy(k1[:, QUAD * g:QUAD * g + QUAD, :], bank4(4 + g)).then_inc(sem("l0x_k_scalar"), 1)
                for g in range(GROUPS):
                    a.wait_ge(sem("l0x_u_mm"), g + 1)
                    S.copy(q_hat[:, QUAD * g:QUAD * g + QUAD, :], bank4(g)).then_inc(sem("l0x_u"), 1)
                for g in range(GROUPS):
                    a.wait_ge(sem("l0x_v_mm"), g + 1)
                    S.copy(values[:, QUAD * g:QUAD * g + QUAD, :], bank4(g)).then_inc(sem("l0x_v"), 1)
                a.wait_ge(sem("l0x_v_mm"), GROUPS)
                for g in range(GROUPS):
                    a.wait_ge(sem("l0x_qhat_mm"), g + 1)
                    S.copy(q_hat[:, QUAD * g:QUAD * g + QUAD, :], bank4(4 + g)).then_inc(sem("l0x_qhat"), 1)
                a.wait_ge(sem("l0x_diff"), 1)
                S.activation(wsoft, wsoft, ACT.Exp).then_inc(sem("l0x_exp"), 1)
                for g in range(GROUPS):
                    a.wait_ge(sem("l0x_mix_turned"), g + 1)
                    S.copy(mix[:, QUAD * g:QUAD * g + QUAD, :].rearrange("p b (r h) -> p b h r", h=HEADS),
                           bank4(g).rearrange("p b (h r) -> p b h r", h=HEADS)).then_inc(sem("l0x_mixed"), 1)

            def vector(v):
                v.wait_ge(sem("load_x"), 16)
                for g in range(GROUPS):
                    measures["l0x"](v, g)
                norm_l0x[0](v)
                for g in range(GROUPS):
                    v.wait_ge(sem("l0x_k_mm"), GROUPS + g + 1)
                    V.tensor_copy(k2[:, QUAD * g:QUAD * g + QUAD, :], bank4(4 + g)).then_inc(sem("l0x_k"), 1)
                ahead["index"](v)
                v.wait_ge(sem("load_consts"), 16)
                v.wait_ge(sem("l0x_k"), GROUPS)
                v.wait_ge(sem("l0x_k_scalar"), GROUPS)
                for g in range(GROUPS):
                    s = slice(QUAD * g, QUAD * g + QUAD)
                    v.wait_ge(sem("l0x_q_mm"), g + 1)
                    V.tensor_tensor(prod1[:, s, :], bank4(g), k1[:, s, :], ALU.mult)
                    V.tensor_tensor(prod2[:, s, :], bank4(g), k2[:, s, :], ALU.mult).then_inc(sem("l0x_prod"), 1)
                for g in range(GROUPS):
                    v.wait_ge(sem("l0x_corr_mm"), g + 1)
                    for i in range(QUAD):
                        b = QUAD * g + i
                        last = V.max(top[:, b, :], bank4(4 + g)[:, i, :])
                    link(v, last)
                    for i in range(QUAD):
                        b = QUAD * g + i
                        last = V.max_index(where[:, b, :], top[:, b, :], bank4(4 + g)[:, i, :])
                link(v, last)
                four = [P, B, CORR_TOP]
                V.tensor_tensor(wsoft, top[:, :, 0:CORR_TOP], top[:, :, 0:1].to_broadcast(four),
                                ALU.subtract).then_inc(sem("l0x_diff"), 1)
                link(v, V.tensor_copy(shift, where[:, :, 0:CORR_TOP]))
                link(v, V.tensor_scalar(shift_i, shift, -1.0, C("dmod"), ALU.mult, ALU.add))
                link(v, V.tensor_scalar(shift_i, shift_i, HEAD - 1, None, ALU.bitwise_and))
                link(v, V.tensor_copy(shift, shift_i))
                full = [P, B, CORR_TOP, HEAD]
                link(v, V.tensor_tensor(hit, spread(shift, 3, full),
                                        C("iota8").unsqueeze(1).unsqueeze(1).to_broadcast(full), ALU.is_equal))
                v.wait_ge(sem("l0x_exp"), 1)
                link(v, V.tensor_reduce(wsum, wsoft, AX.X, ALU.add))
                link(v, V.reciprocal(wsum, wsum))
                link(v, V.tensor_tensor(wsoft, wsoft, spread(wsum, 2, four), ALU.mult))
                link(v, V.tensor_tensor(hit, hit, spread(wsoft, 3, full), ALU.mult))
                link(v, V.tensor_reduce(mix8, hit.rearrange("p b k r -> p b r k"), AX.X, ALU.add))
                for g in range(GROUPS):
                    s = slice(QUAD * g, QUAD * g + QUAD)
                    shape = [P, QUAD, HEADS, HEAD]
                    V.tensor_tensor(mix_T[:, s, :].rearrange("p b (h r) -> p b h r", h=HEADS),
                                    spread(mix8[:, s, :], 2, shape),
                                    C("blockmask").unsqueeze(1).unsqueeze(3).to_broadcast(shape),
                                    ALU.mult).then_inc(sem("l0x_mix"), 1)
                for g in range(GROUPS):
                    s = slice(QUAD * g, QUAD * g + QUAD)
                    v.wait_ge(sem("l0x_out_mm"), g + 1)
                    final(v, "l0f", g, V.tensor_tensor(x[:, s, :], bank4(4 + g), x[:, s, :], ALU.add))
            norm_l0x = norm("l0x")
            return vector, norm_l0x[1], tensor, scalar

        def l0_experts():
            ta, tb = carve(arena_a), carve(arena_b)
            F = lambda n: field["l0f", n]
            C = lambda n: field["consts", n]
            gated = ta(B * T, "p (b l) -> p b l", b=B)
            pairT = ta(B * T, "p (b r) -> p b r", b=B)
            silu = ta(2 * 512, "p (i c) -> p i c", i=2)
            picked = ta(E * P, "p (g k e h) -> p g k e h", g=E, k=2, e=E)
            pair13 = ta(3 * HID0, "p (i h) -> p i h", i=3)
            logitsT = ta(512)
            sums = ta(HID0)
            hiddenT = ta(PAIRS)
            pair = tb(B * 2 * PAIRS, "p (r e g) -> p r e g", r=2 * B, e=E)
            pre = tb(2 * B * HID0, "p (b k h) -> p b k h", k=2, b=B)
            act = tb(2 * B * HID0, "p (b k h) -> p b k h", k=2, b=B)
            score = tb(B * E, "p (b e) -> p b e", b=B)
            biased = tb(B * E, "p (b e) -> p b e", b=B)
            group = tb(B * 4, "p (b e) -> p b e", b=B)
            hot4 = tb(B * 4, "p (b e) -> p b e", b=B)
            keep4 = tb(B * 4, "p (b e) -> p b e", b=B)
            best = tb(B)
            chosen = tb(B * 2 * E, "p (b k e) -> p b k e", b=B, k=2)
            tmp = tb(B * 2 * E, "p (b k e) -> p b k e", b=B, k=2)
            weight = tb(B * 2, "p (b k) -> p b k", b=B)
            local = tb(E)
            ends = tb(E)
            low = tb(E * E, "p (e c) -> p e c", e=E)
            reached = tb(2 * B * (E + 1), "p (r e) -> p r e", r=2 * B)
            member = tb(2 * B * E, "p (r e) -> p r e", r=2 * B)
            by8 = [P, B, E]
            by4 = [P, B, 4]
            n = norm("l0f")
            logits, route, turn_logits, copy_logits = router("l0f", F("wgateT"), logitsT, "l0f_logits")

            def tensor(pe):
                pe.wait_ge(sem("load_l0f"), 16)
                n[2](pe, behind=lambda g: route(pe, g))
                def down(g):
                    pe.wait_ge(sem("l0f_gated"), g + 1)
                    for i in range(QUAD):
                        last = TE.matmul(bank4(4 + g)[:, i, :], gated[:, QUAD * g + i, :], F("sw2T"),
                                         start=True, stop=True)
                    last.then_inc(sem("l0f_shared"), 1)
                for g in range(GROUPS):
                    if g >= 2:
                        pe.wait_ge(sem("l0f_gated"), g - 1)
                    xb = xnT[:, QUAD * g:QUAD * g + QUAD, :]
                    TE.matmul(bank(g % 2), F("sw1T"), xb, start=True, stop=True).then_inc(sem("l0f_gate"), 1)
                    TE.matmul(bank(2 + g % 2), F("sw3T"), xb, start=True, stop=True).then_inc(sem("l0f_up"), 1)
                    if g == 0:
                        turn_logits(pe)
                        pe.wait_ge(sem("l0f_picked"), 1)
                        for e in range(E):
                            last = TE.matmul(bank(7)[:, 0:2 * HID0], picked[:, e, :, :, :],
                                             F("w13")[:, 2 * HID0 * e:2 * HID0 * (e + 1)], start=(e == 0), stop=(e == E - 1))
                        last.then_inc(sem("l0f_pair13_mm"), 1)
                    if g:
                        down(g - 1)
                down(GROUPS - 1)
                pe.wait_ge(sem("l0f_local"), 1)
                TE.matmul(bank(0)[:, 0:E], C("ones"), local, start=True, stop=True).then_inc(sem("l0f_counts"), 1)
                for g in range(GROUPS):
                    pe.wait_ge(sem("l0f_pair"), g + 1)
                    if g < 2:
                        pe.wait_ge(sem("l0f_gated"), GROUPS)
                    for i in range(QUAD):
                        last = TE.transpose(bank4(g)[:, i, :], pair[:, 2 * (QUAD * g + i):2 * (QUAD * g + i) + 2, :, :],
                                            ident)
                    last.then_inc(sem("l0f_pair_turned"), 1)
                pe.wait_ge(sem("l0f_pair13"), 1)
                for b in range(B):
                    pe.wait_ge(sem("l0f_added"), b // QUAD + 1)
                    pe.wait_ge(sem("l0f_pairT"), b // QUAD + 1)
                    last = TE.matmul(bank4(4 + b // QUAD)[:, b % QUAD, :], pairT[:, b, :], pair13[:, 0:2, :],
                                     start=True, stop=True)
                    if b % 8 == 7:
                        last.then_inc(sem("l0f_pre_mm"), 1)
                keep_warm(pe, WARM["act"], 1)
                for b in range(B):
                    pe.wait_ge(sem("l0f_act"), b // 8 + 1)
                    for k in range(2):
                        last = TE.matmul(bank(0)[0:PAIRS, 0:HID0], pair[:, 2 * b + k, :, :], act[:, b, k, :],
                                         start=(k == 0 and b == 0), stop=(k == 1 and b == B - 1))
                last.then_inc(sem("l0f_sums_mm"), 1)
                pe.wait_ge(sem("l0f_hidden"), 1)
                TE.transpose(bank(1)[0:HID0, 0:PAIRS], sums[0:PAIRS, :], ident[0:PAIRS, 0:PAIRS]).then_inc(sem("l0f_hidden_turned"), 1)
                pe.wait_ge(sem("l0f_hiddenT"), 1)
                hT = hiddenT[0:HID0, :].rearrange("p (e g) -> p g e", e=E)
                for g in range(E):
                    last = TE.matmul(bank(2)[0:E, 0:D], hT[:, g, :], F("w2")[0:HID0, D * g:D * g + D],
                                     start=(g == 0), stop=(g == E - 1))
                last.then_inc(sem("l0f_routed"), 1)

            def scalar(a):
                n[3](a)
                copy_logits(a)
                a.wait_ge(sem("l0f_centred"), 1)
                S.activation(score, score, ACT.Exp).then_inc(sem("l0f_exp"), 1)
                for g in range(GROUPS):
                    a.wait_ge(sem("l0f_gate"), g + 1)
                    if g >= 2:
                        a.wait_ge(sem("l0f_gated"), g - 1)
                    S.activation(silu[:, g % 2, :], bank(g % 2), ACT.Silu).then_inc(sem("l0f_silu"), 1)
                for g in range(GROUPS):
                    a.wait_ge(sem("l0f_pair_turned"), g + 1)
                    S.copy(pairT[:, QUAD * g:QUAD * g + QUAD, :], bank4(g)).then_inc(sem("l0f_pairT"), 1)
                for k in range(2):
                    a.wait_ge(sem("l0f_pre"), k + 1)
                    S.activation(act[:, 8 * k:8 * k + 8, :, :], pre[:, 8 * k:8 * k + 8, :, :], ACT.Silu).then_inc(sem("l0f_silu2"), 1)

            def vector(v):
                n[0](v)
                v.wait_ge(sem("load_l0f"), 16)
                link(v, V.memset(pair13, 0.0))
                link(v, V.memset(picked, 0.0))
                v.wait_ge(sem("norm_xnT"), past("l0f", "norm_xnT") + 1)
                for g in range(E):
                    last = V.tensor_copy(picked[:, g, :, :, g], spread(xnT[:, 0, 0:E], 1, [P, 2, E]))
                last.then_inc(sem("l0f_picked"), 1)
                v.wait_ge(sem("l0f_logits"), 1)
                link(v, V.tensor_copy(score.rearrange("p (g i) e -> p g i e", g=GROUPS), logits))
                link(v, V.tensor_reduce(best, score, AX.X, ALU.max))
                V.tensor_tensor(score, score, spread(best, 2, by8), ALU.subtract).then_inc(sem("l0f_centred"), 1)
                def shared(g):
                    v.wait_ge(sem("l0f_silu"), g + 1)
                    v.wait_ge(sem("l0f_up"), g + 1)
                    V.tensor_tensor(gated[:, QUAD * g:QUAD * g + QUAD, :],
                                    silu[:, g % 2, :].rearrange("p (b l) -> p b l", b=QUAD),
                                    bank4(2 + g % 2), ALU.mult).then_inc(sem("l0f_gated"), 1)
                def shared_add(g):
                    v.wait_ge(sem("l0f_shared"), g + 1)
                    s = slice(QUAD * g, QUAD * g + QUAD)
                    V.tensor_tensor(x[:, s, :], bank4(4 + g), x[:, s, :], ALU.add).then_inc(sem("l0f_added"), 1)

                def measured(g):
                    measures["l1x"](v, g)
                v.wait_ge(sem("l0f_pair13_mm"), 1)
                for k in range(2):
                    V.tensor_copy(pair13[PAIRS * k:PAIRS * k + PAIRS, k, :], bank(7)[PAIRS * k:PAIRS * k + PAIRS, 0:HID0])
                V.tensor_copy(pair13[:, 2, :], bank(7)[:, HID0:2 * HID0]).then_inc(sem("l0f_pair13"), 1)
                shared(0)
                v.wait_ge(sem("l0f_exp"), 1)
                link(v, V.tensor_reduce(best, score, AX.X, ALU.add))
                link(v, V.reciprocal(best, best))
                link(v, V.tensor_tensor(score, score, spread(best, 2, by8), ALU.mult))
                link(v, V.tensor_tensor(biased, score, spread(F("ebias"), 1, by8), ALU.add))
                pairs = biased.rearrange("p b (g i) -> p b g i", i=2)
                link(v, V.tensor_tensor(group, pairs[:, :, :, 0], pairs[:, :, :, 1], ALU.add))
                shared(1)
                prio4 = spread(C("prio4"), 1, by4)
                prio = spread(C("prio"), 1, by8)
                first_largest(v, keep4, group, prio4, best, by4)
                link(v, V.scalar_tensor_tensor(group, keep4, -FAR, group, ALU.mult, ALU.add))
                first_largest(v, hot4, group, prio4, best, by4)
                link(v, V.tensor_tensor(keep4, keep4, hot4, ALU.add))
                link(v, V.tensor_scalar(keep4, keep4, -1.0, FAR, ALU.add, ALU.mult))
                link(v, V.tensor_tensor(pairs, pairs, spread(keep4, 3, [P, B, 4, 2]), ALU.add))
                for k in range(2):
                    first_largest(v, chosen[:, :, k, :], biased, prio, best, by8)
                    if k == 0:
                        link(v, V.scalar_tensor_tensor(biased, chosen[:, :, k, :], -FAR, biased, ALU.mult, ALU.add))
                        shared(2)
                link(v, V.tensor_tensor(tmp, chosen, spread(score, 2, [P, B, 2, E]), ALU.mult))
                link(v, V.tensor_reduce(weight, tmp, AX.X, ALU.add))
                V.tensor_reduce(local, chosen.rearrange("p b k e -> p e b k"), AX.XY, ALU.add).then_inc(sem("l0f_local"), 1)
                shared(3)
                v.wait_ge(sem("l0f_counts"), 1)
                link(v, V.tensor_tensor(low, C("lower").rearrange("p (e c) -> p e c", e=E),
                                        spread(bank(0)[:, 0:E], 1, [P, E, E]), ALU.mult))
                link(v, V.tensor_reduce(ends, low, AX.X, ALU.add))
                rows9 = [P, 2 * B, E]
                V.memset(reached[:, :, 0], 1.0)
                link(v, V.tensor_tensor(reached[:, :, 1:E + 1], spread(C("rownum"), 2, rows9),
                                        spread(ends, 1, rows9), ALU.is_ge))
                link(v, V.tensor_tensor(member, reached[:, :, 0:E], reached[:, :, 1:E + 1], ALU.subtract))
                full = [P, 2 * QUAD, E, E]
                for g in range(GROUPS):
                    r = slice(2 * QUAD * g, 2 * QUAD * (g + 1))
                    V.tensor_tensor(pair[:, r, :, :], spread(chosen.rearrange("p b k e -> p (b k) e")[:, r, :], 3, full),
                                    spread(member[:, r, :], 2, full), ALU.mult).then_inc(sem("l0f_pair"), 1)
                for g in range(GROUPS):
                    shared_add(g)
                v.wait_ge(sem("l0f_added"), GROUPS)
                measured(1)
                flat3 = lambda ap: ap.rearrange("p b k h -> p (b k) h")
                weighting = lambda r: spread(weight.rearrange("p b k -> p (b k)")[:, 2 * r.start:2 * r.stop], 2, [P, B, HID0])
                halves = [slice(8 * k, 8 * k + 8) for k in range(2)]
                for k, r in enumerate(halves):
                    v.wait_ge(sem("l0f_pre_mm"), k + 1)
                    V.tensor_tensor(flat3(pre[:, r, :, :]), ps[:, 4 + 2 * k:6 + 2 * k, :].rearrange("p c (b h) -> p (c b) h", b=8),
                                    weighting(r), ALU.mult).then_inc(sem("l0f_pre"), 1)
                for k, r in enumerate(halves):
                    v.wait_ge(sem("l0f_silu2"), k + 1)
                    V.tensor_tensor(flat3(act[:, r, :, :]), flat3(act[:, r, :, :]), weighting(r),
                                    ALU.mult).then_inc(sem("l0f_act"), 1)
                measured(2)
                measured(3)
                v.wait_ge(sem("l0f_sums_mm"), 1)
                V.tensor_tensor(sums[0:PAIRS, :], bank(0)[0:PAIRS, 0:HID0], pair13[0:PAIRS, 2, :],
                                ALU.mult).then_inc(sem("l0f_hidden"), 1)
                v.wait_ge(sem("l0f_hidden_turned"), 1)
                V.tensor_copy(hiddenT[0:HID0, :], bank(1)[0:HID0, 0:PAIRS]).then_inc(sem("l0f_hiddenT"), 1)
                v.wait_ge(sem("l0f_routed"), 1)
                link(v, V.tensor_tensor(x[0:E, 0, :], bank(2)[0:E, 0:D], x[0:E, 0, :], ALU.add))
                starting(v, "l1x")
                measured(0)
            return vector, n[1], tensor, scalar

        def attention(tag, pack, wq, wk, wv, bq=None, bk=None, bv=None, causal=False):
            tb = carve(arena_b)
            qT = tb(B * T, "p (b l) -> p b l", b=B)
            attn = tb(B * T, "p (b l) -> p b l", b=B)
            attnT = tb(B * T, "p (b l) -> p b l", b=B)
            kT = tb(B * T, "p (b l) -> p b l", b=B)
            vals = tb(B * D, "p (b d) -> p b d", b=B)
            neg = tb(B)
            total = tb(B)
            F = lambda name: field[pack, name]
            scale = 1.0 / math.sqrt(D)
            following = {"l1x": "l1", "l2x": "l2f"}[tag]
            n = norm(tag, (1, 2, 3, 0) if tag == "l1x" else range(GROUPS))
            starts[tag] = sem("attn_start")
            quad = lambda ap, g: ap[:, QUAD * g:QUAD * g + QUAD, :]

            def tensor(pe):
                pe.wait_ge(sem("load_" + pack), 16)
                pe.wait_ge(sem("load_ctxT"), 16)
                pe.wait_ge(sem("attn_start"), past(tag, "attn_start") + 1)
                for g in range(GROUPS):
                    TE.matmul(bank(g), F(wk), quad(ctxT, g), start=True, stop=True).then_inc(sem("attn_k_mm"), 1)
                    for i in range(QUAD):
                        last = TE.matmul(bank4(4 + g)[:, i, :], ctxT[:, QUAD * g + i, :], F(wv), start=True, stop=True)
                    last.then_inc(sem("attn_v_mm"), 1)
                pe.wait_ge(sem("attn_k"), past(tag, "attn_k") + GROUPS)

                def queries(g):
                    pe.wait_ge(sem("norm_xnT"), past(tag, "norm_xnT") + g + 1)
                    TE.matmul(bank(g), F(wq), quad(xnT, g), start=True, stop=True).then_inc(sem("attn_q_mm"), 1)
                n[2](pe, behind=queries)
                pe.wait_ge(sem("attn_v"), past(tag, "attn_v") + GROUPS)
                for g in range(GROUPS):
                    pe.wait_ge(sem("attn_q"), past(tag, "attn_q") + g + 1)
                    for i in range(QUAD):
                        b = QUAD * g + i
                        last = TE.matmul(bank4(4 + g)[:, i, :], qT[:, b, :], kT[:, b, :], start=True, stop=True)
                    last.then_inc(sem("attn_logits"), 1)
                for g in range(GROUPS):
                    pe.wait_ge(sem("attn_exp"), past(tag, "attn_exp") + g + 1)
                    for i in range(QUAD):
                        last = TE.transpose(bank4(g)[:, i, :], attn[:, QUAD * g + i, :], ident)
                    last.then_inc(sem("attn_turned2"), 1)
                for g in range(GROUPS):
                    pe.wait_ge(sem("attn_attnT"), past(tag, "attn_attnT") + g + 1)
                    for i in range(QUAD):
                        b = QUAD * g + i
                        last = TE.matmul(bank4(4 + g)[:, i, :], attnT[:, b, :], vals[:, b, :], start=True, stop=True)
                    last.then_inc(sem("attn_out"), 1)

            def scalar(a):
                for g in range(GROUPS):
                    a.wait_ge(sem("attn_k_mm"), past(tag, "attn_k_mm") + g + 1)
                    if bk:
                        last = S.activation(quad(kT, g), bank4(g), ACT.Identity, bias=F(bk))
                    else:
                        last = S.copy(quad(kT, g), bank4(g))
                    last.then_inc(sem("attn_k"), 1)
                n[3](a)
                for g in range(GROUPS):
                    a.wait_ge(sem("attn_neg"), past(tag, "attn_neg") + g + 1)
                    for i in range(QUAD):
                        b = QUAD * g + i
                        src = attn[:, b, :] if causal else bank4(4 + g)[:, i, :]
                        last = S.activation(attn[:, b, :], src, ACT.Exp, bias=neg[:, b:b + 1], accum_out=total[:, b:b + 1])
                    last.then_inc(sem("attn_exp"), 1)
                if causal:
                    for g in range(GROUPS):
                        a.wait_ge(sem("attn_turned2"), past(tag, "attn_turned2") + g + 1)
                        S.copy(quad(attnT, g), bank4(g)).then_inc(sem("attn_attnT"), 1)

            def vector(v):
                n[0](v)
                v.wait_ge(sem("load_" + pack), 16)
                for g in range(GROUPS):
                    v.wait_ge(sem("attn_v_mm"), past(tag, "attn_v_mm") + g + 1)
                    if bv:
                        last = V.tensor_tensor(quad(vals, g), bank4(4 + g), spread(F(bv), 1, [P, QUAD, D]), ALU.add)
                    else:
                        last = V.tensor_copy(quad(vals, g), bank4(4 + g))
                    last.then_inc(sem("attn_v"), 1)
                for g in range(GROUPS):
                    v.wait_ge(sem("attn_q_mm"), past(tag, "attn_q_mm") + g + 1)
                    V.tensor_scalar(quad(qT, g), bank4(g), F(bq) if bq else 0.0, scale, ALU.add,
                                    ALU.mult).then_inc(sem("attn_q"), 1)
                for g in range(GROUPS):
                    v.wait_ge(sem("attn_logits"), past(tag, "attn_logits") + g + 1)
                    src = bank4(4 + g)
                    if causal:
                        src = quad(attn, g)
                        link(v, V.tensor_tensor(src, bank4(4 + g), spread(field["consts", "causal"], 1, [P, QUAD, T]), ALU.add))
                    V.tensor_reduce(neg[:, QUAD * g:QUAD * g + QUAD], src, AX.X, ALU.max,
                                    negate=True).then_inc(sem("attn_neg"), 1)
                if causal:
                    ahead["gather"](v)
                if not causal:
                    for g in range(GROUPS):
                        v.wait_ge(sem("attn_turned2"), past(tag, "attn_turned2") + g + 1)
                        V.tensor_copy(quad(attnT, g), bank4(g)).then_inc(sem("attn_attnT"), 1)
                v.wait_ge(sem("attn_exp"), past(tag, "attn_exp") + GROUPS)
                link(v, V.reciprocal(total, total))
                for g in range(GROUPS):
                    v.wait_ge(sem("attn_out"), past(tag, "attn_out") + g + 1)
                    for i in range(QUAD):
                        b = QUAD * g + i
                        last = V.scalar_tensor_tensor(x[:, b, :], bank4(4 + g)[:, i, :], total[:, b:b + 1], x[:, b, :],
                                                      ALU.mult, ALU.add)
                    final(v, following, g, last)

            def gpsimd(p):
                n[1](p)
                if causal:
                    ahead["scatter"](p)
            return vector, gpsimd, tensor, scalar

        def slotted(tag, cap, nb, gated, onehot, slots, hidden, silu, ring, turned_w, turned_y, taken, slotpos, weights,
                    channel_scale, left_over=None, any_left=None, flag_it=None,
                    vector_meanwhile=None, scalar_meanwhile=None):
            per = E * cap
            parts = -(-per // P)
            of = E // parts
            part = per // parts
            rows = max(part, 96)
            units = [(e, b0) for e in range(E) for b0 in range(0, B, nb)]
            cols = nb * cap
            nw = 2 if gated else 1
            depth = len(ring)
            turns = 4 // nw
            s_ = lambda what: sem("slotted_" + what)
            hot = onehot.rearrange("p (b e c) -> p b e c", b=B, e=E)
            sl = slots.rearrange("p (b e c) -> p b e c", e=E, b=B)
            hid = hidden.rearrange("p (i f n) -> p i f n", i=2, f=CH1)

            def weights_of(e):
                w = ring[e % depth]
                up = w[:, 0:nw * HID1].rearrange("p (i n) -> p i n", i=nw)
                down = w[:, nw * HID1:nw * HID1 + CH1 * D].rearrange("p (f n) -> p f n", f=CH1)
                bias = w[:, nw * HID1 + CH1 * D:]
                return up, down, [bias[:, CH1 * i:CH1 * i + CH1] for i in range(nw)], bias[:, CH1 * nw:CH1 * nw + 1]

            def sync(sp):
                for e in range(E):
                    if e >= depth:
                        sp.wait_ge(s_("y"), past(tag, "slotted_y") + (B // nb) * (e - depth + 1))
                    elif e == 2:
                        sp.wait_ge(s_("taken"), past(tag, "slotted_taken") + 1)
                    sp.dma_start(ring[e % depth], dram[tag + "_experts"][e, :, :]).then_inc(s_(f"ring{e % depth}"), 16)

            def positions_tensor(pe):
                keep_warm(pe, WARM["taken" + tag], 0)
                pe.wait_ge(s_("taken"), past(tag, "slotted_taken") + 1)
                TE.matmul(bank(6)[:, 0:B * E], field["consts", "before"], taken, start=True,
                          stop=True).then_inc(s_("before_mm"), 1)

            def tensor(pe):
                keep_warm(pe, WARM["onehot" + tag], 3)
                for b in range(B):
                    pe.wait_ge(s_("onehot"), past(tag, "slotted_onehot") + b // 2 + 1)
                    if b >= 4:
                        pe.wait_ge(s_("slots"), past(tag, "slotted_slots") + b - 3)
                    TE.matmul(bank(b % 4)[:, 0:per], xn[:, b, :], hot[:, b, :, :], start=True,
                              stop=True).then_inc(s_("slots_mm"), 1)
                pe.wait_ge(s_("slots"), past(tag, "slotted_slots") + B)

                def down(u):
                    e, b0 = units[u]
                    pe.wait_ge(s_("hidden"), past(tag, "slotted_hidden") + CH1 * (u + 1))
                    if u >= 2:
                        pe.wait_ge(s_("y"), past(tag, "slotted_y") + u - 1)
                    for f in range(CH1):
                        last = TE.matmul(bank(4 + u % 2)[:, 0:cols], weights_of(e)[1][:, f, :], hid[:, u % 2, f, :],
                                         start=(f == 0), stop=(f == CH1 - 1))
                    last.then_inc(s_("down_mm"), 1)
                for u, (e, b0) in enumerate(units):
                    if b0 == 0:
                        pe.wait_ge(s_(f"ring{e % depth}"), past(tag, f"slotted_ring{e % depth}") + 16 * (e // depth + 1))
                    for f in range(CH1):
                        k = CH1 * u + f
                        if k >= turns:
                            pe.wait_ge(s_("hidden"), past(tag, "slotted_hidden") + k - turns + 1)
                        for i in range(nw):
                            last = TE.matmul(bank(2 * i + k % turns)[:, 0:cols], weights_of(e)[0][:, i, P * f:P * f + P],
                                             sl[:, b0:b0 + nb, e, :], start=True, stop=True)
                            if gated and i == 0:
                                last.then_inc(s_("gate_mm"), 1)
                        last.then_inc(s_("up_mm"), 1)
                    if u:
                        down(u - 1)
                down(len(units) - 1)
                if left_over:
                    pe.wait_ge(sem("rest_any"), spent("rest_any") + 1)
                    TE.matmul(bank(6)[:, 256:257], field["consts", "ones"], any_left, start=True,
                              stop=True).then_inc(sem("rest_any_mm"), 1)
                pe.wait_ge(s_("weighted"), past(tag, "slotted_weighted") + len(units) // 2)
                pe.wait_ge(s_("y"), past(tag, "slotted_y") + len(units))

                def turn(b):
                    if b >= 2:
                        pe.wait_ge(s_("turned_w"), past(tag, "slotted_turned_w") + b - 1)
                        pe.wait_ge(s_("turned_y"), past(tag, "slotted_turned_y") + b - 1)
                    for j in range(parts):
                        last = TE.transpose(bank4(b % 2)[0:part, j, :], hot[:, b, of * j:of * j + of, :], ident)
                    last.then_inc(s_("turn_w"), 1)
                    for j in range(parts):
                        last = TE.transpose(bank4(2 + b % 2)[0:part, j, :], sl[:, b, of * j:of * j + of, :], ident)
                    last.then_inc(s_("turn_y"), 1)
                turn(0)
                for b in range(B):
                    if left_over and b == 2 * QUAD:
                        pe.wait_ge(sem("rest_flag"), spent("rest_flag") + 1)
                    if b + 1 < B:
                        turn(b + 1)
                    pe.wait_ge(s_("turned_w"), past(tag, "slotted_turned_w") + b + 1)
                    pe.wait_ge(s_("turned_y"), past(tag, "slotted_turned_y") + b + 1)
                    for j in range(parts):
                        last = TE.matmul(bank4(4 + b // QUAD)[:, b % QUAD, :], turned_w[0:rows, b % 2, j, :],
                                         turned_y[0:rows, b % 2, j, :], start=(j == 0), stop=(j == parts - 1))
                    last.then_inc(s_("combined"), 1)

            def scalar(a):
                for b in range(B):
                    a.wait_ge(s_("slots_mm"), past(tag, "slotted_slots_mm") + b + 1)
                    src = bank(b % 4)[:, 0:per].rearrange("p (e c) -> p e c", e=E)
                    if channel_scale is None:
                        last = S.copy(sl[:, b, :, :], src)
                    else:
                        last = S.activation(sl[:, b, :, :], src, ACT.Identity, scale=channel_scale)
                    last.then_inc(s_("slots"), 1)
                    if scalar_meanwhile and b == B // 2:
                        scalar_meanwhile(a)

                for u, (e, b0) in enumerate(units):
                    for f in range(CH1):
                        k = CH1 * u + f
                        if gated:
                            a.wait_ge(s_("gate_mm"), past(tag, "slotted_gate_mm") + k + 1)
                            if k >= 2:
                                a.wait_ge(s_("hidden"), past(tag, "slotted_hidden") + k - 1)
                            S.activation(silu[:, k % 2, 0:cols], bank(k % 2)[:, 0:cols], ACT.Silu,
                                         bias=weights_of(e)[2][0][:, f:f + 1]).then_inc(s_("silu"), 1)
                        else:
                            a.wait_ge(s_("up_mm"), past(tag, "slotted_up_mm") + k + 1)
                            S.activation(hid[:, u % 2, f, :], bank(k % turns)[:, 0:cols], ACT.Relu,
                                         bias=weights_of(e)[2][0][:, f:f + 1]).then_inc(s_("hidden"), 1)
                for b in range(B):
                    a.wait_ge(s_("turn_w"), past(tag, "slotted_turn_w") + b + 1)
                    if b >= 2:
                        a.wait_ge(s_("combined"), past(tag, "slotted_combined") + b - 1)
                    S.copy(turned_w[0:part, b % 2, :, :], bank4(b % 2)[0:part, 0:parts, :]).then_inc(s_("turned_w"), 1)

            def vector(v):
                if rows > part:
                    for turned in (turned_w, turned_y):
                        link(v, V.memset(turned[64:96, :, :, :], 0.0))
                v.wait_ge(s_("before_mm"), past(tag, "slotted_before_mm") + 1)
                link(v, V.scalar_tensor_tensor(slotpos, bank(6)[:, 0:B * E], 1.0, taken, ALU.add, ALU.mult))
                link(v, V.tensor_scalar(slotpos, slotpos, -1.0, None, ALU.add))
                pos = slotpos.rearrange("p (b e) -> p b e", b=B)
                shape = [P, 2 * E, cap]
                flat = onehot.rearrange("p (r c) -> p r c", c=cap)
                for i in range(B // 2):
                    r = slice(2 * E * i, 2 * E * (i + 1))
                    V.tensor_tensor(flat[:, r, :], spread(slotpos[:, r], 2, shape),
                                    spread(field["consts", "slot"][:, 0:cap], 1, shape), ALU.is_equal).then_inc(s_("onehot"), 1)
                if vector_meanwhile:
                    vector_meanwhile(v)
                pieces = len(units) // 2

                def weigh(i):
                    n_ = B * E // pieces
                    r = slice(n_ * i, n_ * i + n_)
                    v.wait_ge(s_("slots_mm"), past(tag, "slotted_slots_mm") + B // pieces * (i + 1))
                    few = [P, n_, cap]
                    V.tensor_tensor(flat[:, r, :], flat[:, r, :], spread(weights[:, r], 2, few),
                                    ALU.mult).then_inc(s_("weighted"), 1)

                def y(u):
                    e, b0 = units[u]
                    v.wait_ge(s_("down_mm"), past(tag, "slotted_down_mm") + u + 1)
                    V.tensor_scalar(sl[:, b0:b0 + nb, e, :], bank(4 + u % 2)[:, 0:cols].rearrange("p (b c) -> p b c", b=nb),
                                    weights_of(e)[3], None, ALU.add).then_inc(s_("y"), 1)
                for u, (e, b0) in enumerate(units):
                    if gated:
                        for f in range(CH1):
                            k = CH1 * u + f
                            if u >= 2 and f == 0:
                                v.wait_ge(s_("down_mm"), past(tag, "slotted_down_mm") + u - 1)
                            v.wait_ge(s_("silu"), past(tag, "slotted_silu") + k + 1)
                            v.wait_ge(s_("up_mm"), past(tag, "slotted_up_mm") + k + 1)
                            V.scalar_tensor_tensor(hid[:, u % 2, f, :], bank(2 + k % 2)[:, 0:cols], weights_of(e)[2][1][:, f:f + 1],
                                                   silu[:, k % 2, 0:cols], ALU.add, ALU.mult).then_inc(s_("hidden"), 1)
                    if u:
                        y(u - 1)
                    if 1 <= u <= pieces:
                        weigh(u - 1)
                    if left_over and u == pieces + 1:
                        left_over(v)
                y(len(units) - 1)
                if left_over:
                    flag_it(v)
                for b in range(B):
                    v.wait_ge(s_("turn_y"), past(tag, "slotted_turn_y") + b + 1)
                    if b >= 2:
                        v.wait_ge(s_("combined"), past(tag, "slotted_combined") + b - 1)
                    V.tensor_copy(turned_y[0:part, b % 2, :, :], bank4(2 + b % 2)[0:part, 0:parts, :]).then_inc(s_("turned_y"), 1)
                for g in range(GROUPS):
                    v.wait_ge(s_("combined"), past(tag, "slotted_combined") + QUAD * (g + 1))
                    q = slice(QUAD * g, QUAD * g + QUAD)
                    V.tensor_tensor(x[:, q, :], bank4(4 + g), x[:, q, :], ALU.add).then_inc(s_("added"), 1)
            return sync, positions_tensor, tensor, scalar, vector

        def l1_experts():
            ta, tb = carve(arena_a), carve(arena_b)
            F = lambda name: field["l1f", name]
            C = lambda name: field["consts", name]
            hidden = ta(2 * CH1 * (B // 2) * CAP1)
            silu = ta(2 * (B // 2) * CAP1, "p (i n) -> p i n", i=2)
            ring = ta(2 * RING1, "p (i n) -> p i n", i=2)
            onehot = tb(B * E * CAP1)
            slots = tb(B * E * CAP1)
            score = tb(B * E, "p (b e) -> p b e", b=B)
            left = tb(B * E, "p (b e) -> p b e", b=B)
            chosen = tb(B * 2 * E, "p (b k e) -> p b k e", b=B, k=2)
            tmp = tb(B * 2 * E, "p (b k e) -> p b k e", b=B, k=2)
            best = tb(B)
            weight = tb(B * 2, "p (b k) -> p b k", b=B)
            second = tb(B)
            taken = tb(B * E)
            slotpos = tb(B * E)
            weights = tb(B * E)
            excess = tb(B * E)
            any_left = tb(1)
            flag = tb(1).bitcast(I32)
            column = tb(B)
            turned_w = hidden[:, 0:1024].rearrange("p (i j n) -> p i j n", i=2, j=4)
            turned_y = hidden[:, 1024:2048].rearrange("p (i j n) -> p i j n", i=2, j=4)
            dense_h = hidden[:, 0:CH1 * 512].rearrange("p (f n) -> p f n", f=CH1)
            dense_y = slots[:, 0:512]
            dense_silu = slots[:, 512:1024]
            n = norm("l1", rms=F("lnw"))
            logits, route, turn_logits, copy_logits = router("l1", F("Wg"), hidden[:, 0:512], "l1_logits")
            sync, positions, tensor_, scalar_, vector_ = slotted(
                "l1", CAP1, B // 2, True, onehot, slots, hidden, silu, [ring[:, 0, :], ring[:, 1, :]], turned_w, turned_y, taken, slotpos, weights,
                F("lnw"), lambda v: left_over(v), any_left, lambda v: flag_it(v), lambda v: weigh_chosen(v),
                lambda a: exp_second(a))

            def weigh_chosen(v):
                link(v, V.tensor_tensor(tmp, chosen, spread(score, 2, [P, B, 2, E]), ALU.mult))
                link(v, V.tensor_reduce(weight, tmp, AX.X, ALU.add))
                V.tensor_tensor(second, weight[:, :, 1], weight[:, :, 0], ALU.subtract).then_inc(sem("l1_second"), 1)
                v.wait_ge(sem("l1_exp"), 1)
                link(v, V.tensor_scalar(best, second, 1.0, None, ALU.add))
                link(v, V.reciprocal(weight[:, :, 0], best))
                link(v, V.tensor_tensor(weight[:, :, 1], second, weight[:, :, 0], ALU.mult))
                link(v, V.tensor_tensor(tmp, chosen, spread(weight, 3, [P, B, 2, E]), ALU.mult))
                link(v, V.tensor_tensor(weights.rearrange("p (b e) -> p b e", b=B), tmp[:, :, 0, :], tmp[:, :, 1, :], ALU.add))

            def left_over(v):
                link(v, V.tensor_scalar(excess, slotpos, float(CAP1), None, ALU.is_ge))
                V.tensor_reduce(any_left, excess, AX.X, ALU.max).then_inc(sem("rest_any"), 1)
                link(v, V.tensor_tensor(excess, excess, weights, ALU.mult))

            def flag_it(v):
                v.wait_ge(sem("rest_any_mm"), spent("rest_any_mm") + 1)
                V.tensor_scalar(flag, bank(6)[:, 256:257], 0.0, None, ALU.is_gt).then_inc(sem("rest_flag"), 1)

            def tensor(pe):
                pe.wait_ge(sem("load_l1f"), 16)
                n[2](pe, behind=lambda g: route(pe, g))
                turn_logits(pe)
                positions(pe)
                tensor_(pe)
                with second_pass(pe):
                    with pe.Fori(0, E) as e:
                        pe.wait_ge(sem("rest_weights"), spent("rest_weights") + 16 * e + 16)
                        for g in range(GROUPS):
                            unit = GROUPS * e + g
                            for f in range(CH1):
                                pe.wait_ge(sem("rest_hidden"), spent("rest_hidden") + CH1 * unit + f)
                                TE.matmul(bank(0), ring[:, 0, P * f:P * f + P], xnT[:, QUAD * g:QUAD * g + QUAD, :],
                                          start=True, stop=True).then_inc(sem("rest_gate"), 1)
                                TE.matmul(bank(1), ring[:, 0, HID1 + P * f:HID1 + P * f + P],
                                          xnT[:, QUAD * g:QUAD * g + QUAD, :], start=True, stop=True).then_inc(sem("rest_up"), 1)
                            pe.wait_ge(sem("rest_hidden"), spent("rest_hidden") + CH1 * unit + CH1)
                            pe.wait_ge(sem("rest_y"), spent("rest_y") + unit)
                            for f in range(CH1):
                                last = TE.matmul(bank(2), ring[:, 0, 2 * HID1 + D * f:2 * HID1 + D * f + D], dense_h[:, f, :],
                                                 start=(f == 0), stop=(f == CH1 - 1))
                            last.then_inc(sem("rest_down"), 1)
                            pe.wait_ge(sem("rest_y"), spent("rest_y") + unit + 1)
                            pe.wait_ge(sem("rest_added"), spent("rest_added") + unit)
                            for i in range(QUAD):
                                last = TE.transpose(bank4(3)[:, i, :], dense_y[:, T * i:T * i + T], ident)
                            last.then_inc(sem("rest_turned"), 1)

            def second_pass(eng):
                eng.wait_ge(sem("rest_flag"), spent("rest_flag") + 1)
                return eng.If(eng.value_load(flag[0:1, 0:1], min_val=0, max_val=1) > 0)

            def exp_second(a):
                a.wait_ge(sem("l1_second"), 1)
                S.activation(second, second, ACT.Exp).then_inc(sem("l1_exp"), 1)

            def scalar(a):
                a.wait_ge(sem("load_l1f"), 16)
                n[3](a)
                copy_logits(a)
                scalar_(a)
                with second_pass(a):
                    with a.Fori(0, E * GROUPS) as unit:
                        for f in range(CH1):
                            a.wait_ge(sem("rest_gate"), spent("rest_gate") + CH1 * unit + f + 1)
                            a.wait_ge(sem("rest_hidden"), spent("rest_hidden") + CH1 * unit + f)
                            S.activation(dense_silu, bank(0), ACT.Silu,
                                         bias=ring[:, 0, 3 * HID1 + f:3 * HID1 + f + 1]).then_inc(sem("rest_silu"), 1)

            def vector(v):
                v.sem_inc(sem("l1_start"), 1)
                n[0](v)
                by8 = [P, B, E]
                prio = spread(C("prio"), 1, by8)
                v.wait_ge(sem("l1_logits"), 1)
                link(v, V.tensor_copy(score.rearrange("p (g i) e -> p g i e", g=GROUPS), logits))
                link(v, V.tensor_tensor(score, score, spread(F("bg"), 1, by8), ALU.add))
                first_largest(v, chosen[:, :, 0, :], score, prio, best, by8)
                link(v, V.scalar_tensor_tensor(left, chosen[:, :, 0, :], -FAR, score, ALU.mult, ALU.add))
                first_largest(v, chosen[:, :, 1, :], left, prio, best, by8)
                V.tensor_tensor(taken.rearrange("p (b e) -> p b e", b=B), chosen[:, :, 0, :], chosen[:, :, 1, :],
                                ALU.add).then_inc(sem("slotted_taken"), 1)
                vector_(v)
                v.wait_ge(sem("slotted_added"), past("l1", "slotted_added") + GROUPS)
                with second_pass(v):
                    with v.Fori(0, E) as e:
                        v.wait_ge(sem("rest_added"), spent("rest_added") + GROUPS * e)
                        V.tensor_copy(column, excess.rearrange("p (b e) -> p b e", b=B)[:, :, bass.ds(e, 1)]).then_inc(sem("rest_column"), 1)
                        v.wait_ge(sem("rest_column"), spent("rest_column") + e + 1)
                        for g in range(GROUPS):
                            unit = GROUPS * e + g
                            v.wait_ge(sem("rest_down"), spent("rest_down") + unit)
                            for f in range(CH1):
                                n_ = CH1 * unit + f + 1
                                v.wait_ge(sem("rest_silu"), spent("rest_silu") + n_)
                                v.wait_ge(sem("rest_up"), spent("rest_up") + n_)
                                b1b = 3 * HID1 + CH1 + f
                                V.scalar_tensor_tensor(dense_h[:, f, :], bank(1), ring[:, 0, b1b:b1b + 1], dense_silu,
                                                       ALU.add, ALU.mult).then_inc(sem("rest_hidden"), 1)
                            v.wait_ge(sem("rest_down"), spent("rest_down") + unit + 1)
                            v.wait_ge(sem("rest_turned"), spent("rest_turned") + unit)
                            V.tensor_scalar(dense_y, bank(2), ring[:, 0, RING1 - 1:RING1], None,
                                            ALU.add).then_inc(sem("rest_y"), 1)
                            v.wait_ge(sem("rest_turned"), spent("rest_turned") + unit + 1)
                            v.wait_ge(sem("rest_added"), spent("rest_added") + unit)
                            for i in range(QUAD):
                                b = QUAD * g + i
                                last = V.scalar_tensor_tensor(x[:, b, :], bank4(3)[:, i, :], column[:, b:b + 1], x[:, b, :],
                                                              ALU.mult, ALU.add)
                            last.then_inc(sem("rest_added"), 1)
                    v.wait_ge(sem("rest_added"), spent("rest_added") + E * GROUPS)
                starting(v, "l2x")
                for g in range(GROUPS):
                    measures["l2x"](v, g, overlap=True)

            def start_sync(sp):
                sp.wait_ge(sem("l1_start"), 1)
                sync(sp)
                sp.wait_ge(sem("slotted_combined"), past("l1", "slotted_combined") + B)
                with second_pass(sp):
                    with sp.Fori(0, E) as e:
                        sp.wait_ge(sem("rest_added"), spent("rest_added") + GROUPS * e)
                        sp.dma_start(ring[:, 0, :], dram["l1_experts"][bass.ds(e, 1), :, :].rearrange("e p n -> (e p) n")
                                     ).then_inc(sem("rest_weights"), 16)
            return vector, n[1], tensor, scalar, start_sync

        def l2_experts():
            ta, tb = carve(arena_a), carve(arena_b)
            F = lambda name: field["l2", name]
            C = lambda name: field["consts", name]
            H = HID2
            NM = M2 // P
            gather = ta(B * M2, "p (b m) -> p b m", b=B)
            scatter = ta(NM * B * T, "p (i b l) -> p i b l", i=NM, b=B)
            both = tb(B * 2 * H, "p (b i h) -> p b i h", b=B, i=2)
            zs = tb(B * H, "p (b h) -> p b h", b=B)
            zsT = tb(B // 2 * T, "p (u l) -> p u l", u=B // 2)
            shared = tb(B * D, "p (b d) -> p b d", b=B)
            sel = tb(2 * NM * E * H, "p (w i e h) -> p w i e h", w=2, i=NM, e=E)
            mine = tb(2 * NM * H, "p (w i h) -> p w i h", w=2, i=NM)
            zm = tb(NM * E * H, "p (i e h) -> p i e h", i=NM, e=E)
            zmT = tb(NM * 4 * P, "p (i j m) -> p i j m", i=NM, j=4)
            rowsT = tb(M2)
            value = tb(NM * (D + 1), "p (i d) -> p i d", i=NM)
            keepmore = tb(B)
            st = tb(2 * B * 6, "p (w b c) -> p w b c", w=2, b=B)
            mv = tb(2 * B * 2, "p (w b c) -> p w b c", w=2, b=B)
            ve = tb(2 * B, "p (w b) -> p w b", w=2)
            rs = tb(2 * B, "p (w b) -> p w b", w=2)
            gate = tb(NM * (E + 1), "p (i e) -> p i e", i=NM)
            score = tb(NM * E, "p (i e) -> p i e", i=NM)
            onehot = tb(NM * E, "p (i e) -> p i e", i=NM)
            picked = tb(NM * E, "p (i e) -> p i e", i=NM)
            best = tb(NM)
            two = tb(NM * 2, "p (i w) -> p i w", i=NM)
            onehotT = tb(NM * P, "p (i m) -> p i m", i=NM)
            update = both.rearrange("p b i h -> p b (i h)")
            n = norm("l2f")
            s_ = lambda what: sem("l2f_" + what)

            def index_ahead(v):
                tc = carve(arena_b, 13312)
                idx = tc(2 * (M2 + NM), "p (w n) -> p w n", w=2)
                inside = tc(2 * (M2 + NM), "p (w n) -> p w n", w=2)
                same = tc(M2)
                at = row_at[:, :]
                v.wait_ge(sem("load_index"), 16)
                link(v, V.tensor_copy(idx, index_sb[:, :, :]))
                for w, size in enumerate((B, T)):
                    link(v, V.tensor_scalar(inside[:, w, :], idx[:, w, :], 0.0, float(size), ALU.is_lt, ALU.mult))
                link(v, V.tensor_tensor(idx, idx, inside, ALU.add))
                for w, size in enumerate((B, T)):
                    link(v, V.tensor_scalar(inside[:, w, :], idx[:, w, :], 0.0, float(size - 1), ALU.max, ALU.min))
                link(v, V.tensor_tensor(inside, inside, idx, ALU.is_equal))
                link(v, V.tensor_tensor(inside[:, 0, :], inside[:, 0, :], inside[:, 1, :], ALU.mult))
                link(v, V.scalar_tensor_tensor(at, idx[:, 0, :], float(T), idx[:, 1, :], ALU.mult, ALU.add))
                link(v, V.scalar_tensor_tensor(at, at, 1.0, inside[:, 0, :], ALU.add, ALU.mult))
                link(v, V.tensor_scalar(at, at, -1.0, None, ALU.add))
                v.wait_ge(sem("load_consts"), 16)
                for i in range(NM):
                    link(v, V.scalar_tensor_tensor(same, at[:, 0:M2], at[:, M2 + i:M2 + i + 1],
                                                   C("earlier")[:, M2 * i:M2 * i + M2], ALU.is_equal, ALU.mult))
                    link(v, V.tensor_reduce(row_first[:, i:i + 1], same, AX.X, ALU.max))
                link(v, V.tensor_scalar(row_first[:, :], row_first[:, :], -1.0, 1.0, ALU.mult, ALU.add))
                v.sem_inc(s_("index"), 1)

            def gather_ahead(v):
                V.tensor_tensor(gather, spread(C("token"), 2, [P, B, M2]), spread(row_at[:, 0:M2], 1, [P, B, M2]),
                                ALU.is_equal).then_inc(s_("gather"), 1)

            def scatter_ahead(p):
                p.wait_ge(s_("index"), 1)
                p.wait_ge(sem("attn_start"), 2)
                for i in range(NM):
                    nc.gpsimd.tensor_scalar(scatter[:, i, :, :], C("tokenrow").rearrange("p (b l) -> p b l", b=B),
                                            row_at[:, M2 + i:M2 + i + 1], None, ALU.is_equal).then_inc(s_("scatter"), 1)
            ahead["index"], ahead["gather"], ahead["scatter"] = index_ahead, gather_ahead, scatter_ahead

            def tensor(pe):
                pe.wait_ge(sem("load_l2"), 16)

                def both_up(g):
                    pe.wait_ge(sem("norm_xnT"), past("l2f", "norm_xnT") + g + 1)
                    for i in range(QUAD):
                        last = TE.matmul(bank4(4 + g)[:, i, :], xnT[:, QUAD * g + i, :], F("sw12T"), start=True, stop=True)
                    last.then_inc(s_("both_mm"), 1)
                n[2](pe, behind=both_up)
                pe.wait_ge(s_("gather"), 1)
                for b in range(B):
                    last = TE.matmul(bank(0)[:, 0:M2], xn[:, b, :], gather[:, b, :], start=(b == 0), stop=(b == B - 1))
                last.then_inc(s_("rows_mm"), 1)
                pe.wait_ge(s_("rowsT"), 1)
                for i in range(NM):
                    last = TE.matmul(bank(1)[:, (E + 1) * i:(E + 1) * (i + 1)], rowsT[:, P * i:P * i + P], F("gateT"),
                                     start=True, stop=True)
                last.then_inc(s_("gate_mm"), 1)
                pe.wait_ge(s_("both"), GROUPS)
                for w, name in enumerate(("ew1T", "ew2T")):
                    for i in range(NM):
                        last = TE.matmul(bank(4 + 2 * w + i), rowsT[:, P * i:P * i + P], F(name), start=True, stop=True)
                    last.then_inc(s_("sel_mm"), 1)
                pe.wait_ge(s_("gate"), 1)
                pe.wait_ge(s_("onehot"), 1)
                for i in range(NM):
                    last = TE.transpose(bank4(1)[0:E, i, :], onehot[:, i, :], ident)
                last.then_inc(s_("onehot_turned"), 1)
                pe.wait_ge(s_("onehotT"), 1)
                for i in range(NM):
                    last = TE.matmul(bank4(1)[:, 2 + i, :], onehotT[0:E, i, :], F("eb12")[0:E, :], start=True, stop=True)
                last.then_inc(s_("bias_mm"), 1)
                keep_warm(pe, WARM["zs"], 2)
                pe.wait_ge(s_("zs"), 1)
                for u in range(B // 2):
                    last = TE.transpose(bank4(2 + u // 4)[:, u % 4, :], zs[:, 2 * u:2 * u + 2, :], ident)
                last.then_inc(s_("zs_turned"), 1)
                pe.wait_ge(s_("zsT"), 1)
                pe.wait_ge(s_("biased"), 1)
                pe.wait_ge(s_("sel"), 2)
                for u in range(B // 2):
                    last = TE.matmul(bank((0, 1, 4, 5)[u // 2])[:, 2 * D * (u % 2):2 * D * (u % 2) + 2 * D], zsT[:, u, :],
                                     F("sw3T"), start=True, stop=True)
                    if u % 4 == 3:
                        last.then_inc(s_("shared_mm"), 1)
                pe.wait_ge(s_("zm"), 1)
                for i in range(NM):
                    for j in range(4):
                        last = TE.transpose(bank4(2 + i)[:, j, :], zm[:, i, 2 * j:2 * j + 2, :], ident)
                    last.then_inc(s_("zm_turned"), 1)
                pe.wait_ge(s_("zmT"), NM)
                for i in range(NM):
                    for j in range(4):
                        TE.matmul(bank4(7)[:, i, :], zmT[:, i, j, :], F("ew3")[:, D * j:D * j + D], start=(j == 0), stop=False)
                    last = TE.matmul(bank4(7)[:, i, :], onehotT[0:E, i, :], F("eb3")[0:E, :], start=False, stop=True)
                last.then_inc(s_("expert_mm"), 1)
                pe.wait_ge(s_("scatter"), NM)
                pe.wait_ge(s_("value"), 1)
                pe.wait_ge(s_("shared"), 2)
                for b in range(B):
                    for i in range(NM):
                        last = TE.matmul(bank(b // 3)[:, (D + 1) * (b % 3):(D + 1) * (b % 3 + 1)], scatter[:, i, b, :],
                                         value[:, i, :], start=(i == 0), stop=(i == NM - 1))
                    if b % 3 == 2 or b == B - 1:
                        last.then_inc(s_("back"), 1)

            def gpsimd(g):
                n[1](g)
                for w, count in enumerate((B, NM)):
                    g.wait_ge(s_(f"ve{w}"), 1)
                    nc.gpsimd.tensor_tensor(rs[:, w, 0:count], ve[:, w, 0:count], minushalf[:, 0:count],
                                            ALU.pow).then_inc(s_(f"rs{w}"), 1)

            def scalar(a):
                n[3](a)
                for g in range(GROUPS):
                    a.wait_ge(s_("both"), g + 1)
                    q = slice(QUAD * g, QUAD * g + QUAD)
                    S.activation(both[:, q, 0, :], both[:, q, 0, :], ACT.Silu).then_inc(s_("silu"), 1)
                a.wait_ge(s_("gate"), 1)
                S.activation(gate, gate, ACT.Sigmoid).then_inc(s_("sigmoid"), 1)
                a.wait_ge(sem("filled"), 2)
                a.wait_ge(s_("rows_mm"), 1)
                ahead["keys"](a, 0)
                a.wait_ge(s_("biased"), 1)
                S.activation(mine[:, 0, :, :], mine[:, 0, :, :], ACT.Silu).then_inc(s_("sel_silu"), 1)
                a.wait_ge(s_("zs_turned"), 1)
                S.activation(zsT, ps[:, 2:4, :].rearrange("p j (u l) -> p (j u) l", u=4), ACT.Identity, bias=F("slnb"),
                             scale=F("slng")).then_inc(s_("zsT"), 1)
                for i in range(NM):
                    a.wait_ge(s_("zm_turned"), i + 1)
                    S.copy(zmT[:, i, :, :], bank4(2 + i)).then_inc(s_("zmT"), 1)
                a.wait_ge(s_("two"), 1)
                S.activation(two, two, ACT.Exp).then_inc(s_("exp"), 1)
                a.wait_ge(s_("back"), -(-B // 3))
                ahead["keys"](a, 1)

            def measured(v, w, src, count):
                for b in range(count):
                    last = V.bn_stats(st[:, w, b, :], src[:, b, :])
                link(v, last)
                for b in range(count):
                    last = V.bn_aggr(mv[:, w, b, :], st[:, w, b, :])
                link(v, last)
                V.tensor_scalar_add(ve[:, w, 0:count], mv[:, w, 0:count, 1], LN_EPS).then_inc(s_(f"ve{w}"), 1)

            def normed(v, w, src, dst, count):
                v.wait_ge(s_(f"rs{w}"), 1)
                shape = [P, count, H]
                link(v, V.tensor_tensor(dst, src, spread(mv[:, w, 0:count, 0], 2, shape), ALU.subtract))
                return V.tensor_tensor(dst, dst, spread(rs[:, w, 0:count], 2, shape), ALU.mult)

            def vector(v):
                n[0](v)
                v.wait_ge(sem("load_l2"), 16)
                for g in range(GROUPS):
                    q = slice(QUAD * g, QUAD * g + QUAD)
                    v.wait_ge(s_("both_mm"), g + 1)
                    V.tensor_tensor(both[:, q, :, :].rearrange("p b i h -> p b (i h)"), bank4(4 + g),
                                    spread(F("sb12"), 1, [P, QUAD, 2 * H]), ALU.add).then_inc(s_("both"), 1)
                v.wait_ge(s_("silu"), GROUPS)
                link(v, V.tensor_tensor(both[:, :, 0, :], both[:, :, 0, :], both[:, :, 1, :], ALU.mult))
                measured(v, 0, both[:, :, 0, :], B)
                v.wait_ge(s_("rows_mm"), 1)
                V.tensor_copy(rowsT, bank(0)[:, 0:M2]).then_inc(s_("rowsT"), 1)
                v.wait_ge(s_("gate_mm"), 1)
                V.tensor_tensor(gate, bank(1)[:, 0:NM * (E + 1)].rearrange("p (i e) -> p i e", i=NM),
                                spread(F("gateb"), 1, [P, NM, E + 1]), ALU.add).then_inc(s_("gate"), 1)
                by = [P, NM, E]
                v.wait_ge(s_("sigmoid"), 1)
                link(v, V.tensor_tensor(score, gate[:, :, 1:E + 1], spread(F("expbias"), 1, by), ALU.add))
                first_largest(v, onehot, score, spread(C("prio"), 1, by), best, by)
                v.sem_inc(s_("onehot"), 1)
                full = [P, NM * E, H]
                hot = spread(onehot.rearrange("p i e -> p (i e)"), 2, full)
                rows16 = lambda ap: ap.rearrange("p i e h -> p (i e) h")
                for w in range(2):
                    v.wait_ge(s_("sel_mm"), w + 1)
                    V.tensor_tensor(rows16(sel[:, w, :, :, :]),
                                    ps[:, 4 + 2 * w:6 + 2 * w, :].rearrange("p i (e h) -> p (i e) h", e=E), hot,
                                    ALU.mult).then_inc(s_("sel"), 1)
                    if w == 0:
                        v.wait_ge(s_("onehot_turned"), 1)
                        V.tensor_copy(onehotT[0:E, :, :], bank4(1)[0:E, 0:NM, :]).then_inc(s_("onehotT"), 1)
                v.wait_ge(s_("sel"), 2)
                for w in range(2):
                    last = V.tensor_reduce(mine[:, w, :, :], sel[:, w, :, :, :].rearrange("p i e h -> p i h e"), AX.X, ALU.add)
                link(v, last)
                v.wait_ge(s_("bias_mm"), 1)
                V.tensor_tensor(mine, mine, bank4(1)[:, 2:2 + NM, :].rearrange("p i (w h) -> p w i h", w=2),
                                ALU.add).then_inc(s_("biased"), 1)
                normed(v, 0, both[:, :, 0, :], zs, B).then_inc(s_("zs"), 1)
                v.wait_ge(s_("sel_silu"), 1)
                link(v, V.tensor_tensor(mine[:, 0, :, :], mine[:, 0, :, :], mine[:, 1, :, :], ALU.mult))
                measured(v, 1, mine[:, 0, :, :], NM)
                link(v, V.tensor_tensor(picked, onehot, gate[:, :, 1:E + 1], ALU.mult))
                link(v, V.tensor_reduce(two[:, :, 1], picked, AX.X, ALU.add))
                link(v, V.tensor_copy(two[:, :, 0], gate[:, :, 0]))
                link(v, V.tensor_reduce(best, two, AX.X, ALU.max))
                V.tensor_tensor(two, two, spread(best, 2, [P, NM, 2]), ALU.subtract).then_inc(s_("two"), 1)
                link(v, normed(v, 1, mine[:, 0, :, :], mine[:, 1, :, :], NM))
                link(v, V.tensor_tensor(mine[:, 1, :, :], mine[:, 1, :, :], spread(F("sellng"), 1, [P, NM, H]), ALU.mult))
                link(v, V.tensor_tensor(mine[:, 1, :, :], mine[:, 1, :, :], spread(F("sellnb"), 1, [P, NM, H]), ALU.add))
                for i in range(NM):
                    last = V.tensor_tensor(zm[:, i, :, :], spread(mine[:, 1, i, :], 1, [P, E, H]),
                                           spread(onehot[:, i, :], 2, [P, E, H]), ALU.mult)
                last.then_inc(s_("zm"), 1)
                for i in range(2):
                    v.wait_ge(s_("shared_mm"), i + 1)
                    V.tensor_tensor(shared[:, 8 * i:8 * i + 8, :], ps[:, 4 * i:4 * i + 2, :].rearrange("p j (b d) -> p (j b) d", b=4),
                                    spread(F("sb3"), 1, [P, B // 2, D]), ALU.add).then_inc(s_("shared"), 1)
                v.wait_ge(s_("exp"), 1)
                link(v, V.tensor_reduce(best, two, AX.X, ALU.add))
                link(v, V.reciprocal(best, best))
                link(v, V.tensor_tensor(two, two, spread(best, 2, [P, NM, 2]), ALU.mult))
                link(v, V.tensor_scalar(two[:, :, 0], two[:, :, 0], -1.0, None, ALU.add))
                link(v, V.tensor_tensor(two, two, spread(row_first[:, :], 2, [P, NM, 2]), ALU.mult))
                v.wait_ge(s_("expert_mm"), 1)
                V.tensor_copy(value[:, :, D:D + 1], two[:, :, 0:1])
                V.tensor_tensor(value[:, :, 0:D], bank4(7)[:, 0:NM, :], spread(two[:, :, 1], 2, [P, NM, D]),
                                ALU.mult).then_inc(s_("value"), 1)
                v.wait_ge(s_("value"), 1)
                ahead["banks"](v)
                for j in range(-(-B // 3)):
                    v.wait_ge(s_("back"), j + 1)
                    seqs = range(3 * j, min(3 * j + 3, B))
                    back = bank(j)[:, 0:(D + 1) * len(seqs)].rearrange("p (i d) -> p i d", i=len(seqs))
                    link(v, V.tensor_scalar(keepmore[:, 3 * j:3 * j + len(seqs)], back[:, :, D], 1.0, None, ALU.add))
                    for i, b in enumerate(seqs):
                        last = V.scalar_tensor_tensor(update[:, b, :], shared[:, b, :], keepmore[:, b:b + 1],
                                                      back[:, i, 0:D], ALU.mult, ALU.add)
                    for g in range(GROUPS):
                        if QUAD * g + QUAD - 1 in seqs:
                            q = slice(QUAD * g, QUAD * g + QUAD)
                            link(v, last)
                            final(v, "l3x", g, V.tensor_tensor(x[:, q, :], x[:, q, :], update[:, q, :], ALU.add))
            return vector, gpsimd, tensor, scalar

        def l3_attention():
            ta, tb = carve(arena_a), carve(arena_b)
            F = lambda name: field["l3", name]
            C9 = HEAD + 1
            PAIR = 2
            keys = ta(2 * PAIR * HEADS * T, "p (i b u g s) -> p i b u g s", i=2, b=PAIR, u=4, g=4)
            vals = tb(B * HEADS * C9, "p (b h c) -> p b h c", b=B, h=HEADS)
            probs = tb(3 * 4 * T, "p (i g s) -> p i g s", i=3, g=4)
            probsT = tb(3 * 4 * T, "p (i g l) -> p i g l", i=3, g=4)
            weighed = tb(2 * 4 * T, "p (i u l) -> p i u l", i=2, u=4)
            neg = tb(3 * 4, "p (i g) -> p i g", i=3)
            att = tb(B * D, "p (b d) -> p b d", b=B)
            attT = tb(B * D, "p (b l) -> p b l", b=B)
            inv = tb(2 * HEADS, "p (i h) -> p i h", i=2)
            n = norm("l3x", scale=1.0 / math.sqrt(HEAD))
            K = 4 * B
            s_ = lambda what: sem("l3x_" + what)

            def clear_banks(v):
                V.memset(ps[:, 6:8, :], 0.0).then_inc(s_("cleared"), 1)
            ahead["banks"] = clear_banks

            def tensor(pe):
                pe.wait_ge(s_("cleared"), spent("l3x_cleared") + 1)

                def score(k):
                    b, u = k // 4, k % 4
                    if b % PAIR == 0 and u == 0:
                        pe.wait_ge(s_(f"keys{b // PAIR % 2}"), spent(f"l3x_keys{b // PAIR % 2}") + 16 * HEADS * (b // (2 * PAIR) + 1))
                    if k < 4:
                        pe.wait_ge(sem("norm_xnT"), past("l3x", "norm_xnT") + k + 1)
                    if k >= 3:
                        pe.wait_ge(s_("probs"), spent("l3x_probs") + k - 2)
                    TE.matmul(bank(k % 3), xnT[:, b, :], keys[:, b // PAIR % 2, b % PAIR, u, :, :], start=True,
                              stop=True).then_inc(s_("score"), 1)

                def turn(k):
                    pe.wait_ge(s_("probs"), spent("l3x_probs") + k + 1)
                    if k >= 3:
                        pe.wait_ge(s_("probsT"), spent("l3x_probsT") + k - 2)
                    for g in range(4):
                        last = TE.transpose(bank4(3 + k % 3)[:, g, :], probs[:, k % 3, g, :], ident)
                    last.then_inc(s_("turned"), 1)

                def weigh(k):
                    b, u = k // 4, k % 4
                    if k == 0:
                        pe.wait_ge(s_("values"), spent("l3x_values") + 16)
                    pe.wait_ge(s_("probsT"), spent("l3x_probsT") + k + 1)
                    if u == 0 and b >= 2:
                        pe.wait_ge(s_("att"), spent("l3x_att") + b - 1)
                    for g in range(4):
                        last = TE.matmul(bank4(6 + b % 2)[32 * g:32 * g + C9, u, :], vals[:, b, 4 * g + u, :],
                                         probsT[:, k % 3, g, :], start=True, stop=True)
                    last.then_inc(s_("weigh"), 1)

                def turn_back(b):
                    pe.wait_ge(s_("weighed"), spent("l3x_weighed") + b + 1)
                    for u in range(4):
                        last = TE.transpose(bank4(6 + b % 2)[:, u, :], weighed[:, b % 2, u, :], ident)
                    last.then_inc(s_("back"), 1)

                def first_scores():
                    score(0)
                    score(1)
                n[2](pe, first_scores)
                for k in range(K):
                    if k + 2 < K:
                        score(k + 2)
                    if k == 0:
                        pe.wait_ge(sem("norm_xnT"), past("l3x", "norm_xnT") + GROUPS)
                    turn(k)
                    if k:
                        weigh(k - 1)
                    if k % 4 == 2 and k >= 4:
                        turn_back(k // 4 - 1)
                weigh(K - 1)
                turn_back(B - 1)
                for g in range(GROUPS):
                    pe.wait_ge(s_("att"), spent("l3x_att") + QUAD * (g + 1))
                    for i in range(QUAD):
                        last = TE.transpose(bank4(g)[:, i, :], att[:, QUAD * g + i, :], ident)
                    last.then_inc(s_("att_turned"), 1)
                pe.wait_ge(s_("att"), spent("l3x_att") + B)
                pe.wait_ge(sem("load_l3"), 16)
                for g in range(GROUPS):
                    pe.wait_ge(s_("attT"), spent("l3x_attT") + g + 1)
                    for i in range(QUAD):
                        last = TE.matmul(bank4(4 + g)[:, i, :], attT[:, QUAD * g + i, :], F("wprojT"), start=True, stop=True)
                    last.then_inc(s_("out"), 1)

            def scalar(a):
                n[3](a)

                def copy_out(b):
                    a.wait_ge(s_("weigh"), spent("l3x_weigh") + 4 * (b + 1))
                    if b >= 2:
                        a.wait_ge(s_("back"), spent("l3x_back") + b - 1)
                    S.copy(weighed[:, b % 2, :, :], bank4(6 + b % 2)).then_inc(s_("weighed"), 1)
                for k in range(K):
                    a.wait_ge(s_("largest"), spent("l3x_largest") + k + 1)
                    if k >= 3:
                        a.wait_ge(s_("turned"), spent("l3x_turned") + k - 2)
                    for g in range(4):
                        last = S.activation(probs[:, k % 3, g, :], bank4(k % 3)[:, g, :], ACT.Exp,
                                            bias=neg[:, k % 3, g:g + 1])
                    last.then_inc(s_("probs"), 1)
                    if k % 4 == 2 and k >= 4:
                        copy_out(k // 4 - 1)
                copy_out(B - 1)
                for g in range(GROUPS):
                    a.wait_ge(s_("att_turned"), spent("l3x_att_turned") + g + 1)
                    S.copy(attT[:, QUAD * g:QUAD * g + QUAD, :], bank4(g)).then_inc(s_("attT"), 1)

            def vector(v):
                v.sem_inc(s_("cleared"), 1)
                n[0](v)
                v.wait_ge(sem("load_l3"), 16)

                def largest(k):
                    v.wait_ge(s_("score"), spent("l3x_score") + k + 1)
                    if k >= 3:
                        v.wait_ge(s_("probs"), spent("l3x_probs") + k - 2)
                    V.tensor_reduce(neg[:, k % 3, :], bank4(k % 3), AX.X, ALU.max, negate=True).then_inc(s_("largest"), 1)

                def copy_turned(k):
                    v.wait_ge(s_("turned"), spent("l3x_turned") + k + 1)
                    if k >= 3:
                        v.wait_ge(s_("weigh"), spent("l3x_weigh") + k - 2)
                    V.tensor_copy(probsT[:, k % 3, :, :], bank4(3 + k % 3)).then_inc(s_("probsT"), 1)

                def divide(b):
                    v.wait_ge(s_("back"), spent("l3x_back") + b + 1)
                    back = bank(6 + b % 2).rearrange("p (u g c) -> p g u c", u=4, g=4)
                    link(v, V.reciprocal(inv[:, b % 2, :].rearrange("p (g u) -> p g u", g=4), back[:, :, :, HEAD]))
                    V.tensor_tensor(att[:, b, :].rearrange("p (g u c) -> p g u c", g=4, u=4), back[:, :, :, 0:HEAD],
                                    spread(inv[:, b % 2, :].rearrange("p (g u) -> p g u", g=4), 3, [P, 4, 4, HEAD]),
                                    ALU.mult).then_inc(s_("att"), 1)
                largest(0)
                largest(1)
                for k in range(K):
                    if k + 2 < K:
                        largest(k + 2)
                    copy_turned(k)
                    if k % 4 == 3 and k >= 4:
                        divide(k // 4 - 1)
                divide(B - 1)
                for g in range(GROUPS):
                    q = slice(QUAD * g, QUAD * g + QUAD)
                    last = V.tensor_tensor(x[:, q, :], x[:, q, :], spread(F("bproj"), 1, [P, QUAD, D]), ALU.add)
                link(v, last)
                for g in range(GROUPS):
                    q = slice(QUAD * g, QUAD * g + QUAD)
                    v.wait_ge(s_("out"), spent("l3x_out") + g + 1)
                    final(v, "l3", g, V.tensor_tensor(x[:, q, :], bank4(4 + g), x[:, q, :], ALU.add))

            def clear_keys(a, half):
                flat = keys.rearrange("p i b u g s -> p i (b u g s)")[:, half, :]
                for i in range(2):
                    n_ = PAIR * HEADS * T // 2
                    S.activation(flat[:, n_ * i:n_ * i + n_], zero[:, 0:1].to_broadcast([P, n_]),
                                 ACT.Copy).then_inc(s_("start"), 1)
            ahead["keys"] = clear_keys

            def load_keys(sp, r):
                for h in range(HEADS):
                    rows_ = slice(HEAD * h, HEAD * h + HEAD)
                    sp.dma_start(keys[rows_, r % 2, :, h % 4, h // 4, :],
                                 dram["ctxT"][rows_, PAIR * r:PAIR * r + PAIR, :]).then_inc(s_(f"keys{r % 2}"), 16)

            def sync(sp):
                sp.wait_ge(s_("start"), spent("l3x_start") + 2)
                load_keys(sp, 0)
                sp.wait_ge(s_("cleared"), spent("l3x_cleared") + 2)
                sp.dma_start(vals, dram["l3_values"].rearrange("p (b h c) -> p b h c", b=B, h=HEADS)).then_inc(s_("values"), 16)
                sp.wait_ge(s_("start"), spent("l3x_start") + 4)
                for r in range(1, B // PAIR):
                    if r >= 2:
                        sp.wait_ge(s_("score"), spent("l3x_score") + 4 * PAIR * (r - 1))
                    load_keys(sp, r)
            return vector, n[1], tensor, scalar, sync

        def l3_experts():
            ta, tb = carve(arena_a), carve(arena_b)
            F = lambda name: field["l3", name]
            C = lambda name: field["consts", name]
            hidden = ta(2 * CH3 * B * CAP)
            ring3 = HID3 + CH3 * D + CH3 + 1
            ring = [ta(ring3) for _ in range(2)]
            onehot = ta(B * E * CAP)
            slots = tb(B * E * CAP)
            route1 = tb(2 * CH3 * 512, "p (i f n) -> p i f n", i=2, f=CH3)
            route2 = tb(2 * CH3 * 512, "p (i f n) -> p i f n", i=2, f=CH3)
            ring += [route1.rearrange("p i f n -> p (i f n)")[:, ring3 * i:ring3 * i + ring3] for i in range(2)]
            score = tb(B * E, "p (b e) -> p b e", b=B)
            left = tb(B * E, "p (b e) -> p b e", b=B)
            chosen = tb(B * 2 * E, "p (b k e) -> p b k e", b=B, k=2)
            best = tb(B)
            taken = tb(B * E)
            slotpos = tb(B * E)
            weights = tb(B * E)
            turned_w = tb(4 * T, "p (i j n) -> p i j n", i=2, j=2)
            turned_y = tb(4 * D, "p (i j n) -> p i j n", i=2, j=2)
            route3 = tb(2 * 512, "p (i n) -> p i n", i=2)
            n = norm("l3")
            s_ = lambda what: sem("l3f_" + what)
            sync, positions, tensor_, scalar_, vector_ = slotted(
                "l3", CAP, B, False, onehot, slots, hidden, None, ring, turned_w, turned_y, taken, slotpos, weights,
                None)

            def tensor(pe):
                n[2](pe)

                def first(g):
                    pe.wait_ge(sem("norm_xnT"), past("l3", "norm_xnT") + g + 1)
                    for f in range(CH3):
                        k = CH3 * g + f
                        if k >= 2:
                            pe.wait_ge(s_("route1"), spent("l3f_route1") + k - 1)
                        TE.matmul(bank(4 + k % 2), F("rW1")[:, P * f:P * f + P], xnT[:, QUAD * g:QUAD * g + QUAD, :],
                                  start=True, stop=True).then_inc(s_("first"), 1)

                def third(g):
                    pe.wait_ge(s_("route2"), spent("l3f_route2") + CH3 * (g + 1))
                    if g >= 2:
                        pe.wait_ge(s_("route3"), spent("l3f_route3") + g - 1)
                    for f in range(CH3):
                        last = TE.matmul(bank(2 + g % 2)[TILE * f:TILE * f + TILE, :], F("rW3")[:, TILE * f:TILE * f + TILE],
                                         route2[:, g % 2, f, :], start=True, stop=True)
                    last.then_inc(s_("third"), 1)

                def turn_third(g):
                    pe.wait_ge(s_("route3"), spent("l3f_route3") + g + 1)
                    if g >= 2:
                        pe.wait_ge(s_("summed"), spent("l3f_summed") + g - 1)
                    for i in range(QUAD):
                        last = TE.transpose(bank4(6 + g % 2)[:, i, :], route3[:, g % 2, T * i:T * i + T], ident)
                    last.then_inc(s_("third_turned"), 1)
                first(0)
                for g in range(GROUPS):
                    if g + 1 < GROUPS:
                        first(g + 1)
                    pe.wait_ge(s_("route1"), spent("l3f_route1") + CH3 * (g + 1))
                    for o in range(CH3):
                        k = CH3 * g + o
                        if k >= 2:
                            pe.wait_ge(s_("route2"), spent("l3f_route2") + k - 1)
                        else:
                            pe.wait_ge(sem("norm_xnT"), past("l3", "norm_xnT") + k + 1)
                        for f in range(CH3):
                            last = TE.matmul(bank(k % 2), F("rW2")[:, HID3 * f + P * o:HID3 * f + P * o + P],
                                             route1[:, g % 2, f, :], start=(f == 0), stop=(f == CH3 - 1))
                        last.then_inc(s_("second"), 1)
                    if g >= 2:
                        turn_third(g - 2)
                    if g:
                        third(g - 1)
                turn_third(GROUPS - 2)
                third(GROUPS - 1)
                turn_third(GROUPS - 1)
                positions(pe)
                tensor_(pe)

            def scalar(a):
                n[3](a)

                def relu2(g):
                    for o in range(CH3):
                        a.wait_ge(s_("second"), spent("l3f_second") + CH3 * g + o + 1)
                        if g >= 2 and o == 0:
                            a.wait_ge(s_("third"), spent("l3f_third") + g - 1)
                        S.activation(route2[:, g % 2, o, :], bank((CH3 * g + o) % 2), ACT.Relu,
                                     bias=F("rb2")[:, o:o + 1]).then_inc(s_("route2"), 1)

                def copy3(g):
                    a.wait_ge(s_("third"), spent("l3f_third") + g + 1)
                    if g >= 2:
                        a.wait_ge(s_("third_turned"), spent("l3f_third_turned") + g - 1)
                    S.copy(route3[:, g % 2, :], bank(2 + g % 2)).then_inc(s_("route3"), 1)
                for g in range(GROUPS):
                    relu2(g)
                    if g:
                        copy3(g - 1)
                copy3(GROUPS - 1)
                a.wait_ge(s_("centred"), spent("l3f_centred") + 1)
                S.activation(score, score, ACT.Exp).then_inc(s_("exp"), 1)
                scalar_(a)

            def vector(v):
                v.sem_inc(s_("start"), 1)
                n[0](v)

                def sum_third(g):
                    v.wait_ge(s_("third_turned"), spent("l3f_third_turned") + g + 1)
                    chunks = bank(6 + g % 2).rearrange("p (i f e) -> p i e f", i=QUAD, f=CH3)[:, :, 0:E, :]
                    V.tensor_reduce(score[:, QUAD * g:QUAD * g + QUAD, :], chunks, AX.X, ALU.add).then_inc(s_("summed"), 1)
                for g in range(GROUPS):
                    for f in range(CH3):
                        k = CH3 * g + f
                        v.wait_ge(s_("first"), spent("l3f_first") + k + 1)
                        if g >= 2 and f == 0:
                            v.wait_ge(s_("second"), spent("l3f_second") + CH3 * (g - 1))
                        V.tensor_scalar(route1[:, g % 2, f, :], bank(4 + k % 2), F("rb1")[:, f:f + 1], 0.0, ALU.add,
                                        ALU.max).then_inc(s_("route1"), 1)
                    if g >= 3:
                        sum_third(g - 3)
                for g in range(GROUPS - 3, GROUPS):
                    sum_third(g)
                v.wait_ge(s_("summed"), spent("l3f_summed") + GROUPS)
                by8 = [P, B, E]
                prio = spread(C("prio"), 1, by8)
                link(v, V.tensor_tensor(score, score, spread(F("rb3"), 1, by8), ALU.add))
                link(v, V.tensor_reduce(best, score, AX.X, ALU.max))
                V.tensor_tensor(score, score, spread(best, 2, by8), ALU.subtract).then_inc(s_("centred"), 1)
                v.wait_ge(s_("exp"), spent("l3f_exp") + 1)
                link(v, V.tensor_reduce(best, score, AX.X, ALU.add))
                link(v, V.reciprocal(best, best))
                link(v, V.tensor_tensor(score, score, spread(best, 2, by8), ALU.mult))
                first_largest(v, chosen[:, :, 0, :], score, prio, best, by8)
                link(v, V.scalar_tensor_tensor(left, chosen[:, :, 0, :], -FAR, score, ALU.mult, ALU.add))
                first_largest(v, chosen[:, :, 1, :], left, prio, best, by8)
                by = lambda ap: ap.rearrange("p (b e) -> p b e", b=B)
                link(v, V.tensor_tensor(by(taken), chosen[:, :, 0, :], chosen[:, :, 1, :], ALU.add))
                v.sem_inc(sem("slotted_taken"), 1)
                link(v, V.tensor_tensor(by(weights), by(taken), score, ALU.mult))
                vector_(v)

            def start_sync(sp):
                sp.wait_ge(s_("start"), spent("l3f_start") + 1)
                sync(sp)
            return vector, n[1], tensor, scalar, start_sync

        phases = [l0_attention, l0_experts,
                  lambda: attention("l1x", "l1x", "Wq", "Wk", "Wv", "bq", "bk", "bv"), l1_experts,
                  lambda: attention("l2x", "l2", "WqT", "WqT", "WqT", causal=True),
                  l2_experts, l3_attention, l3_experts]
        phases = [p() for p in phases]

        block = f.enter_context(nc.Block())

        @block.sync
        def _(sp):
            n = 2 * T + D
            sp.dma_start(packed["fourier"][:, 0:n], dram["fourier"][:, 0:n]).then_inc(sem("load_first"), 16)
            sp.dma_start(ctxT[:, QUAD:B, :], dram["ctxT"][:, QUAD:B, :]).then_inc(sem("load_ctxT"), 16)
            sp.dma_start(ctx_tok[:, :, :], dram["ctx"].rearrange("b l d -> l b d")).then_inc(sem("load_ctx"), 16)
            sp.dma_start(packed["fourier"][:, n:], dram["fourier"][:, n:]).then_inc(sem("load_fourier"), 16)
            sp.dma_start(packed["consts"][:, :], dram["consts"]).then_inc(sem("load_consts"), 16)
            for pack in ("l0f", "l1x", "l1f", "l2", "l3"):
                sp.dma_start(packed[pack][:, :], dram[pack]).then_inc(sem("load_" + pack), 16)
            for p in phases:
                if len(p) > 4:
                    p[4](sp)
            for g in range(GROUPS):
                q = slice(QUAD * g, QUAD * g + QUAD)
                sp.wait_ge(sem("slotted_added"), past("l3", "slotted_added") + g + 1)
                sp.dma_start(out[q, :, :].rearrange("b l d -> l b d"), x[:, q, :]).then_inc(sem("stored"), 16)
            sp.wait_ge(sem("stored"), 16 * GROUPS)

        @block.gpsimd
        def _(g):
            nc.gpsimd.memset(minushalf[:, :], -0.5).then_inc(sem("filled"), 1)
            nc.gpsimd.memset(zero[:, :], 0.0).then_inc(sem("filled"), 1)
            g.wait_ge(sem("filled"), 2)
            for p in phases:
                p[1](g)

        @block.scalar
        def _(a):
            a.dma_start(ctxT[:, 0:QUAD, :], dram["ctxT"][:, 0:QUAD, :]).then_inc(sem("load_first"), 16)
            a.dma_start(x[:, :, :], dram["x"].rearrange("b l d -> l b d")).then_inc(sem("load_x"), 16)
            a.dma_start(index_sb[:, :, :], dram["index"].rearrange("p (w n) -> p w n", w=2)).then_inc(sem("load_index"), 16)
            for p in phases:
                p[3](a)

        @block.vector
        def _(v):
            for p in phases:
                p[0](v)

        @block.tensor
        def _(pe):
            for p in phases:
                p[2](pe)


def fourier_constants():
    n = T
    t = np.arange(n)
    half = n // 2
    fwd1, fwd2, inv1, inv2 = (np.zeros((n, n)) for _ in range(4))
    for j in range(half + 1):
        c = np.cos(2 * np.pi * j * t / n)
        s = np.sin(2 * np.pi * j * t / n)
        w = (1.0 if j in (0, half) else 2.0) / n
        fwd1[j], inv1[j] = c, w * c
        if 0 < j < half:
            fwd1[half + j], inv1[half + j] = -s, w * c
            fwd2[j], inv2[j] = -s, w * s
            fwd2[half + j], inv2[half + j] = c, -w * s
    dft = np.concatenate([fwd1.T, fwd2.T], axis=1)
    idft = np.concatenate([inv1, inv2], axis=1)
    return dft.astype(np.float32), idft.astype(np.float32)


def constants():
    p = np.arange(P)
    e = np.arange(E)
    dft, idft = fourier_constants()
    m = np.arange(M2)

    def rows(v):
        return np.tile(np.asarray(v, np.float32).reshape(1, -1), (P, 1))
    return {
        "dft": dft, "idft": idft, "ident": np.eye(P, dtype=np.float32),
        "blockmask": (p[:, None] // HEAD == np.arange(HEADS)[None]).astype(np.float32),
        "dmod": (p[:, None] % HEAD + T).astype(np.float32),
        "iota8": rows(np.arange(HEAD)), "prio": rows(E - e), "prio4": rows(4 - np.arange(4)),
        "lower": rows((e[None, :] <= e[:, None])),
        "rownum": (2 * (np.arange(B)[None, :, None] * T + p[:, None, None]) + np.arange(2)[None, None]).reshape(P, 2 * B).astype(np.float32),
        "ones": np.ones((P, P), np.float32),
        "before": (p[:, None] < p[None, :]).astype(np.float32),
        "causal": np.where(p[None, :] <= p[:, None], 0.0, -FAR).astype(np.float32),
        "slot": rows(np.arange(CAP1)),
        "token": (np.arange(B)[None] * T + p[:, None]).astype(np.float32),
        "tokenrow": rows(np.arange(B * T)),
        "earlier": np.concatenate([(m[None] < p[:, None]), (m[None] < P + p[:, None])], axis=1).astype(np.float32),
    }


def kernel(**inputs):
    import concourse.bacc as bacc
    from concourse.bass_utils import run_bass_kernel_spmd

    i = {k: np.asarray(v) for k, v in inputs.items()}

    def rows(v):
        return np.tile(v.reshape(1, -1), (P, 1))

    def col(v):
        return v.reshape(-1, P).T

    def cols(v):
        return v.reshape(E, -1, P).transpose(0, 2, 1)

    def tall(v):
        return np.concatenate([v, np.zeros((P - v.shape[0], v.shape[1]), v.dtype)])

    def tile32(v):
        return np.concatenate([v, np.zeros(v.shape[:-1] + (TILE - v.shape[-1],), v.dtype)], axis=-1)

    def blocks(v):
        z = np.zeros_like(v)
        return np.concatenate([np.concatenate([v, z], axis=1), np.concatenate([z, v], axis=1)])

    def twice(v):
        return np.concatenate([v, v])

    c = constants()
    fields = {
        ("fourier", "wk"): i["L0_xattn_wk"], ("fourier", "wq"): i["L0_xattn_wq"],
        ("fourier", "wv"): i["L0_xattn_wv"], ("fourier", "wo"): i["L0_xattn_wo"],
        ("l0f", "wgateT"): tile32(i["L0_ffn_w_gate"].T),
        ("l0f", "sw1T"): i["L0_ffn_sw1"].T, ("l0f", "sw3T"): i["L0_ffn_sw3"].T, ("l0f", "sw2T"): i["L0_ffn_sw2"].T,
        ("l0f", "ebias"): rows(i["L0_ffn_expert_bias"]),
        ("l0f", "w13"): np.concatenate([i["L0_ffn_w1"], i["L0_ffn_w3"]], axis=2).transpose(1, 0, 2).reshape(P, -1),
        ("l0f", "w2"): tall(i["L0_ffn_w2"].transpose(1, 0, 2).reshape(HID0, -1)),
        ("l1x", "Wq"): i["L1_xattn_Wq"], ("l1x", "Wk"): i["L1_xattn_Wk"], ("l1x", "Wv"): i["L1_xattn_Wv"],
        ("l1x", "bq"): col(i["L1_xattn_bq"]), ("l1x", "bk"): col(i["L1_xattn_bk"]), ("l1x", "bv"): rows(i["L1_xattn_bv"]),
        ("l1f", "lnw"): col(i["L1_ffn_ln_w"]), ("l1f", "Wg"): tile32(i["L1_ffn_Wg"]), ("l1f", "bg"): rows(i["L1_ffn_bg"]),
        ("l2", "WqT"): i["L2_xattn_Wq"].T,
        ("l2", "sw12T"): np.concatenate([i["L2_ffn_sw1"].T, i["L2_ffn_sw2"].T], axis=1),
        ("l2", "sb12"): rows(np.concatenate([i["L2_ffn_sb1"], i["L2_ffn_sb2"]])),
        ("l2", "sw3T"): blocks(i["L2_ffn_sw3"].T), ("l2", "sb3"): rows(i["L2_ffn_sb3"]),
        ("l2", "slng"): twice(i["L2_ffn_s_ln_g"].reshape(-1, 1)), ("l2", "slnb"): twice(i["L2_ffn_s_ln_b"].reshape(-1, 1)),
        ("l2", "gateT"): np.concatenate([i["L2_ffn_sg_w"], i["L2_ffn_eg_w"]]).T,
        ("l2", "gateb"): rows(np.concatenate([i["L2_ffn_sg_b"], i["L2_ffn_eg_b"]])),
        ("l2", "expbias"): rows(i["L2_ffn_exp_bias"]),
        ("l2", "ew1T"): i["L2_ffn_ew1"].transpose(2, 0, 1).reshape(P, -1),
        ("l2", "ew2T"): i["L2_ffn_ew2"].transpose(2, 0, 1).reshape(P, -1),
        ("l2", "eb12"): tall(np.concatenate([i["L2_ffn_eb1"], i["L2_ffn_eb2"]], axis=1)),
        ("l2", "ew3"): i["L2_ffn_ew3"].transpose(0, 2, 1).reshape(E // 2, P, D).transpose(1, 0, 2).reshape(P, -1),
        ("l2", "eb3"): tall(i["L2_ffn_eb3"]),
        ("l2", "sellng"): rows(i["L2_ffn_sel_ln_g"]), ("l2", "sellnb"): rows(i["L2_ffn_sel_ln_b"]),
        ("l3", "wprojT"): i["L3_xattn_w_proj"].T, ("l3", "bproj"): rows(i["L3_xattn_b_proj"]),
        ("l3", "rW1"): i["L3_ffn_rW1"], ("l3", "rb1"): col(i["L3_ffn_rb1"]),
        ("l3", "rW2"): i["L3_ffn_rW2"].reshape(CH3, P, HID3).transpose(1, 0, 2).reshape(P, -1), ("l3", "rb2"): col(i["L3_ffn_rb2"]),
        ("l3", "rW3"): tile32(i["L3_ffn_rW3"].reshape(CH3, P, E)).transpose(1, 0, 2).reshape(P, -1), ("l3", "rb3"): rows(i["L3_ffn_rb3"]),
    }
    arrays = {"x": i["x"], "ctx": i["ctx_1024"], "ctxT": i["ctx_1024"].transpose(2, 0, 1),
              "index": np.concatenate([v for w in ("b", "t") for v in (rows(i["L2_ffn_index_" + w]), col(i["L2_ffn_index_" + w]))],
                                      axis=1)}
    arrays["l1_experts"] = np.concatenate([
        i["L1_ffn_W1a"], i["L1_ffn_W1b"],
        i["L1_ffn_W2"].reshape(E, CH1, P, D).transpose(0, 2, 1, 3).reshape(E, P, -1),
        cols(i["L1_ffn_b1a"]), cols(i["L1_ffn_b1b"]), cols(i["L1_ffn_b2"])], axis=2)
    arrays["l3_experts"] = np.concatenate([
        i["L3_ffn_eW1"], i["L3_ffn_eW2"].reshape(E, CH3, P, D).transpose(0, 2, 1, 3).reshape(E, P, -1),
        cols(i["L3_ffn_eb1"]), cols(i["L3_ffn_eb2"])], axis=2)
    vals = np.ones((T, B, HEADS, HEAD + 1), i["ctx_1024"].dtype)
    vals[..., 0:HEAD] = i["ctx_1024"].reshape(B, T, HEADS, HEAD).transpose(1, 0, 2, 3)
    arrays["l3_values"] = vals.reshape(P, -1)
    for pack, names in PACKS.items():
        arrays[pack] = np.concatenate([fields.get((pack, n), c.get(n)) for n, _ in names], axis=1)

    nc = bacc.Bacc("TRN2", target_bir_lowering=False, num_devices=1)
    feeds, dram = {}, {}
    for name, a in arrays.items():
        a = np.ascontiguousarray(a)
        feeds[f"in_{name}_dram"] = a
        dram[name] = nc.dram_tensor(f"in_{name}_dram", a.shape, mybir.dt.from_np(a.dtype), kind="ExternalInput").ap()
    out = nc.dram_tensor("out_0_dram", (B, T, D), F32, kind="ExternalOutput").ap()
    build(nc, dram, out)
    r = run_bass_kernel_spmd(nc, [feeds], core_ids=[0])
    return r.results[0]["out_0_dram"]
```
